# Optimizing a Trainium2 kernel written in Bass

```python
import numpy as np
import jax
import jax.numpy as jnp

def _softmax(x, axis=-1):
    return jax.nn.softmax(x, axis=axis)

def _gelu(x):
    return jax.nn.gelu(x, approximate=True)

def _silu(x):
    return jax.nn.silu(x)

def _sigmoid(x):
    return jax.nn.sigmoid(x)

def _layernorm(x, axis=-1, eps=1e-05):
    m = jnp.mean(x, axis=axis, keepdims=True)
    v = jnp.var(x, axis=axis, keepdims=True)
    return (x - m) / jnp.sqrt(v + eps)

def _scatter_add(tgt, idx, src, axis=0):
    return tgt.at[idx].add(src)

def _segment_sum(src, seg, n):
    return jax.ops.segment_sum(src, seg, n)
kernel_name = 'mk_gps_d1_gnn_r8_1d7ac7'

def setup_inputs(seed: int=0):
    np.random.seed(seed)
    _w = jnp.asarray

    def _rec_inputs():
        import jax
        import jax.numpy as jnp
        _gk = jax.random.key(seed)
        x = -0.0003713 + 1 * jax.random.normal(jax.random.fold_in(_gk, 1), (6250, 256), jnp.float32)
        src = jax.random.randint(jax.random.fold_in(_gk, 2), (200000,), 0, 6250, jnp.int32)
        dst = jnp.minimum((6250 * jax.random.uniform(jax.random.fold_in(_gk, 3), (200000,)) ** 2.0).astype(jnp.int32), 49999)
        _o = jnp.argsort(dst, stable=True)
        src = src[_o]
        dst = dst[_o]
        return (x, src, dst)
    x, src, dst = _rec_inputs()

    def _L0_gnn_setup():
        import jax, jax.numpy as jnp
        import numpy as np
        N, E = (6250, 100000)
        IN_C, OUT_C, HEADS = (256, 64, 4)
        NEG_SLOPE = 0.2
        key = jax.random.key(seed)
        k1, k2, k3, k4, k5, k6 = jax.random.split(key, 6)
        x = jax.random.normal(k1, (N, IN_C), dtype=jnp.float32)
        edge_index = jax.random.randint(k2, (2, E), 0, N, dtype=jnp.int64)
        W = jax.random.normal(k3, (IN_C, HEADS * OUT_C), dtype=jnp.float32) * (1.0 / np.sqrt(IN_C))
        att_src = jax.random.normal(k4, (HEADS, OUT_C), dtype=jnp.float32) * (1.0 / np.sqrt(OUT_C))
        att_dst = jax.random.normal(k5, (HEADS, OUT_C), dtype=jnp.float32) * (1.0 / np.sqrt(OUT_C))
        bias = jnp.zeros((HEADS * OUT_C,), dtype=jnp.float32)
        return {'x': x, 'edge_index': edge_index, 'W': W, 'att_src': att_src, 'att_dst': att_dst, 'bias': bias}
    _L0_gnn_all = _L0_gnn_setup()
    _L0_gnn_in = {k: v for k, v in _L0_gnn_all.items() if k in ('W', 'att_src', 'att_dst', 'bias')}
    del _L0_gnn_all

    def _L0_mix_setup():
        import jax, jax.numpy as jnp
        import numpy as np
        HEADS = 4
        DIM_HEAD = 32
        key = jax.random.key(seed)
        k1, k2, k3 = jax.random.split(key, 3)
        B, L, D = (16, 1024, 256)
        hidden = HEADS * DIM_HEAD
        x = jax.random.normal(k1, (B, L, D), dtype=jnp.float32)
        W_qkv = jax.random.normal(k2, (D, 3 * hidden), dtype=jnp.float32) * D ** (-0.5)
        W_out = jax.random.normal(k3, (hidden, D), dtype=jnp.float32) * hidden ** (-0.5)
        b_out = jnp.zeros((D,), dtype=jnp.float32)
        return {'x': x, 'W_qkv': W_qkv, 'W_out': W_out, 'b_out': b_out}
    _L0_mix_all = _L0_mix_setup()
    _L0_mix_in = {k: v for k, v in _L0_mix_all.items() if k in ('W_qkv', 'W_out', 'b_out')}
    del _L0_mix_all

    def _L0_ffn_setup():
        import jax, jax.numpy as jnp
        import numpy as np
        B, N, D = (16, 512, 256)
        NUM_EXPERTS, TOP_K, HEADS = (4, 2, 4)
        N_EDGES = 131072
        LN_EPS = 1e-05

        def _layernorm(x, g, b):
            mu = x.mean(-1, keepdims=True)
            var = ((x - mu) ** 2).mean(-1, keepdims=True)
            return (x - mu) * jax.lax.rsqrt(var + LN_EPS) * g + b

        def _forward(x, edge_index, W_gat, att_src, att_dst, b_gat, ln_gamma, ln_beta, W1, b1, W2, b2):
            Bc, Nc, Dc = x.shape
            M = Bc * Nc
            x_flat = x.reshape(M, Dc)
            h = (x_flat @ W_gat).reshape(M, HEADS, NUM_EXPERTS)
            loops = jnp.arange(M, dtype=edge_index.dtype)
            src = jnp.concatenate([edge_index[0], loops])
            dst = jnp.concatenate([edge_index[1], loops])
            a_src = (h * att_src).sum(-1)
            a_dst = (h * att_dst).sum(-1)
            e = jax.nn.leaky_relu(a_src[src] + a_dst[dst], negative_slope=0.2)
            e_max = jax.ops.segment_max(e, dst, num_segments=M)
            ee = jnp.exp(e - e_max[dst])
            denom = jax.ops.segment_sum(ee, dst, num_segments=M)
            alpha = ee / (denom[dst] + 1e-16)
            msg = h[src] * alpha[:, :, None]
            agg = jax.ops.segment_sum(msg, dst, num_segments=M).reshape(M, HEADS * NUM_EXPERTS) + b_gat
            scores = _layernorm(agg, ln_gamma, ln_beta).reshape(M, HEADS, NUM_EXPERTS).mean(1)
            scores = scores.reshape(Bc, Nc, NUM_EXPERTS)
            topk_s, topk_i = jax.lax.top_k(scores, TOP_K)
            w = jax.nn.softmax(topk_s, axis=-1)
            out = jnp.zeros_like(x)
            for ei in range(NUM_EXPERTS):
                g = jnp.where(topk_i == ei, w, 0.0).sum(-1)
                hh = jax.nn.gelu(x @ W1[ei] + b1[ei], approximate=False)
                out = out + g[..., None] * (hh @ W2[ei] + b2[ei])
            return out
        key = jax.random.key(seed)
        ks = jax.random.split(key, 8)
        s = 0.05
        return {'x': jax.random.normal(ks[0], (B, N, D), jnp.float32), 'W_gat': jax.random.normal(ks[1], (D, HEADS * NUM_EXPERTS), jnp.float32) * s, 'att_src': jax.random.normal(ks[2], (HEADS, NUM_EXPERTS), jnp.float32) * s, 'att_dst': jax.random.normal(ks[3], (HEADS, NUM_EXPERTS), jnp.float32) * s, 'b_gat': jnp.zeros((HEADS * NUM_EXPERTS,), jnp.float32), 'ln_gamma': jnp.ones((HEADS * NUM_EXPERTS,), jnp.float32), 'ln_beta': jnp.zeros((HEADS * NUM_EXPERTS,), jnp.float32), 'W1': jax.random.normal(ks[4], (NUM_EXPERTS, D, 2 * D), jnp.float32) * s, 'b1': jnp.zeros((NUM_EXPERTS, 2 * D), jnp.float32), 'W2': jax.random.normal(ks[5], (NUM_EXPERTS, 2 * D, D), jnp.float32) * s, 'b2': jnp.zeros((NUM_EXPERTS, D), jnp.float32), 'edge_index': jax.random.randint(ks[6], (2, N_EDGES), 0, B * N, jnp.int32)}
    _L0_ffn_all = _L0_ffn_setup()
    _L0_ffn_in = {k: v for k, v in _L0_ffn_all.items() if k in ('W_gat', 'att_src', 'att_dst', 'b_gat', 'ln_gamma', 'ln_beta', 'W1', 'b1', 'W2', 'b2', 'edge_index')}
    del _L0_ffn_all
    return {'x': x, 'src': src, 'dst': dst, 'L0_gnn_W': _L0_gnn_in['W'], 'L0_gnn_att_src': _L0_gnn_in['att_src'], 'L0_gnn_att_dst': _L0_gnn_in['att_dst'], 'L0_gnn_bias': _L0_gnn_in['bias'], 'L0_mix_W_qkv': _L0_mix_in['W_qkv'], 'L0_mix_W_out': _L0_mix_in['W_out'], 'L0_mix_b_out': _L0_mix_in['b_out'], 'L0_ffn_W_gat': _L0_ffn_in['W_gat'], 'L0_ffn_att_src': _L0_ffn_in['att_src'], 'L0_ffn_att_dst': _L0_ffn_in['att_dst'], 'L0_ffn_b_gat': _L0_ffn_in['b_gat'], 'L0_ffn_ln_gamma': _L0_ffn_in['ln_gamma'], 'L0_ffn_ln_beta': _L0_ffn_in['ln_beta'], 'L0_ffn_W1': _L0_ffn_in['W1'], 'L0_ffn_b1': _L0_ffn_in['b1'], 'L0_ffn_W2': _L0_ffn_in['W2'], 'L0_ffn_b2': _L0_ffn_in['b2'], 'L0_ffn_edge_index': _L0_ffn_in['edge_index']}

def reference(x, src, dst, L0_gnn_W, L0_gnn_att_src, L0_gnn_att_dst, L0_gnn_bias, L0_mix_W_qkv, L0_mix_W_out, L0_mix_b_out, L0_ffn_W_gat, L0_ffn_att_src, L0_ffn_att_dst, L0_ffn_b_gat, L0_ffn_ln_gamma, L0_ffn_ln_beta, L0_ffn_W1, L0_ffn_b1, L0_ffn_W2, L0_ffn_b2, L0_ffn_edge_index):
    import jax
    import jax.numpy as jnp

    def _L0_gnn_ref(x, edge_index, W, att_src, att_dst, bias):
        import jax, jax.numpy as jnp
        import numpy as np
        N, E = (6250, 100000)
        IN_C, OUT_C, HEADS = (256, 64, 4)
        NEG_SLOPE = 0.2
        n = x.shape[0]
        loops = jnp.arange(n, dtype=edge_index.dtype)
        src = jnp.concatenate([edge_index[0], loops])
        dst = jnp.concatenate([edge_index[1], loops])
        h = (x @ W).reshape(n, HEADS, OUT_C)
        a_src = jnp.einsum('nhc,hc->nh', h, att_src)
        a_dst = jnp.einsum('nhc,hc->nh', h, att_dst)
        alpha = a_src[src] + a_dst[dst]
        alpha = jnp.where(alpha >= 0, alpha, NEG_SLOPE * alpha)
        amax = jax.ops.segment_max(alpha, dst, num_segments=n)
        amax = jax.lax.stop_gradient(jnp.where(jnp.isfinite(amax), amax, 0.0))
        ex = jnp.exp(alpha - amax[dst])
        denom = jax.ops.segment_sum(ex, dst, num_segments=n)
        coef = ex / (denom[dst] + 1e-16)
        msgs = h[src] * coef[:, :, None]
        out = jax.ops.segment_sum(msgs, dst, num_segments=n)
        return out.reshape(n, HEADS * OUT_C) + bias

    def _L0_mix_ref(x, W_qkv, W_out, b_out):
        import jax, jax.numpy as jnp
        import numpy as np
        HEADS = 4
        DIM_HEAD = 32
        B, L, D = x.shape
        scale = DIM_HEAD ** (-0.5)
        qkv = jnp.einsum('bld,df->blf', x, W_qkv)
        qkv = qkv.reshape(B, L, 3, HEADS, DIM_HEAD)
        q = jnp.transpose(qkv[:, :, 0], (0, 2, 1, 3)) * scale
        k = jax.nn.softmax(jnp.transpose(qkv[:, :, 1], (0, 2, 1, 3)), axis=2)
        v = jnp.transpose(qkv[:, :, 2], (0, 2, 1, 3))
        context = jnp.einsum('bhld,bhle->bhde', k, v)
        out = jnp.einsum('bhde,bhld->bhle', context, q)
        out = jnp.transpose(out, (0, 2, 1, 3)).reshape(B, L, HEADS * DIM_HEAD)
        return jnp.einsum('blf,fd->bld', out, W_out) + b_out

    def _L0_ffn_ref(x, W_gat, att_src, att_dst, b_gat, ln_gamma, ln_beta, W1, b1, W2, b2, edge_index):
        import jax, jax.numpy as jnp
        import numpy as np
        B, N, D = (16, 512, 256)
        NUM_EXPERTS, TOP_K, HEADS = (4, 2, 4)
        N_EDGES = 131072
        LN_EPS = 1e-05

        def _layernorm(x, g, b):
            mu = x.mean(-1, keepdims=True)
            var = ((x - mu) ** 2).mean(-1, keepdims=True)
            return (x - mu) * jax.lax.rsqrt(var + LN_EPS) * g + b

        def _forward(x, edge_index, W_gat, att_src, att_dst, b_gat, ln_gamma, ln_beta, W1, b1, W2, b2):
            Bc, Nc, Dc = x.shape
            M = Bc * Nc
            x_flat = x.reshape(M, Dc)
            h = (x_flat @ W_gat).reshape(M, HEADS, NUM_EXPERTS)
            loops = jnp.arange(M, dtype=edge_index.dtype)
            src = jnp.concatenate([edge_index[0], loops])
            dst = jnp.concatenate([edge_index[1], loops])
            a_src = (h * att_src).sum(-1)
            a_dst = (h * att_dst).sum(-1)
            e = jax.nn.leaky_relu(a_src[src] + a_dst[dst], negative_slope=0.2)
            e_max = jax.ops.segment_max(e, dst, num_segments=M)
            ee = jnp.exp(e - e_max[dst])
            denom = jax.ops.segment_sum(ee, dst, num_segments=M)
            alpha = ee / (denom[dst] + 1e-16)
            msg = h[src] * alpha[:, :, None]
            agg = jax.ops.segment_sum(msg, dst, num_segments=M).reshape(M, HEADS * NUM_EXPERTS) + b_gat
            scores = _layernorm(agg, ln_gamma, ln_beta).reshape(M, HEADS, NUM_EXPERTS).mean(1)
            scores = scores.reshape(Bc, Nc, NUM_EXPERTS)
            topk_s, topk_i = jax.lax.top_k(scores, TOP_K)
            w = jax.nn.softmax(topk_s, axis=-1)
            out = jnp.zeros_like(x)
            for ei in range(NUM_EXPERTS):
                g = jnp.where(topk_i == ei, w, 0.0).sum(-1)
                hh = jax.nn.gelu(x @ W1[ei] + b1[ei], approximate=False)
                out = out + g[..., None] * (hh @ W2[ei] + b2[ei])
            return out
        return _forward(x, edge_index, W_gat, att_src, att_dst, b_gat, ln_gamma, ln_beta, W1, b1, W2, b2)
    edge_index = jnp.stack([src, dst])
    xn = _layernorm(x, axis=-1)
    x = x + _L0_gnn_ref(xn, edge_index, L0_gnn_W, L0_gnn_att_src, L0_gnn_att_dst, L0_gnn_bias) + _L0_mix_ref(xn[None], L0_mix_W_qkv, L0_mix_W_out, L0_mix_b_out)[0]
    x = x + _L0_ffn_ref(_layernorm(x, axis=-1)[None], L0_ffn_W_gat, L0_ffn_att_src, L0_ffn_att_dst, L0_ffn_b_gat, L0_ffn_ln_gamma, L0_ffn_ln_beta, L0_ffn_W1, L0_ffn_b1, L0_ffn_W2, L0_ffn_b2, L0_ffn_edge_index)[0]
    return x

_drawn_inputs = setup_inputs


def setup_inputs(seed=0):
    import zlib

    import numpy as np

    out = dict(_drawn_inputs(seed))
    spreads = {'L0_gnn_bias': (0.0, 0.1),
     'L0_mix_b_out': (0.0, 0.1),
     'L0_ffn_b_gat': (0.0, 0.1),
     'L0_ffn_ln_gamma': (1.0, 0.2),
     'L0_ffn_ln_beta': (0.0, 0.1),
     'L0_ffn_b1': (0.0, 0.1),
     'L0_ffn_b2': (0.0, 0.1)}
    factors = {}
    for name, (base, spread) in spreads.items():
        noise = np.random.default_rng([zlib.crc32(name.encode()), seed]).standard_normal(out[name].shape)
        drawn = base * np.exp(spread * noise) if base else spread * noise
        out[name] = jnp.asarray(drawn.astype(out[name].dtype))
    for name, factor in factors.items():
        out[name] = (out[name] * factor).astype(out[name].dtype)
    return out
```

```python
from contextlib import ExitStack

import concourse.bass as bass
from concourse import mybir

ALU = mybir.AluOpType
ACT = mybir.ActivationFunctionType
F32 = mybir.dt.float32
I32 = mybir.dt.int32
AX_X = mybir.AxisListType.X
RMAX = bass.bass_isa.ReduceOp.max

P = 128
N = 6250
D = 256
NB = 125
BLOCKS = N // NB
KC = D // P
EPS = 1e-5
SLOPE = 0.2

GH, GC = 4, 64
EDGES = 200000
EP = 125
GT = 4
GROUPS = EDGES // (EP * GT)
ROW = D + GH
SLOTS = 6
AHEAD = 3
PAIRS = GROUPS + BLOCKS - 1
STEPS = (PAIRS + SLOTS - 1) // SLOTS * SLOTS
LISTED = STEPS + AHEAD
CH = 100
CHUNKS = GROUPS // CH
FAR = -1.0e7
SPREAD = 70.0

MH, MD = 4, 32
MW = MH * MD

XH, XE = 4, 4
XF = XH * XE
XROW = XF + XH
XEDGES = 131072
XT = 4
XGROUPS = XEDGES // (P * XT)
XSLOTS = 4
XAHEAD = 2
HID = 2 * D
HC = HID // P


class Chain:

    def __init__(self, eng, sem, base=0):
        self.eng, self.sem, self.base, self.n = eng, sem, base, 0

    def link(self, ins):
        ins.then_inc(self.sem, 1)
        self.n += 1
        self.eng.wait_ge(self.sem, self.base + self.n)


def bcast(ap, axis, n):
    shape = list(ap.shape)
    shape.insert(axis, n)
    return ap.unsqueeze(axis).to_broadcast(shape)


def floor_div(nc, ch, x, q, qi, t, d):
    ch.link(nc.vector.tensor_scalar(qi, x, 1.0 / d, None, ALU.mult))
    ch.link(nc.vector.tensor_copy(q, qi))
    ch.link(nc.vector.scalar_tensor_tensor(t, q, float(-d), x, ALU.mult, ALU.add))
    ch.link(nc.vector.tensor_scalar(t, t, 0.0, None, ALU.is_lt))
    ch.link(nc.vector.tensor_tensor(q, q, t, ALU.subtract))
    ch.link(nc.vector.scalar_tensor_tensor(t, q, float(-d), x, ALU.mult, ALU.add))
    ch.link(nc.vector.tensor_scalar(t, t, float(d), None, ALU.is_ge))
    ch.link(nc.vector.tensor_tensor(q, q, t, ALU.add))


def mean_and_variance(nc, ch, stats, mean, var):
    V = nc.vector
    m0, v0, m1, v1 = stats[:, :, 1], stats[:, :, 2], stats[:, :, 4], stats[:, :, 5]
    ch.link(V.tensor_tensor(var, m0, m1, ALU.subtract))
    ch.link(V.tensor_tensor(var, var, var, ALU.mult))
    ch.link(V.tensor_tensor(mean, v0, v1, ALU.add))
    ch.link(V.tensor_scalar(mean, mean, 1.0 / D, None, ALU.mult))
    ch.link(V.scalar_tensor_tensor(var, var, 0.25, mean, ALU.mult, ALU.add))
    ch.link(V.tensor_tensor(mean, m0, m1, ALU.add))
    ch.link(V.tensor_scalar(mean, mean, 0.5, None, ALU.mult))


def build(nc, x, src, dst, W, att_src, att_dst, gbias, W_qkv, W_out, b_out, W_gat, xatt_src, xatt_dst, b_gat,
          gamma, beta, W1, b1, W2, b2, xedges, out):
    table = nc.dram_tensor("table", [N, ROW], F32).ap()
    xtable = nc.dram_tensor("xtable", [N, XROW], F32).ap()
    xtable_dst = nc.dram_tensor("xtable_dst", [N, 2 * XH], F32).ap()

    def row(v):
        return v.rearrange("(a n) -> a n", a=1)

    with ExitStack() as whole:
        def scope(ctx):
            def sb(name, shape, dt=F32):
                return ctx.enter_context(nc.sbuf_tensor(name, shape, dt))

            def ps(name, shape):
                return ctx.enter_context(nc.psum_tensor(name, shape, F32))

            def sem(name):
                return ctx.enter_context(nc.semaphore(name))
            return sb, ps, sem

        sb, _, sem = scope(whole)
        x_all = sb("x_all", [NB, BLOCKS, D])
        ident = sb("ident", [P, P])
        ones = sb("ones", [P, P])
        zeros = sb("zeros", [P, 512])
        node = sb("node", [P, NB])
        as_all = sb("as_all", [NB, BLOCKS, GH])
        ad_m = sb("ad_m", [NB, BLOCKS, 2 * GH])
        ex_self = sb("ex_self", [NB, BLOCKS, GH])
        hg_all = sb("hg_all", [NB, BLOCKS, XROW])
        xad_all = sb("xad_all", [NB, BLOCKS, 2 * XH])
        gate = sb("gate", [NB, BLOCKS, XE])
        room = sb("room", [P, BLOCKS, ROW])
        qk = room[:, :, 0:2 * NB]
        agg = room[0:NB, :, :]
        xnT = room[:, :, 0:KC * NB]

        linear_attention_and_projections(nc, scope, x, W, att_src, att_dst, gbias, W_qkv, W_out, b_out, table,
                                         x_all, ident, ones, zeros, node, as_all, ad_m, qk, row)
        with ExitStack() as inner:
            isb, _, _ = scope(inner)
            src_i = isb("src_i", [EP, GROUPS, GT], I32)
            dst_f = isb("dst_f", [EP, GROUPS, GT])
            neg_base = isb("neg_base", [EP, LISTED])
            step_group = isb("step_group", [EP, LISTED], I32)
            step_block = isb("step_block", [EP, LISTED + 1], I32)
            sweeps = isb("sweeps", [EP, 1], I32)
            schedule(nc, scope, src, dst, ones, as_all, ad_m, ex_self, agg, src_i, dst_f, neg_base, step_group,
                     step_block, sweeps)
            edges(nc, scope, table, ident, zeros, node, ad_m, agg, src_i, dst_f, neg_base, step_group, step_block,
                  sweeps)
        nodes(nc, scope, table, W_gat, xatt_src, xatt_dst, xtable, xtable_dst, x_all, ident, agg, ex_self,
              xnT, hg_all, xad_all, row)
        gating(nc, scope, xedges, xtable, xtable_dst, b_gat, gamma, beta, zeros, node, hg_all, xad_all, gate, row)
        experts(nc, scope, W1, b1, W2, b2, x_all, ones, xnT, gate, out)


def linear_attention_and_projections(nc, scope, x, W, att_src, att_dst, gbias, W_qkv, W_out, b_out, table,
                                     x_all, ident, ones, zeros, node, as_all, ad_m, qk, row):
    U = 2
    with ExitStack() as ctx:
        sb, ps, sem = scope(ctx)
        w_sb = sb("w_sb", [P, KC, D])
        qkv_sb = sb("qkv_sb", [P, KC, 3 * MW])
        wout_sb = sb("wout_sb", [MW, D])
        attS = sb("attS", [NB, D])
        attD = sb("attD", [NB, D])
        brow = sb("brow", [1, 2, D])
        stats = sb("stats", [NB, BLOCKS, 6])
        mean = sb("mean", [NB, BLOCKS])
        rstd = sb("rstd", [NB, BLOCKS])
        eps = sb("eps", [NB, 1])
        xn = sb("xn", [NB, U, D])
        xnT = sb("xnT_a", [P, U, KC, NB])
        hrow = sb("hrow", [NB, U, ROW])
        prod = sb("prod", [NB, U, 2, D])
        v_all = sb("v_all", [NB, BLOCKS, MW + 1])
        nmax = sb("nmax", [MW, 1])
        kx = sb("kx", [MW, U, NB])
        kxT = sb("kxT", [NB, U, MW])
        rk = sb("rk", [MW, 1])
        cbd = sb("cbd", [MW, MW])
        cbdT = sb("cbdT", [MW, MW])
        m_sb = sb("m_sb", [MW, D])
        qs = sb("qs", [MW, U, NB])

        psT = ps("psT", [P, U, 512])
        psH = ps("psH", [NB, U, 512])
        psQ = ps("psQ", [P, U, 512])
        psC = ps("psC", [P, 512])

        loaded = sem("loaded")
        consts = sem("consts")
        consts0 = sem("consts0")
        var_ready = sem("var_ready")
        std_ready = sem("std_ready")
        normed = sem("normed")
        turned = sem("turned")
        turned_sb = sem("turned_sb")
        projected = sem("projected")
        qk_kept = sem("qk_kept")
        h_kept = sem("h_kept")
        v_kept = sem("v_kept")
        logits_kept = sem("logits_kept")
        row_stored = [sem(f"row_stored{u}") for u in range(U)]
        dve_chain = sem("dve_chain_a")
        max_known = sem("max_known")
        k_exp = sem("k_exp")
        k_turned = sem("k_turned")
        k_kept = sem("k_kept")
        context_part = sem("context_part")
        context_masked = sem("context_masked")
        context_turned = sem("context_turned")
        context_kept = sem("context_kept")
        m_ready = sem("m_ready")
        m_kept = sem("m_kept")
        q_staged = sem("q_staged")
        mixed = sem("mixed")
        mix_added = sem("mix_added")
        LOADS = 8
        block = ctx.enter_context(nc.Block())

        @block.sync
        def _(sp):
            sp.dma_start(x_all[:], x.rearrange("(b p) d -> p b d", p=NB)).then_inc(loaded, 16)
            sp.dma_start(w_sb[:], W.rearrange("(c p) n -> p c n", p=P)).then_inc(loaded, 16)
            sp.dma_start(qkv_sb[:], W_qkv.rearrange("(c p) n -> p c n", p=P)).then_inc(loaded, 16)
            sp.dma_start(wout_sb[:], W_out).then_inc(loaded, 16)
            for tile, vec in ((attS, att_src), (attD, att_dst)):
                flat = row(vec.rearrange("h c -> (h c)"))
                sp.dma_start(tile[:], flat.to_broadcast([NB, D])).then_inc(loaded, 16)
            sp.dma_start(brow[:, 0, :], row(b_out)).then_inc(loaded, 16)
            sp.dma_start(brow[:, 1, :], row(gbias)).then_inc(loaded, 16)
            with sp.Fori(0, BLOCKS // U) as i:
                for u in range(U):
                    sp.wait_ge(h_kept, U * i + u + 1)
                    sp.wait_ge(logits_kept, U * i + u + 1)
                    sp.dma_start(table[bass.ds((U * i + u) * NB, NB), :], hrow[:, u, :]).then_inc(row_stored[u], 16)
            for u in range(U):
                sp.wait_ge(row_stored[u], 16 * (BLOCKS // U))

        @block.gpsimd
        def _(pool):
            nc.gpsimd.memset(ones[:], 1.0).then_inc(consts0, 1)
            nc.gpsimd.memset(zeros[:], 0.0).then_inc(consts0, 1)
            nc.gpsimd.memset(v_all[:], 1.0).then_inc(consts, 1)
            nc.gpsimd.memset(cbd[:], 0.0).then_inc(consts, 1)
            nc.gpsimd.iota(node[:], [[1, NB]], base=0, channel_multiplier=0,
                           allow_small_or_imprecise_dtypes=True).then_inc(consts, 1)
            pool.wait_ge(consts0, 2)
            nc.gpsimd.affine_select(out=ident[:], in_=ones[:], compare_op=ALU.is_equal, fill=0.0, base=0,
                                    pattern=[[-1, P]], channel_multiplier=1).then_inc(consts, 1)

        @block.vector
        def _(dve):
            dve.wait_ge(loaded, 16 * LOADS)
            dve.wait_ge(consts, 4)
            with dve.Fori(0, BLOCKS) as i:
                nc.vector.bn_stats(stats[:, bass.ds(i, 1), :].rearrange("p a s -> p (a s)"),
                                   x_all[:, bass.ds(i, 1), :].rearrange("p a d -> p (a d)")).then_inc(dve_chain, 1)
            dve.wait_ge(dve_chain, BLOCKS)
            ch = Chain(dve, dve_chain, BLOCKS)
            mean_and_variance(nc, ch, stats, mean[:], rstd[:])
            ch.link(nc.vector.memset(eps[:], EPS))
            nc.vector.tensor_copy(stats[:, :, 0], rstd[:]).then_inc(var_ready, 1)
            dve.wait_ge(std_ready, 1)
            ch.link(nc.vector.reciprocal(rstd[:], rstd[:]))
            base = ch.base + ch.n
            PER = 4
            with dve.Fori(0, BLOCKS // U) as i:
                for u in range(U):
                    n = U * i + u
                    ch = Chain(dve, dve_chain, base + PER * n)
                    xb = x_all[:, bass.ds(n, 1), :].rearrange("p a d -> p (a d)")
                    nc.vector.tensor_scalar(xn[:, u, :], xb, mean[:, bass.ds(n, 1)], rstd[:, bass.ds(n, 1)],
                                            ALU.subtract, ALU.mult).then_inc(normed, 1)
                    dve.wait_ge(h_kept, n + 1)
                    nc.vector.tensor_tensor(prod[:, u, 0, :], hrow[:, u, 0:D], attS[:], ALU.mult).then_inc(dve_chain, 1)
                    nc.vector.tensor_tensor(prod[:, u, 1, :], hrow[:, u, 0:D], attD[:], ALU.mult).then_inc(dve_chain, 1)
                    ch.n += 2
                    dve.wait_ge(dve_chain, base + PER * n + ch.n)
                    ch.link(nc.vector.reduce_sum(as_all[:, bass.ds(n, 1), :],
                                                 prod[:, u, 0, :].rearrange("p (a h c) -> p a h c", a=1, h=GH), AX_X))
                    ch.link(nc.vector.reduce_sum(ad_m[:, bass.ds(n, 1), 0:GH],
                                                 prod[:, u, 1, :].rearrange("p (a h c) -> p a h c", a=1, h=GH), AX_X))
                    assert ch.n == PER
                    nc.vector.tensor_scalar(hrow[:, u, D:ROW].rearrange("p (a h) -> p a h", a=1),
                                            as_all[:, bass.ds(n, 1), :], 1.0, None, ALU.mult).then_inc(logits_kept, 1)
            done = base + PER * BLOCKS
            ch = Chain(dve, dve_chain, done)
            dve.wait_ge(qk_kept, BLOCKS)
            nc.vector.tensor_reduce(nmax[:], qk[:, :, NB:], mybir.AxisListType.XY, ALU.max, negate=True).then_inc(max_known, 1)
            with dve.Fori(0, BLOCKS // U) as i:
                for u in range(U):
                    n = U * i + u
                    dve.wait_ge(k_turned, n + 1)
                    dve.wait_ge(context_part, (U * i) if u == 0 else (U * i))
                    nc.vector.tensor_copy(kxT[:, u, :], psT[0:NB, u, 0:MW]).then_inc(k_kept, 1)
            dve.wait_ge(context_part, BLOCKS + 1)
            ch.link(nc.vector.reciprocal(rk[:], psC[:, MW:MW + 1]))
            for h in range(MH):
                s = slice(h * MD, (h + 1) * MD)
                last = nc.vector.tensor_scalar(cbd[s, s], psC[s, s], rk[s, :], float(MD) ** -0.5, ALU.mult, ALU.mult)
                last.then_inc(context_masked, 1)
            dve.wait_ge(context_turned, 1)
            nc.vector.tensor_copy(cbdT[:], psT[:, 0, 0:MW]).then_inc(context_kept, 1)
            dve.wait_ge(m_ready, 1)
            nc.vector.tensor_copy(m_sb[:], psQ[:, 0, 0:D]).then_inc(m_kept, 1)
            with dve.Fori(0, BLOCKS // U) as i:
                for u in range(U):
                    n = U * i + u
                    dve.wait_ge(mixed, n + 1)
                    xb = x_all[:, bass.ds(n, 1), :]
                    nc.vector.tensor_tensor(xb, xb, psH[:, u, 0:D].rearrange("p (a d) -> p a d", a=1), ALU.add) \
                        .then_inc(mix_added, 1)

        @block.scalar
        def _(act):
            act.wait_ge(var_ready, 1)
            nc.scalar.activation(rstd[:], stats[:, :, 0], ACT.Sqrt, bias=eps[:]).then_inc(std_ready, 1)
            with act.Fori(0, BLOCKS // U) as i:
                for u in range(U):
                    n = U * i + u
                    act.wait_ge(turned, n + 1)
                    nc.scalar.copy(xnT[:, u, :, :], psT[:, u, 0:KC * NB].rearrange("p (c n) -> p c n", c=KC)) \
                        .then_inc(turned_sb, 1)
                    act.wait_ge(projected, n + 1)
                    nc.scalar.copy(qk[:, bass.ds(n, 1), :], psQ[:, u, 0:2 * NB].rearrange("p (a n) -> p a n", a=1)) \
                        .then_inc(qk_kept, 1)
                    act.wait_ge(row_stored[u], 16 * i)
                    nc.scalar.copy(hrow[:, u, 0:D], psH[:, u, 0:D]).then_inc(h_kept, 1)
                    nc.scalar.copy(v_all[:, bass.ds(n, 1), 0:MW],
                                   psH[:, u, D:D + MW].rearrange("p (a h) -> p a h", a=1)).then_inc(v_kept, 1)
            act.wait_ge(max_known, 1)
            with act.Fori(0, BLOCKS // U) as i:
                for u in range(U):
                    n = U * i + u
                    act.wait_ge(k_turned, U * i)
                    nc.scalar.activation(kx[:, u, :], qk[:, bass.ds(n, 1), NB:].rearrange("p a n -> p (a n)"), ACT.Exp, bias=nmax[:]) \
                        .then_inc(k_exp, 1)
            with act.Fori(0, BLOCKS // U) as i:
                for u in range(U):
                    n = U * i + u
                    act.wait_ge(mixed, U * i)
                    nc.scalar.copy(qs[:, u, :], qk[:, bass.ds(n, 1), 0:NB].rearrange("p a n -> p (a n)")).then_inc(q_staged, 1)

        @block.tensor
        def _(pe):
            pe.wait_ge(loaded, 16 * LOADS)
            pe.wait_ge(consts, 4)
            with pe.Fori(0, BLOCKS // U) as i:
                for u in range(U):
                    n = U * i + u
                    pe.wait_ge(normed, n + 1)
                    for c in range(KC):
                        last = nc.tensor.transpose(psT[:, u, c * NB:(c + 1) * NB], xn[:, u, c * P:(c + 1) * P],
                                                   ident[0:NB, 0:NB])
                    last.then_inc(turned, 1)
                    pe.wait_ge(turned_sb, n + 1)
                    pe.wait_ge(v_kept, U * i)
                    for w, a, b in ((w_sb[:], 0, D), (qkv_sb[:, :, 2 * MW:], D, D + MW)):
                        for c in range(KC):
                            nc.tensor.matmul(psH[:, u, a:b], xnT[:, u, c, :], w[:, c, :], start=c == 0,
                                             stop=c == KC - 1)
                    for t in range(2):
                        for c in range(KC):
                            last = nc.tensor.matmul(psQ[:, u, t * NB:(t + 1) * NB], qkv_sb[:, c, t * MW:(t + 1) * MW],
                                                    xnT[:, u, c, :], start=c == 0, stop=c == KC - 1)
                    last.then_inc(projected, 1)
            nc.tensor.matmul(psC[:, 0:MW + 1], zeros[:, 0:P], zeros[:, 0:MW + 1], start=True, stop=False,
                             skip_group_check=True).then_inc(context_part, 1)
            with pe.Fori(0, BLOCKS // U) as i:
                for u in range(U):
                    n = U * i + u
                    pe.wait_ge(k_exp, n + 1)
                    pe.wait_ge(k_kept, U * i)
                    nc.tensor.transpose(psT[0:NB, u, 0:MW], kx[:, u, :], ident[:]).then_inc(k_turned, 1)
                    pe.wait_ge(k_kept, n + 1)
                    nc.tensor.matmul(psC[:, 0:MW + 1], kxT[:, u, :],
                                     v_all[:, bass.ds(n, 1), :].rearrange("p a d -> p (a d)"), start=False,
                                     stop=False, skip_group_check=True).then_inc(context_part, 1)
            pe.wait_ge(context_masked, MH)
            nc.tensor.transpose(psT[:, 0, 0:MW], cbd[:], ident[:]).then_inc(context_turned, 1)
            pe.wait_ge(context_kept, 1)
            nc.tensor.matmul(psQ[:, 0, 0:D], cbdT[:], wout_sb[:], start=True, stop=True).then_inc(m_ready, 1)
            pe.wait_ge(m_kept, 1)
            with pe.Fori(0, BLOCKS // U) as i:
                for u in range(U):
                    n = U * i + u
                    pe.wait_ge(q_staged, n + 1)
                    pe.wait_ge(mix_added, U * i)
                    nc.tensor.matmul(psH[:, u, 0:D], qs[:, u, :], m_sb[:], start=True, stop=False)
                    nc.tensor.matmul(psH[:, u, 0:D], ones[0:1, 0:NB], brow[:, 0, :], start=False, stop=False)
                    nc.tensor.matmul(psH[:, u, 0:D], ones[0:1, 0:NB], brow[:, 1, :], start=False, stop=True) \
                        .then_inc(mixed, 1)


def schedule(nc, scope, src, dst, ones, as_all, ad_m, ex_self, agg, src_i, dst_f, neg_base, step_group, step_block,
             sweeps):
    with ExitStack() as ctx:
        sb, ps, sem = scope(ctx)
        dst_i = sb("dst_i", [EP, GROUPS, GT], I32)
        rows = sb("rows", [CH, 2, CHUNKS, EP * GT], I32)
        ext = sb("ext", [CH, 3, CHUNKS])
        extb = sb("extb", [CH, 3, CHUNKS])
        exti = sb("exti", [CH, 3, CHUNKS], I32)
        extt = sb("extt", [CH, 3, CHUNKS])
        gid = sb("gid", [CH, CHUNKS])
        stp = sb("stp", [P, LISTED])
        below = sb("below", [CH, CHUNKS, LISTED])
        broken = sb("broken", [CH, CHUNKS])
        flag = sb("flag", [EP, 1])
        keep = sb("keep", [EP, 1])
        grp = sb("grp", [EP, LISTED])
        alt = sb("alt", [EP, LISTED])
        top = sb("top", [NB, GH])
        topall = sb("topall", [NB, GH])
        s_self = sb("s_self", [NB, BLOCKS, GH])
        s_top = sb("s_top", [NB, BLOCKS, GH])
        psG = ps("psG", [EP, 512])
        psF = ps("psF", [EP, 512])
        loaded = sem("sched_loaded")
        prev0 = sem("prev0")
        iotas = sem("iotas")
        chain = sem("sched_chain")
        marks = sem("marks")
        counted = sem("counted")
        top_known = sem("top_known")
        top_shared = sem("top_shared")
        self_shifted = sem("self_shifted")
        self_weight = sem("self_weight")
        block = ctx.enter_context(nc.Block())
        L = EP * GT

        @block.sync
        def _(sp):
            sp.dma_start(rows[:, 0, :, :], dst.rearrange("(c p e) -> p c e", c=CHUNKS, e=L)).then_inc(loaded, 16)
            sp.wait_ge(prev0, 1)
            sp.dma_start(rows[1:CH, 1, 0, :], dst[0:(CH - 1) * L].rearrange("(p e) -> p e", e=L)).then_inc(loaded, 16)
            for c in range(1, CHUNKS):
                a = (c * CH - 1) * L
                sp.dma_start(rows[:, 1, c, :], dst[a:a + CH * L].rearrange("(p e) -> p e", e=L)).then_inc(loaded, 16)
            sp.dma_start(src_i[:], src.rearrange("(g p j) -> p g j", p=EP, j=GT)).then_inc(loaded, 16)
            sp.dma_start(dst_i[:], dst.rearrange("(g p j) -> p g j", p=EP, j=GT)).then_inc(loaded, 16)

        @block.gpsimd
        def _(pool):
            nc.gpsimd.memset(rows[0:1, 1, 0, :], 0).then_inc(prev0, 1)
            nc.gpsimd.iota(gid[:], [[CH, CHUNKS]], base=0, channel_multiplier=1,
                           allow_small_or_imprecise_dtypes=True).then_inc(iotas, 1)
            nc.gpsimd.iota(stp[:], [[1, LISTED]], base=0, channel_multiplier=0,
                           allow_small_or_imprecise_dtypes=True).then_inc(iotas, 1)
            nc.gpsimd.memset(agg[:], 0.0).then_inc(iotas, 1)
            pool.wait_ge(top_known, 1)
            nc.gpsimd.partition_all_reduce(topall[:], top[:], NB, RMAX).then_inc(top_shared, 1)

        @block.vector
        def _(dve):
            ch = Chain(dve, chain)
            V = nc.vector
            V.tensor_reduce(top[:], as_all[:].rearrange("p b h -> p h b"), AX_X, ALU.max).then_inc(top_known, 1)
            ch.link(V.tensor_tensor(s_self[:], as_all[:], ad_m[:, :, 0:GH], ALU.add))
            ch.link(V.scalar_tensor_tensor(s_self[:], s_self[:], SLOPE, s_self[:], ALU.mult, ALU.max))
            dve.wait_ge(top_shared, 1)
            ch.link(V.tensor_tensor(s_top[:], ad_m[:, :, 0:GH], bcast(topall[:], 1, BLOCKS), ALU.add))
            ch.link(V.scalar_tensor_tensor(s_top[:], s_top[:], SLOPE, s_top[:], ALU.mult, ALU.max))
            ch.link(V.scalar_tensor_tensor(ad_m[:, :, GH:], s_self[:], SPREAD, s_top[:], ALU.add, ALU.min))
            V.tensor_tensor(s_self[:], s_self[:], ad_m[:, :, GH:], ALU.subtract).then_inc(self_shifted, 1)

            dve.wait_ge(loaded, 16 * (CHUNKS + 3))
            dve.wait_ge(iotas, 3)
            ch.link(V.tensor_scalar(src_i[:], src_i[:], N - 1, None, ALU.min))
            ch.link(V.tensor_copy(dst_f[:], dst_i[:]))
            ch.link(V.tensor_reduce(ext[:, 0, :], rows[:, 0, :, :], AX_X, ALU.max))
            ch.link(V.tensor_reduce(ext[:, 1, :], rows[:, 0, :, :], AX_X, ALU.min))
            ch.link(V.tensor_reduce(ext[:, 2, :], rows[:, 1, :, :], AX_X, ALU.max))
            ch.link(V.tensor_scalar(ext[:], ext[:], float(N - 1), None, ALU.min))
            floor_div(nc, ch, ext[:], extb[:], exti[:], extt[:], NB)
            ch.link(V.tensor_tensor(broken[:], extb[:, 2, :], extb[:, 1, :], ALU.is_gt))
            ch.link(V.tensor_tensor(gid[:], gid[:], extb[:, 0, :], ALU.add))
            for c in range(CHUNKS):
                V.tensor_scalar(below[:, c, :], stp[0:CH, :], gid[:, c:c + 1], None, ALU.is_gt).then_inc(marks, 1)
            dve.wait_ge(counted, 1)
            ch.link(V.tensor_reduce(flag[:], psF[:, 0:CHUNKS], AX_X, ALU.max))
            ch.link(V.tensor_scalar(flag[:], flag[:], 0.5, None, ALU.is_gt))
            ch.link(V.tensor_scalar(keep[:], flag[:], -1.0, 1.0, ALU.mult, ALU.add))
            ch.link(V.tensor_scalar(sweeps[:], flag[:], float(BLOCKS - 1), 1.0, ALU.mult, ALU.add))
            ch.link(V.tensor_scalar(grp[:], psG[:, 0:LISTED], float(GROUPS - 1), None, ALU.min))
            ch.link(V.tensor_tensor(alt[:], stp[0:EP, :], grp[:], ALU.subtract))
            ch.link(V.tensor_scalar(alt[:], alt[:], float(BLOCKS - 1), keep[:], ALU.min, ALU.mult))
            ch.link(V.tensor_copy(step_block[:, 1:], alt[:]))
            ch.link(V.tensor_copy(step_block[:, 0:1], alt[:, 0:1]))
            ch.link(V.tensor_scalar(neg_base[:], alt[:], float(-NB), None, ALU.mult))
            ch.link(V.tensor_scalar(alt[:], stp[0:EP, :], GROUPS - 0.5, flag[:], ALU.is_gt, ALU.mult))
            ch.link(V.scalar_tensor_tensor(neg_base[:], alt[:], FAR, neg_base[:], ALU.mult, ALU.add))
            ch.link(V.memset(neg_base[:, PAIRS:], FAR))
            ch.link(V.tensor_scalar(grp[:], grp[:], keep[:], None, ALU.mult))
            ch.link(V.tensor_scalar(alt[:], stp[0:EP, :], float(GROUPS - 1), flag[:], ALU.min, ALU.mult))
            ch.link(V.tensor_tensor(grp[:], grp[:], alt[:], ALU.add))
            ch.link(V.tensor_copy(step_group[:], grp[:]))

        @block.scalar
        def _(act):
            act.wait_ge(self_shifted, 1)
            nc.scalar.activation(ex_self[:], s_self[:], ACT.Exp).then_inc(self_weight, 1)

        @block.tensor
        def _(pe):
            pe.wait_ge(marks, CHUNKS)
            for c in range(CHUNKS):
                k = CH - (c == CHUNKS - 1)
                nc.tensor.matmul(psG[:, 0:LISTED], ones[0:k, 0:EP], below[0:k, c, :], start=c == 0,
                                 stop=c == CHUNKS - 1)
            nc.tensor.matmul(psF[:, 0:CHUNKS], ones[0:CH, 0:EP], broken[:], start=True, stop=True).then_inc(counted, 1)


def edges(nc, scope, table, ident, zeros, node, ad_m, agg, src_i, dst_f, neg_base, step_group, step_block, sweeps):
    with ExitStack() as ctx:
        sb, ps, sem = scope(ctx)
        idx = sb("idx", [EP, SLOTS, GT], I32)
        rel = sb("rel", [EP, SLOTS, GT])
        msg = sb("msg", [EP, SLOTS, GT, ROW])
        hot = sb("hot", [EP, SLOTS, GT, NB])
        hotT = sb("hotT", [NB, 2, GT, EP])
        lg = sb("lg", [EP, SLOTS, GT, GH])
        psT = ps("psT_e", [NB, 2, 512])
        psD = ps("psD_e", [EP, 2, 512])
        psS = ps("psS_e", [NB, 2, 512])
        staged = sem("staged")
        opened = sem("opened")
        gathered = [sem(f"gathered{u}") for u in range(SLOTS)]
        hot_ready = sem("hot_ready")
        hot_turned = sem("hot_turned")
        hotT_ready = sem("hotT_ready")
        dst_picked = sem("dst_picked")
        logits = sem("logits")
        weights = sem("weights")
        weighed = sem("weighed")
        summed = sem("summed")
        added = sem("added")
        chain = sem("edge_chain")
        moved = sem("moved")
        block = ctx.enter_context(nc.Block())
        TRIPS = STEPS // SLOTS
        assert TRIPS * SLOTS == STEPS

        def count(eng):
            return eng.value_load(sweeps[0:1, 0:1], min_val=1, max_val=BLOCKS)

        @block.gpsimd
        def _(pool):
            n_sweeps = count(pool)
            with pool.Fori(0, n_sweeps) as s:
                with pool.Fori(0, TRIPS) as i:
                    for u in range(SLOTS):
                        pool.wait_ge(staged, s * LISTED + i * SLOTS + (u + 1))
                        pool.sem_inc(opened, 1)
                        for j in range(GT):
                            nc.gpsimd.indirect_dma_start(
                                msg[:, u, j, :], None, table[:, :],
                                bass.IndirectOffsetOnAxis(ap=idx[:, u, j:j + 1], axis=0)).then_inc(gathered[u], 16)

        @block.scalar
        def _(act):
            n_sweeps = count(act)

            def stage(at, u, free, done):
                g = act.value_load(step_group[0:1, bass.ds(at, 1)], min_val=0, max_val=GROUPS - 1)
                act.wait_ge(free, done)
                nc.scalar.copy(idx[:, u, :], src_i[:, bass.ds(g, 1), :].rearrange("p a j -> p (a j)"))
                nc.scalar.activation(rel[:, u, :], dst_f[:, bass.ds(g, 1), :].rearrange("p a j -> p (a j)"),
                                     ACT.Identity, bias=neg_base[:, bass.ds(at, 1)]).then_inc(staged, 1)

            def keep_turned(u, done):
                act.wait_ge(hot_turned, done)
                nc.scalar.copy(hotT[:, u % 2, :, :], psT[:, u % 2, 0:GT * EP].rearrange("p (j e) -> p j e", j=GT)) \
                    .then_inc(hotT_ready, 1)

            with act.Fori(0, n_sweeps) as s:
                for a in range(AHEAD):
                    stage(a, a, moved, 2 * s + 1)
                keep_turned(0, s * (STEPS + 2) + 1)
                with act.Fori(0, TRIPS) as i:
                    for u in range(SLOTS):
                        act.wait_ge(logits, s * STEPS + i * SLOTS + (u + 1))
                        nc.scalar.activation(msg[:, u, :, D:ROW], lg[:, u, :, :], ACT.Exp).then_inc(weights, 1)
                        keep_turned(u + 1, s * (STEPS + 2) + i * SLOTS + (u + 2))
                        stage(i * SLOTS + (u + AHEAD), (u + AHEAD) % SLOTS, summed,
                              s * (STEPS + 1) + i * SLOTS + (u + 2))

        @block.vector
        def _(dve):
            dve.sem_inc(moved, 1)
            n_sweeps = count(dve)
            PER = 3

            def one_hot(u, done):
                dve.wait_ge(staged, done)
                nc.vector.tensor_tensor(hot[:, u, :, :], bcast(node[0:EP, :], 1, GT), bcast(rel[:, u, :], 2, NB),
                                        ALU.is_equal).then_inc(hot_ready, 1)

            def add(at, bank, s):
                b = dve.value_load(step_block[0:1, bass.ds(at, 1)], min_val=0, max_val=BLOCKS - 1)
                to = agg[:, bass.ds(b, 1), :]
                dve.wait_ge(summed, s * (STEPS + 1) + at + (1 + AHEAD))
                dve.wait_ge(added, s * (STEPS + 1) + at + 1)
                nc.vector.tensor_tensor(to, to, psS[:, bank, 0:ROW].rearrange("p (a r) -> p a r", a=1),
                                        ALU.add).then_inc(added, 1)

            with dve.Fori(0, n_sweeps) as s:
                one_hot(0, s * LISTED + 1)
                one_hot(1, s * LISTED + 2)
                with dve.Fori(0, TRIPS) as i:
                    for u in range(SLOTS):
                        k = s * STEPS + i * SLOTS + u
                        ch = Chain(dve, chain, PER * k)
                        dve.wait_ge(gathered[u], (s * TRIPS + i + 1) * (16 * GT))
                        dve.wait_ge(dst_picked, s * (STEPS + 1) + i * SLOTS + (u + 1))
                        pick = psD[:, u % 2, 0:GT * 2 * GH].rearrange("p (j f) -> p j f", j=GT)
                        ch.link(nc.vector.tensor_tensor(lg[:, u, :, :], msg[:, u, :, D:ROW], pick[:, :, 0:GH], ALU.add))
                        ch.link(nc.vector.scalar_tensor_tensor(lg[:, u, :, :], lg[:, u, :, :], SLOPE, lg[:, u, :, :],
                                                               ALU.mult, ALU.max))
                        ch.link(nc.vector.tensor_tensor(lg[:, u, :, :], lg[:, u, :, :], pick[:, :, GH:], ALU.subtract))
                        nc.vector.tensor_scalar(lg[:, u, :, :], lg[:, u, :, :], 80.0, None, ALU.min).then_inc(logits, 1)
                        assert ch.n == PER
                        one_hot((u + 2) % SLOTS, s * LISTED + i * SLOTS + (u + 3))
                        add(i * SLOTS + u, (u + 1) % 2, s)
                        dve.wait_ge(weights, k + 1)
                        m = msg[:, u, :, 0:D].rearrange("p j (h c) -> p j h c", h=GH)
                        nc.vector.tensor_tensor(m, m, bcast(msg[:, u, :, D:ROW], 3, GC), ALU.mult).then_inc(weighed, 1)
                add(STEPS, (STEPS + 1) % 2, s)
                dve.wait_ge(staged, (s + 1) * LISTED)
                dve.wait_ge(dst_picked, (s + 1) * (STEPS + 1))
                dve.wait_ge(added, (s + 1) * (STEPS + 1) + 1)
                nc.vector.tensor_scalar(neg_base[:], neg_base[:], float(-NB), None, ALU.add).then_inc(moved, 1)
                nc.vector.tensor_scalar(step_block[:], step_block[:], 1, None, ALU.add).then_inc(moved, 1)
                dve.wait_ge(moved, 2 * s + 3)

        @block.tensor
        def _(pe):
            pe.sem_inc(summed, AHEAD)
            pe.sem_inc(added, 1)
            n_sweeps = count(pe)

            def turn(u, done):
                pe.wait_ge(hot_ready, done)
                for j in range(GT):
                    last = nc.tensor.transpose(psT[:, u % 2, j * EP:(j + 1) * EP], hot[:, u, j, :],
                                               ident[0:EP, 0:EP])
                last.then_inc(hot_turned, 1)

            def pick(at, u, done):
                b = pe.value_load(step_block[0:1, bass.ds(at + 1, 1)], min_val=0, max_val=BLOCKS - 1)
                pe.wait_ge(hotT_ready, done)
                for j in range(GT):
                    last = nc.tensor.matmul(psD[:, u % 2, j * 2 * GH:(j + 1) * 2 * GH], hotT[:, u % 2, j, :],
                                            ad_m[:, bass.ds(b, 1), :].rearrange("p a f -> p (a f)"),
                                            start=True, stop=True)
                last.then_inc(dst_picked, 1)

            with pe.Fori(0, n_sweeps) as s:
                turn(0, s * (STEPS + 2) + 1)
                turn(1, s * (STEPS + 2) + 2)
                pick(0, 0, s * (STEPS + 2) + 1)
                pe.wait_ge(added, s * (STEPS + 1) + 1)
                nc.tensor.matmul(psS[:, 1, 0:ROW], zeros[:, 0:NB], zeros[:, 0:ROW], start=True, stop=True) \
                    .then_inc(summed, 1)
                with pe.Fori(0, TRIPS) as i:
                    for u in range(SLOTS):
                        k = i * SLOTS + u
                        pick(k + 1, u + 1, s * (STEPS + 2) + k + 2)
                        pe.wait_ge(weighed, s * STEPS + k + 1)
                        pe.wait_ge(added, s * (STEPS + 1) + k + 1)
                        for j in range(GT):
                            last = nc.tensor.matmul(psS[:, u % 2, 0:ROW], hot[:, u, j, :], msg[:, u, j, :],
                                                    start=j == 0, stop=j == GT - 1)
                        last.then_inc(summed, 1)
                        turn((u + 2) % SLOTS, s * (STEPS + 2) + k + 3)


def nodes(nc, scope, table, W_gat, xatt_src, xatt_dst, xtable, xtable_dst, x_all, ident, agg, ex_self, xnT_all,
          hg_all, xad_all, row):
    U = 2
    with ExitStack() as ctx:
        sb, ps, sem = scope(ctx)
        wg = sb("wg", [P, KC, XF])
        atS = sb("atS", [NB, XF])
        atD = sb("atD", [NB, XF])
        hs = sb("hs", [NB, U, D])
        den = sb("den", [NB, U, GH])
        num = sb("num", [NB, U, D])
        stats = sb("stats_n", [NB, BLOCKS, 6])
        mean = sb("mean_n", [NB, BLOCKS])
        rstd = sb("rstd_n", [NB, BLOCKS])
        eps = sb("eps_n", [NB, 1])
        xn = sb("xn_n", [NB, U, D])
        xT = sb("xT_n", [P, U, KC, NB])
        prod = sb("prod_n", [NB, BLOCKS, XF])
        top = sb("top_n", [NB, XH])
        topall = sb("topall_n", [NB, XH])
        s_self = sb("s_self_n", [NB, BLOCKS, XH])
        s_top = sb("s_top_n", [NB, BLOCKS, XH])
        psT = ps("psT_n", [P, U, 512])
        psG = ps("psG_n", [NB, U, 512])
        loaded = sem("loaded_n")
        h_back = [sem(f"h_back{u}") for u in range(U)]
        h_used = sem("h_used")
        chain = sem("chain_n")
        measured = sem("measured_n")
        var_ready = sem("var_ready_n")
        std_ready = sem("std_ready_n")
        normed = sem("normed_n")
        turned = sem("turned_n")
        kept = sem("kept_n")
        projected = sem("projected_n")
        proj_kept = sem("proj_kept_n")
        top_known = sem("top_known_n")
        top_shared = sem("top_shared_n")
        tables = sem("tables_n")
        stored = sem("stored_n")
        block = ctx.enter_context(nc.Block())

        @block.sync
        def _(sp):
            sp.dma_start(wg[:], W_gat.rearrange("(c p) n -> p c n", p=P)).then_inc(loaded, 16)
            for tile, vec in ((atS, xatt_src), (atD, xatt_dst)):
                sp.dma_start(tile[:], row(vec.rearrange("h c -> (h c)")).to_broadcast([NB, XF])).then_inc(loaded, 16)
            with sp.Fori(0, BLOCKS // U) as i:
                for u in range(U):
                    sp.wait_ge(h_used, U * i)
                    sp.dma_start(hs[:, u, :], table[bass.ds((U * i + u) * NB, NB), 0:D]).then_inc(h_back[u], 16)
            sp.wait_ge(tables, 1)
            sp.dma_start(xtable.rearrange("(b p) f -> p b f", p=NB), hg_all[:]).then_inc(stored, 16)
            sp.dma_start(xtable_dst.rearrange("(b p) f -> p b f", p=NB), xad_all[:]).then_inc(stored, 16)
            sp.wait_ge(stored, 32)

        @block.vector
        def _(dve):
            V = nc.vector
            PER = 6
            dve.wait_ge(loaded, 48)
            with dve.Fori(0, BLOCKS // U) as i:
                for u in range(U):
                    n = U * i + u
                    ch = Chain(dve, chain, PER * n)
                    xb = x_all[:, bass.ds(n, 1), :].rearrange("p a d -> p (a d)")
                    ex = ex_self[:, bass.ds(n, 1), :].rearrange("p a h -> p (a h)")
                    ag = agg[:, bass.ds(n, 1), :].rearrange("p a r -> p (a r)")
                    hsu = hs[:, u, :].rearrange("p (h c) -> p h c", h=GH)
                    numu = num[:, u, :].rearrange("p (h c) -> p h c", h=GH)
                    dve.wait_ge(h_back[u], 16 * (i + 1))
                    ch.link(V.tensor_tensor(numu, hsu, bcast(ex, 2, GC), ALU.mult))
                    V.tensor_tensor(num[:, u, :], num[:, u, :], ag[:, 0:D], ALU.add).then_inc(h_used, 1)
                    ch.link(V.tensor_tensor(den[:, u, :], ag[:, D:ROW], ex, ALU.add))
                    ch.link(V.scalar_tensor_tensor(den[:, u, :], ex, 1e-16, den[:, u, :], ALU.mult, ALU.add))
                    ch.link(V.reciprocal(den[:, u, :], den[:, u, :]))
                    dve.wait_ge(h_used, n + 1)
                    ch.link(V.tensor_tensor(numu, numu, bcast(den[:, u, :], 2, GC), ALU.mult))
                    ch.link(V.tensor_tensor(xb, xb, num[:, u, :], ALU.add))
                    assert ch.n == PER
                    V.bn_stats(stats[:, bass.ds(n, 1), :].rearrange("p a s -> p (a s)"), xb).then_inc(measured, 1)
            ch = Chain(dve, chain, PER * BLOCKS)
            dve.wait_ge(measured, BLOCKS)
            mean_and_variance(nc, ch, stats, mean[:], rstd[:])
            ch.link(V.memset(eps[:], EPS))
            V.tensor_copy(stats[:, :, 0], rstd[:]).then_inc(var_ready, 1)
            dve.wait_ge(std_ready, 1)
            ch.link(V.reciprocal(rstd[:], rstd[:]))
            with dve.Fori(0, BLOCKS // U) as i:
                for u in range(U):
                    n = U * i + u
                    dve.wait_ge(turned, U * i)
                    V.tensor_scalar(xn[:, u, :], x_all[:, bass.ds(n, 1), :].rearrange("p a d -> p (a d)"),
                                    mean[:, bass.ds(n, 1)], rstd[:, bass.ds(n, 1)], ALU.subtract, ALU.mult) \
                        .then_inc(normed, 1)
            dve.wait_ge(proj_kept, BLOCKS)
            h4 = hg_all[:, :, 0:XF]
            ch.link(V.tensor_tensor(prod[:], h4, bcast(atS[:], 1, BLOCKS), ALU.mult))
            ch.link(V.reduce_sum(hg_all[:, :, XF:], prod[:].rearrange("p b (h e) -> p b h e", h=XH), AX_X))
            ch.link(V.tensor_tensor(prod[:], h4, bcast(atD[:], 1, BLOCKS), ALU.mult))
            ch.link(V.reduce_sum(xad_all[:, :, 0:XH], prod[:].rearrange("p b (h e) -> p b h e", h=XH), AX_X))
            V.tensor_reduce(top[:], hg_all[:, :, XF:].rearrange("p b h -> p h b"), AX_X, ALU.max).then_inc(top_known, 1)
            ch.link(V.tensor_tensor(s_self[:], hg_all[:, :, XF:], xad_all[:, :, 0:XH], ALU.add))
            ch.link(V.scalar_tensor_tensor(s_self[:], s_self[:], SLOPE, s_self[:], ALU.mult, ALU.max))
            dve.wait_ge(top_shared, 1)
            ch.link(V.tensor_tensor(s_top[:], xad_all[:, :, 0:XH], bcast(topall[:], 1, BLOCKS), ALU.add))
            ch.link(V.scalar_tensor_tensor(s_top[:], s_top[:], SLOPE, s_top[:], ALU.mult, ALU.max))
            V.scalar_tensor_tensor(xad_all[:, :, XH:], s_self[:], SPREAD, s_top[:], ALU.add, ALU.min) \
                .then_inc(tables, 1)

        @block.gpsimd
        def _(pool):
            pool.wait_ge(top_known, 1)
            nc.gpsimd.partition_all_reduce(topall[:], top[:], NB, RMAX).then_inc(top_shared, 1)

        @block.scalar
        def _(act):
            act.wait_ge(var_ready, 1)
            nc.scalar.activation(rstd[:], stats[:, :, 0], ACT.Sqrt, bias=eps[:]).then_inc(std_ready, 1)
            with act.Fori(0, BLOCKS // U) as i:
                for u in range(U):
                    n = U * i + u
                    act.wait_ge(turned, n + 1)
                    pv = psT[:, u, 0:KC * NB].rearrange("p (c n) -> p c n", c=KC)
                    nc.scalar.copy(xnT_all[:, bass.ds(n, 1), :], psT[:, u, 0:KC * NB].rearrange("p (a n) -> p a n", a=1))
                    nc.scalar.copy(xT[:, u, :, :], pv).then_inc(kept, 1)
                    act.wait_ge(projected, n + 1)
                    nc.scalar.copy(hg_all[:, bass.ds(n, 1), 0:XF],
                                   psG[:, u, 0:XF].rearrange("p (a f) -> p a f", a=1)).then_inc(proj_kept, 1)

        @block.tensor
        def _(pe):
            pe.wait_ge(loaded, 48)
            with pe.Fori(0, BLOCKS // U) as i:
                for u in range(U):
                    n = U * i + u
                    pe.wait_ge(normed, n + 1)
                    pe.wait_ge(kept, U * i)
                    for c in range(KC):
                        last = nc.tensor.transpose(psT[:, u, c * NB:(c + 1) * NB], xn[:, u, c * P:(c + 1) * P],
                                                   ident[0:NB, 0:NB])
                    last.then_inc(turned, 1)
                    pe.wait_ge(kept, n + 1)
                    pe.wait_ge(proj_kept, U * i)
                    for c in range(KC):
                        last = nc.tensor.matmul(psG[:, u, 0:XF], xT[:, u, c, :], wg[:, c, :], start=c == 0,
                                                stop=c == KC - 1)
                    last.then_inc(projected, 1)


def gating(nc, scope, xedges, xtable, xtable_dst, b_gat, gamma, beta, zeros, node, hg_all, xad_all, gate, row):
    HALF = BLOCKS // 2
    with ExitStack() as ctx:
        sb, ps, sem = scope(ctx)
        bg = sb("bg", [NB, 3, XF])
        src_i = sb("xsrc_i", [P, XGROUPS, XT], I32)
        dst_i = sb("xdst_i", [P, XGROUPS, XT], I32)
        blk = sb("blk", [P, XGROUPS, XT])
        loc = sb("loc", [P, XGROUPS, XT])
        tmp = sb("tmp", [P, XGROUPS, XT])
        idx = sb("xidx", [P, XSLOTS, 2, XT], I32)
        pos = sb("pos", [P, XSLOTS, 2, XT])
        msg = sb("xmsg", [P, XSLOTS, XT, XROW])
        adm = sb("xadm", [P, XSLOTS, XT, 2 * XH])
        lo = sb("lo", [P, XSLOTS, XT, NB])
        hi = sb("hi", [P, XSLOTS, XT, BLOCKS])
        wide = sb("wide", [P, 2, XT, BLOCKS, XROW])
        lg = sb("xlg", [P, XSLOTS, XT, XH])
        bid = sb("bid", [P, BLOCKS])
        ext = sb("xext", [NB, BLOCKS, XH])
        num = sb("xnum", [NB, BLOCKS, XROW])
        a1 = sb("a1", [NB, BLOCKS, XF])
        red = sb("red", [NB, BLOCKS, 1])
        red2 = sb("red2", [NB, BLOCKS, 1])
        sc = sb("sc", [NB, BLOCKS, XE])
        rank = sb("rank", [NB, BLOCKS, XE])
        cmp = sb("cmp", [NB, BLOCKS, 1])
        first = sb("first", [NB, BLOCKS, XE])
        second = sb("second", [NB, BLOCKS, XE])
        acc = ps("acc", [NB, 2, 512])
        loaded = sem("loaded_g")
        iotas = sem("iotas_g")
        chain = sem("chain_g")
        prepared = sem("prepared")
        staged = sem("staged_g")
        opened = sem("opened_g")
        gathered = [sem(f"gathered_g{u}") for u in range(XSLOTS)]
        logits = sem("logits_g")
        weights = sem("weights_g")
        widened = sem("widened")
        summed = sem("summed_g")
        to_exp = sem("to_exp")
        exped = sem("exped")
        block = ctx.enter_context(nc.Block())
        TRIPS = XGROUPS // XSLOTS

        @block.sync
        def _(sp):
            v = xedges.rearrange("s (g p j) -> s p g j", p=P, j=XT)
            sp.dma_start(src_i[:], v[0]).then_inc(loaded, 16)
            sp.dma_start(dst_i[:], v[1]).then_inc(loaded, 16)
            for n, vec in enumerate((b_gat, gamma, beta)):
                sp.dma_start(bg[:, n, :], row(vec).to_broadcast([NB, XF])).then_inc(loaded, 16)

        @block.gpsimd
        def _(pool):
            nc.gpsimd.iota(bid[:], [[1, BLOCKS]], base=0, channel_multiplier=0,
                           allow_small_or_imprecise_dtypes=True).then_inc(iotas, 1)
            with pool.Fori(0, TRIPS) as i:
                for u in range(XSLOTS):
                    k = i * XSLOTS + u
                    pool.wait_ge(staged, k + 1)
                    pool.sem_inc(opened, 1)
                    for j in range(XT):
                        nc.gpsimd.indirect_dma_start(
                            msg[:, u, j, :], None, xtable[:, :],
                            bass.IndirectOffsetOnAxis(ap=idx[:, u, 0, j:j + 1], axis=0)).then_inc(gathered[u], 16)
                        nc.gpsimd.indirect_dma_start(
                            adm[:, u, j, :], None, xtable_dst[:, :],
                            bass.IndirectOffsetOnAxis(ap=idx[:, u, 1, j:j + 1], axis=0)).then_inc(gathered[u], 16)

        @block.scalar
        def _(act):
            act.wait_ge(prepared, 1)

            def stage(at, u):
                for s, (ints, where) in enumerate(((src_i, blk), (dst_i, loc))):
                    nc.scalar.copy(idx[:, u, s, :], ints[:, bass.ds(at, 1), :].rearrange("p a j -> p (a j)"))
                    last = nc.scalar.copy(pos[:, u, s, :], where[:, bass.ds(at, 1), :].rearrange("p a j -> p (a j)"))
                last.then_inc(staged, 1)

            def weigh(u, done):
                act.wait_ge(logits, done)
                nc.scalar.activation(msg[:, u, :, XF:], lg[:, u, :, :], ACT.Exp).then_inc(weights, 1)

            for a in range(XAHEAD):
                stage(a, a)
            with act.Fori(0, TRIPS - 1) as i:
                for u in range(XSLOTS):
                    k = i * XSLOTS + u
                    weigh(u, k + 1)
                    act.wait_ge(summed, k + 1)
                    stage(k + XAHEAD, (u + XAHEAD) % XSLOTS)
            for k in range(XGROUPS - XSLOTS, XGROUPS):
                weigh(k % XSLOTS, k + 1)
                if k + XAHEAD < XGROUPS:
                    act.wait_ge(summed, k + 1)
                    stage(k + XAHEAD, (k + XAHEAD) % XSLOTS)
            act.wait_ge(to_exp, 1)
            nc.scalar.activation(ext[:], ext[:], ACT.Exp).then_inc(exped, 1)
            act.wait_ge(to_exp, 2)
            nc.scalar.activation(red2[:], red2[:], ACT.Sqrt).then_inc(exped, 1)
            act.wait_ge(to_exp, 3)
            nc.scalar.activation(cmp[:], cmp[:], ACT.Exp).then_inc(exped, 1)

        @block.vector
        def _(dve):
            V = nc.vector
            ch = Chain(dve, chain)
            dve.wait_ge(loaded, 16 * 5)
            ch.link(V.tensor_copy(loc[:], dst_i[:]))
            floor_div(nc, ch, loc[:], blk[:], dst_i[:], tmp[:], NB)
            ch.link(V.tensor_scalar(dst_i[:], loc[:], float(N - 1), None, ALU.min))
            ch.link(V.scalar_tensor_tensor(loc[:], blk[:], float(-NB), loc[:], ALU.mult, ALU.add))
            dve.wait_ge(iotas, 1)
            V.tensor_scalar(src_i[:], src_i[:], N - 1, None, ALU.min).then_inc(prepared, 1)
            base = ch.n
            PER = 4
            with dve.Fori(0, TRIPS) as i:
                for u in range(XSLOTS):
                    k = i * XSLOTS + u
                    ch = Chain(dve, chain, base + PER * k)
                    dve.wait_ge(staged, k + 1)
                    V.tensor_tensor(lo[:, u, :, :], bcast(node[:], 1, XT), bcast(pos[:, u, 1, :], 2, NB), ALU.is_equal)
                    ch.link(V.tensor_tensor(hi[:, u, :, :], bcast(bid[:], 1, XT), bcast(pos[:, u, 0, :], 2, BLOCKS),
                                            ALU.is_equal))
                    dve.wait_ge(gathered[u], (i + 1) * (16 * 2 * XT))
                    l = lg[:, u, :, :]
                    ch.link(V.tensor_tensor(l, msg[:, u, :, XF:], adm[:, u, :, 0:XH], ALU.add))
                    ch.link(V.scalar_tensor_tensor(l, l, SLOPE, l, ALU.mult, ALU.max))
                    V.tensor_tensor(l, l, adm[:, u, :, XH:], ALU.subtract).then_inc(logits, 1)
                    dve.wait_ge(weights, k + 1)
                    m = msg[:, u, :, 0:XF].rearrange("p j (h e) -> p j h e", h=XH)
                    ch.link(V.tensor_tensor(m, m, bcast(msg[:, u, :, XF:], 3, XE), ALU.mult))
                    dve.wait_ge(summed, k + XAHEAD - 1)
                    for j in range(XT):
                        last = V.tensor_tensor(wide[:, u % 2, j], bcast(hi[:, u, j, :], 2, XROW),
                                               bcast(msg[:, u, j, :], 1, BLOCKS), ALU.mult)
                    last.then_inc(widened, 1)
                    assert ch.n == PER
            ch = Chain(dve, chain, base + PER * XGROUPS)
            dve.wait_ge(summed, XGROUPS + 1 + XAHEAD)
            ch.link(V.tensor_tensor(ext[:], hg_all[:, :, XF:], xad_all[:, :, 0:XH], ALU.add))
            ch.link(V.scalar_tensor_tensor(ext[:], ext[:], SLOPE, ext[:], ALU.mult, ALU.max))
            V.tensor_tensor(ext[:], ext[:], xad_all[:, :, XH:], ALU.subtract).then_inc(to_exp, 1)
            dve.wait_ge(exped, 1)

            def heads(t):
                return t.rearrange("p b (h e) -> p b h e", h=XH)

            ch.link(V.tensor_tensor(heads(num[:, :, 0:XF]), heads(hg_all[:, :, 0:XF]), bcast(ext[:], 3, XE), ALU.mult))
            for half in range(2):
                s = slice(half * HALF, (half + 1) * HALF)
                sums = acc[:, half, 0:HALF * XROW].rearrange("p (b r) -> p b r", r=XROW)
                ch.link(V.tensor_tensor(num[:, s, 0:XF], num[:, s, 0:XF], sums[:, :, 0:XF], ALU.add))
                ch.link(V.tensor_tensor(num[:, s, XF:], ext[:, s, :], sums[:, :, XF:], ALU.add))
            ch.link(V.scalar_tensor_tensor(num[:, :, XF:], ext[:], 1e-16, num[:, :, XF:], ALU.mult, ALU.add))
            ch.link(V.reciprocal(num[:, :, XF:], num[:, :, XF:]))
            ch.link(V.tensor_tensor(heads(a1[:]), heads(num[:, :, 0:XF]), bcast(num[:, :, XF:], 3, XE), ALU.mult))
            ch.link(V.tensor_tensor(a1[:], a1[:], bcast(bg[:, 0, :], 1, BLOCKS), ALU.add))
            r1 = red[:].rearrange("p b a -> p (b a)")
            r2 = red2[:].rearrange("p b a -> p (b a)")
            ch.link(V.reduce_sum(r1, a1[:], AX_X))
            ch.link(V.tensor_scalar(r1, r1, 1.0 / XF, None, ALU.mult))
            ch.link(V.tensor_tensor(a1[:], a1[:], bcast(r1, 2, XF), ALU.subtract))
            ch.link(V.tensor_tensor(num[:, :, 0:XF], a1[:], a1[:], ALU.mult))
            ch.link(V.reduce_sum(r2, num[:, :, 0:XF], AX_X))
            V.tensor_scalar(r2, r2, 1.0 / XF, EPS, ALU.mult, ALU.add).then_inc(to_exp, 1)
            dve.wait_ge(exped, 2)
            ch.link(V.reciprocal(r2, r2))
            ch.link(V.tensor_tensor(a1[:], a1[:], bcast(r2, 2, XF), ALU.mult))
            ch.link(V.tensor_tensor(a1[:], a1[:], bcast(bg[:, 1, :], 1, BLOCKS), ALU.mult))
            ch.link(V.tensor_tensor(a1[:], a1[:], bcast(bg[:, 2, :], 1, BLOCKS), ALU.add))
            ch.link(V.reduce_sum(sc[:], a1[:].rearrange("p b (h e) -> p b e h", h=XH), AX_X))
            ch.link(V.tensor_scalar(sc[:], sc[:], 1.0 / XH, None, ALU.mult))
            ch.link(V.memset(rank[:], 0.0))
            for e in range(XE):
                for o in range(XE):
                    if o != e:
                        op = ALU.is_ge if o < e else ALU.is_gt
                        ch.link(V.tensor_tensor(cmp[:], sc[:, :, o:o + 1], sc[:, :, e:e + 1], op))
                        ch.link(V.tensor_tensor(rank[:, :, e:e + 1], rank[:, :, e:e + 1], cmp[:], ALU.add))
            ch.link(V.tensor_scalar(first[:], rank[:], 0.0, None, ALU.is_equal))
            ch.link(V.tensor_scalar(second[:], rank[:], 1.0, None, ALU.is_equal))
            ch.link(V.tensor_tensor(rank[:], first[:], sc[:], ALU.mult))
            ch.link(V.reduce_sum(r1, rank[:], AX_X))
            ch.link(V.tensor_tensor(rank[:], second[:], sc[:], ALU.mult))
            ch.link(V.reduce_sum(r2, rank[:], AX_X))
            V.tensor_tensor(cmp[:], red2[:], red[:], ALU.subtract).then_inc(to_exp, 1)
            dve.wait_ge(exped, 3)
            ch.link(V.tensor_scalar(red[:], cmp[:], 1.0, None, ALU.add))
            ch.link(V.reciprocal(red[:], red[:]))
            ch.link(V.tensor_tensor(red2[:], red[:], cmp[:], ALU.mult))
            ch.link(V.tensor_tensor(first[:], first[:], bcast(r1, 2, XE), ALU.mult))
            ch.link(V.tensor_tensor(second[:], second[:], bcast(r2, 2, XE), ALU.mult))
            ch.link(V.tensor_tensor(gate[:], first[:], second[:], ALU.add))

        @block.tensor
        def _(pe):
            pe.sem_inc(summed, XAHEAD)
            for half in range(2):
                last = nc.tensor.matmul(acc[:, half, 0:HALF * XROW], zeros[:, 0:NB], zeros[:, 0:HALF * XROW],
                                        start=True, stop=False, skip_group_check=True)
            with pe.Fori(0, TRIPS) as i:
                for u in range(XSLOTS):
                    k = i * XSLOTS + u
                    pe.wait_ge(widened, k + 1)
                    w = wide[:, u % 2].rearrange("p j b r -> p j (b r)")
                    for j in range(XT):
                        for half in range(2):
                            a = half * HALF * XROW
                            last = nc.tensor.matmul(acc[:, half, 0:HALF * XROW], lo[:, u, j, :],
                                                    w[:, j, a:a + HALF * XROW], start=False, stop=False,
                                                    skip_group_check=True)
                    last.then_inc(summed, 1)
            for half in range(2):
                last = nc.tensor.matmul(acc[:, half, 0:HALF * XROW], zeros[:, 0:NB], zeros[:, 0:HALF * XROW],
                                        start=False, stop=True, skip_group_check=True)
            last.then_inc(summed, 1)


def experts(nc, scope, W1, b1, W2, b2, x_all, ones, xnT, gate, out):
    PAIR = 2
    PN = PAIR * NB
    with ExitStack() as ctx:
        sb, ps, sem = scope(ctx)
        w1 = sb("w1", [P, XE, KC, HID])
        w2 = sb("w2", [P, XE, HC, D])
        b1c = sb("b1c", [P, XE, HC])
        b2r = sb("b2r", [1, XE, D])
        hid = sb("hid", [P, 2, HC, PN])
        psA = ps("psA", [P, 4, 512])
        psY = ps("psY", [NB, 4, 512])
        loaded = sem("loaded_x")
        hid_ready = sem("hid_ready")
        act_done = sem("act_done")
        y_ready = sem("y_ready")
        y_added = sem("y_added")
        stored = sem("stored_x")
        block = ctx.enter_context(nc.Block())
        LOADS = 2 + 2 * XE

        @block.sync
        def _(sp):
            for e in range(XE):
                sp.dma_start(w1[:, e], W1[e].rearrange("(c p) n -> p c n", p=P)).then_inc(loaded, 16)
                sp.dma_start(w2[:, e], W2[e].rearrange("(c p) n -> p c n", p=P)).then_inc(loaded, 16)
            sp.dma_start(b1c[:], b1.rearrange("e (c p) -> p e c", p=P), allow_slow_non_contiguous=True).then_inc(loaded, 16)
            sp.dma_start(b2r[:], b2.rearrange("(a e) n -> a e n", a=1)).then_inc(loaded, 16)
            with sp.Fori(0, BLOCKS // PAIR) as i:
                sp.wait_ge(y_added, (i + 1) * (XE * PAIR))
                sp.dma_start(out.rearrange("(b p) d -> p b d", p=NB)[:, bass.ds(i * PAIR, PAIR), :],
                             x_all[:, bass.ds(i * PAIR, PAIR), :]).then_inc(stored, 16)
            sp.wait_ge(stored, 16 * (BLOCKS // PAIR))

        @block.tensor
        def _(pe):
            pe.wait_ge(loaded, 16 * LOADS)
            with pe.Fori(0, BLOCKS // PAIR) as i:
                for e in range(XE):
                    for c in range(HC):
                        pe.wait_ge(act_done, i * (XE * HC) + e * HC)
                        for kc in range(KC):
                            last = nc.tensor.matmul(psA[:, c, 0:PN], w1[:, e, kc, c * P:(c + 1) * P],
                                                    xnT[:, bass.ds(i * PAIR, PAIR), kc * NB:(kc + 1) * NB], start=kc == 0, stop=kc == KC - 1)
                        last.then_inc(hid_ready, 1)
                    pe.wait_ge(act_done, i * (XE * HC) + (e + 1) * HC)
                    for h in range(PAIR):
                        s = (e * PAIR + h) % 4
                        if e * PAIR + h >= 4:
                            pe.wait_ge(y_added, i * (XE * PAIR) + e * PAIR + h - 3)
                        else:
                            pe.wait_ge(y_added, i * (XE * PAIR))
                        for c in range(HC):
                            nc.tensor.matmul(psY[:, s, 0:D], hid[:, e % 2, c, h * NB:(h + 1) * NB], w2[:, e, c, :],
                                             start=c == 0, stop=False)
                        nc.tensor.matmul(psY[:, s, 0:D], ones[0:1, 0:NB], b2r[:, e, :], start=False, stop=True) \
                            .then_inc(y_ready, 1)

        @block.scalar
        def _(act):
            act.wait_ge(loaded, 16 * LOADS)
            with act.Fori(0, BLOCKS // PAIR) as i:
                for e in range(XE):
                    if e >= 2:
                        act.wait_ge(y_ready, i * (XE * PAIR) + (e - 1) * PAIR)
                    else:
                        act.wait_ge(y_ready, i * (XE * PAIR))
                    for c in range(HC):
                        act.wait_ge(hid_ready, i * (XE * HC) + e * HC + c + 1)
                        nc.scalar.activation(hid[:, e % 2, c, :], psA[:, c, 0:PN], ACT.Gelu, bias=b1c[:, e, c:c + 1]) \
                            .then_inc(act_done, 1)

        @block.vector
        def _(dve):
            with dve.Fori(0, BLOCKS // PAIR) as i:
                for e in range(XE):
                    for h in range(PAIR):
                        s = (e * PAIR + h) % 4
                        dve.wait_ge(y_ready, i * (XE * PAIR) + e * PAIR + h + 1)
                        xb = x_all[:, bass.ds(i * PAIR + h, 1), :].rearrange("p a d -> p (a d)")
                        g = gate[:, bass.ds(i * PAIR + h, 1), e:e + 1].rearrange("p a d -> p (a d)")
                        if e > 0:
                            dve.wait_ge(y_added, i * (XE * PAIR) + (e - 1) * PAIR + h + 1)
                        nc.vector.scalar_tensor_tensor(xb, psY[:, s, 0:D], g, xb, ALU.mult, ALU.add) \
                            .then_inc(y_added, 1)


_INS = ['x', 'src', 'dst', 'L0_gnn_W', 'L0_gnn_att_src', 'L0_gnn_att_dst', 'L0_gnn_bias', 'L0_mix_W_qkv',
        'L0_mix_W_out', 'L0_mix_b_out', 'L0_ffn_W_gat', 'L0_ffn_att_src', 'L0_ffn_att_dst', 'L0_ffn_b_gat',
        'L0_ffn_ln_gamma', 'L0_ffn_ln_beta', 'L0_ffn_W1', 'L0_ffn_b1', 'L0_ffn_W2', 'L0_ffn_b2',
        'L0_ffn_edge_index']


def kernel(**inputs):
    import numpy as _np
    import concourse.bacc as _bacc
    from concourse import mybir as _mybir
    from concourse.bass_utils import run_bass_kernel_spmd as _run

    nc = _bacc.Bacc("TRN2", target_bir_lowering=False, num_devices=1)
    arrays, args = {}, []
    for name in _INS:
        a = _np.ascontiguousarray(inputs[name])
        arrays[f"in_{name}"] = a
        args.append(nc.dram_tensor(f"in_{name}", a.shape, _mybir.dt.from_np(a.dtype), kind="ExternalInput").ap())
    o = nc.dram_tensor("out_0", (N, D), F32, kind="ExternalOutput").ap()
    build(nc, *args, o)
    r = _run(nc, [arrays], core_ids=[0])
    return r.results[0]["out_0"]
```

```python
from contextlib import ExitStack

import concourse.bass as bass
from concourse import mybir

ALU = mybir.AluOpType
ACT = mybir.ActivationFunctionType
F32 = mybir.dt.float32
BF16 = mybir.dt.bfloat16
F32R = mybir.dt.float32r
I32 = mybir.dt.int32
AX_X = mybir.AxisListType.X
RMAX = bass.bass_isa.ReduceOp.max

P = 128
N = 6250
D = 256
NB = 125
BLOCKS = N // NB
KC = D // P
EPS = 1e-5
SLOPE = 0.2

GH, GC = 4, 64
EDGES = 200000
EP = 125
GT = 4
GROUPS = EDGES // (EP * GT)
ROW = D + GH
SLOTS = 6
AHEAD = 3
PAIRS = GROUPS + BLOCKS - 1
STEPS = (PAIRS + SLOTS - 1) // SLOTS * SLOTS
LISTED = STEPS + AHEAD
CH = 100
CHUNKS = GROUPS // CH
FAR = -1.0e7
SPREAD = 70.0

MH, MD = 4, 32
MW = MH * MD

XH, XE = 4, 4
XF = XH * XE
XROW = XF + XH
XEDGES = 131072
XT = 4
XGROUPS = XEDGES // (P * XT)
XSLOTS = 5
XAHEAD = 2
XPARTS = 1
XWHOLE = XT - XPARTS
HID = 2 * D
HC = HID // P


class Chain:

    def __init__(self, eng, sem, base=0):
        self.eng, self.sem, self.base, self.n = eng, sem, base, 0

    def link(self, ins):
        ins.then_inc(self.sem, 1)
        self.n += 1
        self.eng.wait_ge(self.sem, self.base + self.n)


def each_block(eng, step):
    for u in range(2):
        step(u, u, True, False)
    with eng.Fori(1, BLOCKS // 2 - 1) as i:
        for u in range(2):
            step(2 * i + u, u, False, False)
    for u in range(2):
        step(BLOCKS - 2 + u, u, False, True)


def bcast(ap, axis, n):
    shape = list(ap.shape)
    shape.insert(axis, n)
    return ap.unsqueeze(axis).to_broadcast(shape)


def floor_div(nc, ch, x, q, qi, t, d):
    ch.link(nc.vector.tensor_scalar(qi, x, 1.0 / d, None, ALU.mult))
    ch.link(nc.vector.tensor_copy(q, qi))
    ch.link(nc.vector.scalar_tensor_tensor(t, q, float(-d), x, ALU.mult, ALU.add))
    ch.link(nc.vector.tensor_scalar(t, t, 0.0, None, ALU.is_lt))
    ch.link(nc.vector.tensor_tensor(q, q, t, ALU.subtract))
    ch.link(nc.vector.scalar_tensor_tensor(t, q, float(-d), x, ALU.mult, ALU.add))
    ch.link(nc.vector.tensor_scalar(t, t, float(d), None, ALU.is_ge))
    ch.link(nc.vector.tensor_tensor(q, q, t, ALU.add))


def mean_and_variance(nc, ch, stats, mean, var):
    V = nc.vector
    m0, v0, m1, v1 = stats[:, :, 1], stats[:, :, 2], stats[:, :, 4], stats[:, :, 5]
    ch.link(V.tensor_tensor(var, m0, m1, ALU.subtract))
    ch.link(V.tensor_tensor(var, var, var, ALU.mult))
    ch.link(V.tensor_tensor(mean, v0, v1, ALU.add))
    ch.link(V.tensor_scalar(mean, mean, 1.0 / D, None, ALU.mult))
    ch.link(V.scalar_tensor_tensor(var, var, 0.25, mean, ALU.mult, ALU.add))
    ch.link(V.tensor_tensor(mean, m0, m1, ALU.add))
    ch.link(V.tensor_scalar(mean, mean, 0.5, None, ALU.mult))


def build(nc, x, src, dst, W, att_src, att_dst, gbias, W_qkv, W_out, b_out, W_gat, xatt_src, xatt_dst, b_gat,
          gamma, beta, W1, b1, W2, b2, xedges, out):
    table = nc.dram_tensor("table", [N, ROW], F32).ap()
    xtable = nc.dram_tensor("xtable", [N, XROW], F32).ap()
    xtable_dst = nc.dram_tensor("xtable_dst", [N, 2 * XH], F32).ap()

    def row(v):
        return v.rearrange("(a n) -> a n", a=1)

    with ExitStack() as whole:
        def scope(ctx):
            def sb(name, shape, dt=F32):
                return ctx.enter_context(nc.sbuf_tensor(name, shape, dt))

            def ps(name, shape):
                return ctx.enter_context(nc.psum_tensor(name, shape, F32))

            def sem(name):
                return ctx.enter_context(nc.semaphore(name))
            return sb, ps, sem

        sb, _, sem = scope(whole)
        x_all = sb("x_all", [NB, BLOCKS, D])
        ident = sb("ident", [P, P])
        ones = sb("ones", [P, P])
        zeros = sb("zeros", [P, 512])
        node = sb("node", [P, NB])
        as_all = sb("as_all", [NB, BLOCKS, GH])
        ad_m = sb("ad_m", [NB, BLOCKS, 2 * GH])
        ex_self = sb("ex_self", [NB, BLOCKS, GH])
        hg_all = sb("hg_all", [NB, BLOCKS, XROW])
        xad_all = sb("xad_all", [NB, BLOCKS, 2 * XH])
        gate = sb("gate", [NB, BLOCKS, XE])
        room = sb("room", [P, BLOCKS, ROW])
        qk = room[:, :, 0:2 * NB]
        agg = room[0:NB, :, :]
        xnT = room[:, :, 0:KC * NB]

        with ExitStack() as inner:
            isb, _, _ = scope(inner)
            src_i = isb("src_i", [EP, GROUPS, GT], I32)
            dst_i = isb("dst_i", [EP, GROUPS, GT], I32)
            edges_loaded = sem("edges_loaded")
            linear_attention_and_projections(nc, scope, x, W, att_src, att_dst, gbias, W_qkv, W_out, b_out, table,
                                             x_all, ident, ones, zeros, node, as_all, ad_m, qk, row, src, dst,
                                             src_i, dst_i, edges_loaded)
            dst_f = isb("dst_f", [EP, GROUPS, GT])
            neg_base = isb("neg_base", [EP, LISTED])
            step_group = isb("step_group", [EP, LISTED], I32)
            step_block = isb("step_block", [EP, LISTED + 1], I32)
            sweeps = isb("sweeps", [EP, 1], I32)
            schedule(nc, scope, dst, ones, as_all, ad_m, ex_self, agg, src_i, dst_i, dst_f, neg_base, step_group,
                     step_block, sweeps, edges_loaded)
            edges(nc, scope, table, ident, zeros, node, ad_m, agg, src_i, dst_f, neg_base, step_group, step_block,
                  sweeps)
        nodes(nc, scope, table, W_gat, xatt_src, xatt_dst, xtable, xtable_dst, x_all, ident, agg, ex_self,
              xnT, hg_all, xad_all, row)
        y_dram = nc.dram_tensor("experts_out", [XE * (BLOCKS // 2) + 1, NB, 2 * D], F32).ap()
        acc = whole.enter_context(nc.psum_tensor("acc", [NB, 2, 512], F32))
        gating_sums_and_experts(nc, scope, xedges, xtable, xtable_dst, W1, b1, W2, b2, zeros, node, xnT, acc,
                                y_dram, row)
        gates(nc, scope, b_gat, gamma, beta, hg_all, xad_all, acc, gate, row)
        combine(nc, scope, x_all, gate, y_dram, out)


def linear_attention_and_projections(nc, scope, x, W, att_src, att_dst, gbias, W_qkv, W_out, b_out, table,
                                     x_all, ident, ones, zeros, node, as_all, ad_m, qk, row, src, dst,
                                     src_i, dst_i, edges_loaded):
    U = 2
    with ExitStack() as ctx:
        sb, ps, sem = scope(ctx)
        w_sb = sb("w_sb", [P, KC, D])
        qkv_sb = sb("qkv_sb", [P, KC, 3 * MW])
        wout_sb = sb("wout_sb", [MW, D])
        att = sb("att", [NB, 2, D])
        bias = sb("bias", [NB, 2, D])
        stats = sb("stats", [NB, BLOCKS, 6])
        mean = sb("mean", [NB, BLOCKS])
        rstd = sb("rstd", [NB, BLOCKS])
        eps = sb("eps", [NB, 1])
        xn = sb("xn", [NB, U, D])
        xnT = sb("xnT_a", [P, U, KC, NB])
        hrow = sb("hrow", [NB, U, ROW])
        prod = sb("prod", [NB, U, 2, D])
        v_all = sb("v_all", [NB, BLOCKS, MW + 1])
        nmax = sb("nmax", [MW, 1])
        kx = sb("kx", [MW, U, NB])
        kxT = sb("kxT", [NB, U, MW])
        rk = sb("rk", [MW, 1])
        cbd = sb("cbd", [MW, MW])
        cbdT = sb("cbdT", [MW, MW])
        m_sb = sb("m_sb", [MW, D])
        qs = sb("qs", [MW, U, NB])

        psT = ps("psT", [P, U, 512])
        psH = ps("psH", [NB, U, 512])
        psQ = ps("psQ", [P, U, 512])
        psC = ps("psC", [P, 512])

        loaded = sem("loaded")
        consts = sem("consts")
        consts0 = sem("consts0")
        bias_summed = sem("bias_summed")
        biased = sem("biased")
        var_ready = sem("var_ready")
        std_ready = sem("std_ready")
        normed = sem("normed")
        turned = sem("turned")
        turned_sb = sem("turned_sb")
        projected = sem("projected")
        qk_kept = sem("qk_kept")
        h_kept = sem("h_kept")
        v_kept = sem("v_kept")
        logits_kept = sem("logits_kept")
        row_stored = [sem(f"row_stored{u}") for u in range(U)]
        dve_chain = sem("dve_chain_a")
        max_known = sem("max_known")
        k_exp = sem("k_exp")
        k_turned = sem("k_turned")
        k_kept = sem("k_kept")
        context_part = sem("context_part")
        context_masked = sem("context_masked")
        context_turned = sem("context_turned")
        context_kept = sem("context_kept")
        m_ready = sem("m_ready")
        m_kept = sem("m_kept")
        q_staged = sem("q_staged")
        mixed = sem("mixed")
        mix_added = sem("mix_added")
        LOADS = 7
        XCH = 5
        XB = BLOCKS // XCH
        x_loaded = [sem(f"x_loaded{c}") for c in range(XCH)]
        block = ctx.enter_context(nc.Block())

        @block.sync
        def _(sp):
            xv = x.rearrange("(b p) d -> p b d", p=NB)
            for c in range(XCH):
                sp.dma_start(x_all[:, c * XB:(c + 1) * XB, :], xv[:, c * XB:(c + 1) * XB, :]) \
                    .then_inc(x_loaded[c], 16)
            sp.dma_start(w_sb[:], W.rearrange("(c p) n -> p c n", p=P)).then_inc(loaded, 16)
            sp.dma_start(qkv_sb[:], W_qkv.rearrange("(c p) n -> p c n", p=P)).then_inc(loaded, 16)
            sp.dma_start(wout_sb[:], W_out).then_inc(loaded, 16)
            for n, vec in enumerate((att_src, att_dst)):
                flat = row(vec.rearrange("h c -> (h c)"))
                sp.dma_start(att[:, n, :], flat.to_broadcast([NB, D])).then_inc(loaded, 16)
            for n, vec in enumerate((b_out, gbias)):
                sp.dma_start(bias[:, n, :], row(vec).to_broadcast([NB, D])).then_inc(loaded, 16)
            sp.dma_start(src_i[:], src.rearrange("(g p j) -> p g j", p=EP, j=GT)).then_inc(edges_loaded, 16)
            sp.dma_start(dst_i[:], dst.rearrange("(g p j) -> p g j", p=EP, j=GT)).then_inc(edges_loaded, 16)

            def store_row(n, u, first, last):
                sp.wait_ge(h_kept, n + 1)
                sp.wait_ge(logits_kept, n + 1)
                sp.dma_start(table[bass.ds(n * NB, NB), :], hrow[:, u, :]).then_inc(row_stored[u], 16)

            each_block(sp, store_row)
            for u in range(U):
                sp.wait_ge(row_stored[u], 16 * (BLOCKS // U))

        @block.gpsimd
        def _(pool):
            nc.gpsimd.memset(ones[:], 1.0).then_inc(consts0, 1)
            nc.gpsimd.memset(zeros[:], 0.0).then_inc(consts0, 1)
            nc.gpsimd.iota(node[:], [[1, NB]], base=0, channel_multiplier=0,
                           allow_small_or_imprecise_dtypes=True).then_inc(consts, 1)
            pool.wait_ge(consts0, 2)
            nc.gpsimd.affine_select(out=ident[:], in_=ones[:], compare_op=ALU.is_equal, fill=0.0, base=0,
                                    pattern=[[-1, P]], channel_multiplier=1).then_inc(consts, 1)
            nc.gpsimd.memset(v_all[:, :, MW:], 1.0).then_inc(consts, 1)
            nc.gpsimd.memset(cbd[:], 0.0).then_inc(consts, 1)
            pool.wait_ge(loaded, 16 * LOADS)
            nc.gpsimd.tensor_tensor(bias[:, 0, :], bias[:, 0, :], bias[:, 1, :], ALU.add).then_inc(bias_summed, 1)
            pool.wait_ge(bias_summed, 1)
            pool.wait_ge(normed, BLOCKS)
            nc.gpsimd.tensor_tensor(x_all[:], x_all[:], bcast(bias[:, 0, :], 1, BLOCKS), ALU.add).then_inc(biased, 1)

        @block.vector
        def _(dve):
            for c in range(XCH):
                dve.wait_ge(x_loaded[c], 16)
                with dve.Fori(c * XB, (c + 1) * XB) as i:
                    nc.vector.bn_stats(stats[:, bass.ds(i, 1), :].rearrange("p a s -> p (a s)"),
                                       x_all[:, bass.ds(i, 1), :].rearrange("p a d -> p (a d)")) \
                        .then_inc(dve_chain, 1)
            dve.wait_ge(dve_chain, BLOCKS)
            ch = Chain(dve, dve_chain, BLOCKS)
            mean_and_variance(nc, ch, stats, mean[:], rstd[:])
            ch.link(nc.vector.memset(eps[:], EPS))
            nc.vector.tensor_copy(stats[:, :, 0], rstd[:]).then_inc(var_ready, 1)
            dve.wait_ge(std_ready, 1)
            ch.link(nc.vector.reciprocal(rstd[:], rstd[:]))
            dve.wait_ge(loaded, 16 * LOADS)
            dve.wait_ge(consts, 4)
            base = ch.base + ch.n
            PER = 3

            def normalize(n, u):
                nc.vector.tensor_scalar(xn[:, u, :], x_all[:, bass.ds(n, 1), :].rearrange("p a d -> p (a d)"),
                                        mean[:, bass.ds(n, 1)], rstd[:, bass.ds(n, 1)],
                                        ALU.subtract, ALU.mult).then_inc(normed, 1)

            def logits_of(n, u, first, last):
                ch = Chain(dve, dve_chain, base + PER * n)
                if not last:
                    dve.wait_ge(turned, n + 1)
                    normalize(n + 2, u)
                dve.wait_ge(h_kept, n + 1)
                ch.link(nc.vector.tensor_tensor(prod[:, u, :, :], bcast(hrow[:, u, 0:D], 1, 2), att[:], ALU.mult))
                ch.link(nc.vector.reduce_sum(as_all[:, bass.ds(n, 1), :],
                                             prod[:, u, 0, :].rearrange("p (a h c) -> p a h c", a=1, h=GH), AX_X))
                ch.link(nc.vector.reduce_sum(ad_m[:, bass.ds(n, 1), 0:GH],
                                             prod[:, u, 1, :].rearrange("p (a h c) -> p a h c", a=1, h=GH), AX_X))
                assert ch.n == PER
                nc.vector.tensor_scalar(hrow[:, u, D:ROW].rearrange("p (a h) -> p a h", a=1),
                                        as_all[:, bass.ds(n, 1), :], 1.0, None, ALU.mult).then_inc(logits_kept, 1)

            for u in range(U):
                normalize(u, u)
            each_block(dve, logits_of)
            ch = Chain(dve, dve_chain, base + PER * BLOCKS)
            dve.wait_ge(qk_kept, BLOCKS)
            nc.vector.tensor_reduce(nmax[:], qk[:, :, NB:], mybir.AxisListType.XY, ALU.max, negate=True) \
                .then_inc(max_known, 1)

            def keep_k(n, u, first, last):
                dve.wait_ge(k_turned, n + 1)
                if not first:
                    dve.wait_ge(context_part, n)
                nc.vector.tensor_copy(kxT[:, u, :], psT[0:NB, u, 0:MW]).then_inc(k_kept, 1)

            each_block(dve, keep_k)
            dve.wait_ge(context_part, BLOCKS + 1)
            ch.link(nc.vector.reciprocal(rk[:], psC[:, MW:MW + 1]))
            for h in range(MH):
                s = slice(h * MD, (h + 1) * MD)
                nc.vector.tensor_scalar(cbd[s, s], psC[s, s], rk[s, :], float(MD) ** -0.5, ALU.mult, ALU.mult) \
                    .then_inc(context_masked, 1)
            dve.wait_ge(context_turned, 1)
            nc.vector.tensor_copy(cbdT[:], psT[:, 0, 0:MW]).then_inc(context_kept, 1)
            dve.wait_ge(m_ready, 1)
            nc.vector.tensor_copy(m_sb[:], psQ[:, 0, 0:D]).then_inc(m_kept, 1)

            dve.wait_ge(biased, 1)

            def add_mix(n, u, first, last):
                dve.wait_ge(mixed, n + 1)
                xb = x_all[:, bass.ds(n, 1), :]
                nc.vector.tensor_tensor(xb, xb, psH[:, u, 0:D].rearrange("p (a d) -> p a d", a=1), ALU.add) \
                    .then_inc(mix_added, 1)

            each_block(dve, add_mix)

        @block.scalar
        def _(act):
            act.wait_ge(var_ready, 1)
            nc.scalar.activation(rstd[:], stats[:, :, 0], ACT.Sqrt, bias=eps[:]).then_inc(std_ready, 1)

            def keep_turned(n, u):
                act.wait_ge(turned, n + 1)
                nc.scalar.copy(xnT[:, u, :, :], psT[:, u, 0:KC * NB].rearrange("p (c n) -> p c n", c=KC)) \
                    .then_inc(turned_sb, 1)

            def keep_projected(n, u, first, last):
                if not (last and u == U - 1):
                    keep_turned(n + 1, (u + 1) % U)
                act.wait_ge(projected, n + 1)
                nc.scalar.copy(qk[:, bass.ds(n, 1), :], psQ[:, u, 0:2 * NB].rearrange("p (a n) -> p a n", a=1)) \
                    .then_inc(qk_kept, 1)
                if not first:
                    act.wait_ge(row_stored[u], (n - u) * (16 // U))
                nc.scalar.copy(hrow[:, u, 0:D], psH[:, u, 0:D]).then_inc(h_kept, 1)
                nc.scalar.copy(v_all[:, bass.ds(n, 1), 0:MW],
                               psH[:, u, D:D + MW].rearrange("p (a h) -> p a h", a=1)).then_inc(v_kept, 1)

            keep_turned(0, 0)
            each_block(act, keep_projected)
            act.wait_ge(max_known, 1)

            def exp_k(n, u, first, last):
                if not first:
                    act.wait_ge(k_turned, n - 1)
                nc.scalar.activation(kx[:, u, :], qk[:, bass.ds(n, 1), NB:].rearrange("p a n -> p (a n)"), ACT.Exp,
                                     bias=nmax[:]).then_inc(k_exp, 1)

            each_block(act, exp_k)

            def stage_q(n, u, first, last):
                if not first:
                    act.wait_ge(mixed, n - 1)
                nc.scalar.copy(qs[:, u, :], qk[:, bass.ds(n, 1), 0:NB].rearrange("p a n -> p (a n)")) \
                    .then_inc(q_staged, 1)

            each_block(act, stage_q)

        @block.tensor
        def _(pe):
            pe.wait_ge(loaded, 16 * LOADS)
            pe.wait_ge(consts, 4)

            def turn(n, u):
                pe.wait_ge(normed, n + 1)
                for c in range(KC):
                    last = nc.tensor.transpose(psT[:, u, c * NB:(c + 1) * NB], xn[:, u, c * P:(c + 1) * P],
                                               ident[0:NB, 0:NB])
                last.then_inc(turned, 1)

            def project(n, u, first, last):
                if not (last and u == U - 1):
                    turn(n + 1, (u + 1) % U)
                pe.wait_ge(turned_sb, n + 1)
                if not first:
                    pe.wait_ge(v_kept, n - 1)
                for w, a, b in ((w_sb[:], 0, D), (qkv_sb[:, :, 2 * MW:], D, D + MW)):
                    for c in range(KC):
                        nc.tensor.matmul(psH[:, u, a:b], xnT[:, u, c, :], w[:, c, :], start=c == 0,
                                         stop=c == KC - 1)
                for t in range(2):
                    for c in range(KC):
                        mm = nc.tensor.matmul(psQ[:, u, t * NB:(t + 1) * NB], qkv_sb[:, c, t * MW:(t + 1) * MW],
                                              xnT[:, u, c, :], start=c == 0, stop=c == KC - 1)
                mm.then_inc(projected, 1)

            turn(0, 0)
            each_block(pe, project)
            nc.tensor.matmul(psC[:, 0:MW + 1], zeros[:, 0:P], zeros[:, 0:MW + 1], start=True, stop=False,
                             skip_group_check=True).then_inc(context_part, 1)

            def turn_k(n, u):
                pe.wait_ge(k_exp, n + 1)
                nc.tensor.transpose(psT[0:NB, u, 0:MW], kx[:, u, :], ident[:]).then_inc(k_turned, 1)

            def context(n, u, first, last):
                if not (last and u == U - 1):
                    turn_k(n + 1, (u + 1) % U)
                pe.wait_ge(k_kept, n + 1)
                nc.tensor.matmul(psC[:, 0:MW + 1], kxT[:, u, :],
                                 v_all[:, bass.ds(n, 1), :].rearrange("p a d -> p (a d)"), start=False,
                                 stop=False, skip_group_check=True).then_inc(context_part, 1)

            turn_k(0, 0)
            each_block(pe, context)
            pe.wait_ge(context_masked, MH)
            nc.tensor.transpose(psT[:, 0, 0:MW], cbd[:], ident[:]).then_inc(context_turned, 1)
            pe.wait_ge(context_kept, 1)
            nc.tensor.matmul(psQ[:, 0, 0:D], cbdT[:], wout_sb[:], start=True, stop=True).then_inc(m_ready, 1)
            pe.wait_ge(m_kept, 1)

            def mix(n, u, first, last):
                pe.wait_ge(q_staged, n + 1)
                if not first:
                    pe.wait_ge(mix_added, n - 1)
                nc.tensor.matmul(psH[:, u, 0:D], qs[:, u, :], m_sb[:], start=True, stop=True).then_inc(mixed, 1)

            each_block(pe, mix)


def schedule(nc, scope, dst, ones, as_all, ad_m, ex_self, agg, src_i, dst_i, dst_f, neg_base, step_group,
             step_block, sweeps, edges_loaded):
    with ExitStack() as ctx:
        sb, ps, sem = scope(ctx)
        rows = sb("rows", [CH, 2, CHUNKS, EP * GT], I32)
        ext = sb("ext", [CH, 3, CHUNKS])
        extb = sb("extb", [CH, 3, CHUNKS])
        exti = sb("exti", [CH, 3, CHUNKS], I32)
        extt = sb("extt", [CH, 3, CHUNKS])
        gid = sb("gid", [CH, CHUNKS])
        stp = sb("stp", [P, LISTED])
        below = sb("below", [CH, CHUNKS, LISTED])
        broken = sb("broken", [CH, CHUNKS])
        flag = sb("flag", [EP, 1])
        keep = sb("keep", [EP, 1])
        grp = sb("grp", [EP, LISTED])
        alt = sb("alt", [EP, LISTED])
        top = sb("top", [NB, GH])
        topall = sb("topall", [NB, GH])
        s_self = sb("s_self", [NB, BLOCKS, GH])
        s_top = sb("s_top", [NB, BLOCKS, GH])
        psG = ps("psG", [EP, 512])
        psF = ps("psF", [EP, 512])
        loaded = sem("sched_loaded")
        prev0 = sem("prev0")
        iotas = sem("iotas")
        chain = sem("sched_chain")
        marks = sem("marks")
        counted = sem("counted")
        top_known = sem("top_known")
        top_shared = sem("top_shared")
        self_shifted = sem("self_shifted")
        self_weight = sem("self_weight")
        block = ctx.enter_context(nc.Block())
        L = EP * GT

        @block.sync
        def _(sp):
            sp.dma_start(rows[:, 0, :, :], dst.rearrange("(c p e) -> p c e", c=CHUNKS, e=L)).then_inc(loaded, 16)
            sp.wait_ge(prev0, 1)
            sp.dma_start(rows[1:CH, 1, 0, :], dst[0:(CH - 1) * L].rearrange("(p e) -> p e", e=L)).then_inc(loaded, 16)
            for c in range(1, CHUNKS):
                a = (c * CH - 1) * L
                sp.dma_start(rows[:, 1, c, :], dst[a:a + CH * L].rearrange("(p e) -> p e", e=L)).then_inc(loaded, 16)

        @block.gpsimd
        def _(pool):
            nc.gpsimd.memset(rows[0:1, 1, 0, :], 0).then_inc(prev0, 1)
            nc.gpsimd.iota(gid[:], [[CH, CHUNKS]], base=0, channel_multiplier=1,
                           allow_small_or_imprecise_dtypes=True).then_inc(iotas, 1)
            nc.gpsimd.iota(stp[:], [[1, LISTED]], base=0, channel_multiplier=0,
                           allow_small_or_imprecise_dtypes=True).then_inc(iotas, 1)
            nc.gpsimd.memset(agg[:], 0.0).then_inc(iotas, 1)
            pool.wait_ge(top_known, 1)
            nc.gpsimd.partition_all_reduce(topall[:], top[:], NB, RMAX).then_inc(top_shared, 1)

        @block.vector
        def _(dve):
            ch = Chain(dve, chain)
            V = nc.vector
            V.tensor_reduce(top[:], as_all[:].rearrange("p b h -> p h b"), AX_X, ALU.max).then_inc(top_known, 1)
            ch.link(V.tensor_tensor(s_self[:], as_all[:], ad_m[:, :, 0:GH], ALU.add))
            ch.link(V.scalar_tensor_tensor(s_self[:], s_self[:], SLOPE, s_self[:], ALU.mult, ALU.max))
            dve.wait_ge(top_shared, 1)
            ch.link(V.tensor_tensor(s_top[:], ad_m[:, :, 0:GH], bcast(topall[:], 1, BLOCKS), ALU.add))
            ch.link(V.scalar_tensor_tensor(s_top[:], s_top[:], SLOPE, s_top[:], ALU.mult, ALU.max))
            ch.link(V.scalar_tensor_tensor(ad_m[:, :, GH:], s_self[:], SPREAD, s_top[:], ALU.add, ALU.min))
            V.tensor_tensor(s_self[:], s_self[:], ad_m[:, :, GH:], ALU.subtract).then_inc(self_shifted, 1)

            dve.wait_ge(loaded, 16 * (CHUNKS + 1))
            dve.wait_ge(edges_loaded, 32)
            dve.wait_ge(iotas, 3)
            ch.link(V.tensor_scalar(src_i[:], src_i[:], N - 1, None, ALU.min))
            ch.link(V.tensor_copy(dst_f[:], dst_i[:]))
            ch.link(V.tensor_reduce(ext[:, 0, :], rows[:, 0, :, :], AX_X, ALU.max))
            ch.link(V.tensor_reduce(ext[:, 1, :], rows[:, 0, :, :], AX_X, ALU.min))
            ch.link(V.tensor_reduce(ext[:, 2, :], rows[:, 1, :, :], AX_X, ALU.max))
            ch.link(V.tensor_scalar(ext[:], ext[:], float(N - 1), None, ALU.min))
            floor_div(nc, ch, ext[:], extb[:], exti[:], extt[:], NB)
            ch.link(V.tensor_tensor(broken[:], extb[:, 2, :], extb[:, 1, :], ALU.is_gt))
            ch.link(V.tensor_tensor(gid[:], gid[:], extb[:, 0, :], ALU.add))
            for c in range(CHUNKS):
                V.tensor_scalar(below[:, c, :], stp[0:CH, :], gid[:, c:c + 1], None, ALU.is_gt).then_inc(marks, 1)
            dve.wait_ge(counted, 1)
            ch.link(V.tensor_reduce(flag[:], psF[:, 0:CHUNKS], AX_X, ALU.max))
            ch.link(V.tensor_scalar(flag[:], flag[:], 0.5, None, ALU.is_gt))
            ch.link(V.tensor_scalar(keep[:], flag[:], -1.0, 1.0, ALU.mult, ALU.add))
            ch.link(V.tensor_scalar(sweeps[:], flag[:], float(BLOCKS - 1), 1.0, ALU.mult, ALU.add))
            ch.link(V.tensor_scalar(grp[:], psG[:, 0:LISTED], float(GROUPS - 1), None, ALU.min))
            ch.link(V.tensor_tensor(alt[:], stp[0:EP, :], grp[:], ALU.subtract))
            ch.link(V.tensor_scalar(alt[:], alt[:], float(BLOCKS - 1), keep[:], ALU.min, ALU.mult))
            ch.link(V.tensor_copy(step_block[:, 1:], alt[:]))
            ch.link(V.tensor_copy(step_block[:, 0:1], alt[:, 0:1]))
            ch.link(V.tensor_scalar(neg_base[:], alt[:], float(-NB), None, ALU.mult))
            ch.link(V.tensor_scalar(alt[:], stp[0:EP, :], GROUPS - 0.5, flag[:], ALU.is_gt, ALU.mult))
            ch.link(V.scalar_tensor_tensor(neg_base[:], alt[:], FAR, neg_base[:], ALU.mult, ALU.add))
            ch.link(V.memset(neg_base[:, PAIRS:], FAR))
            ch.link(V.tensor_scalar(grp[:], grp[:], keep[:], None, ALU.mult))
            ch.link(V.tensor_scalar(alt[:], stp[0:EP, :], float(GROUPS - 1), flag[:], ALU.min, ALU.mult))
            ch.link(V.tensor_tensor(grp[:], grp[:], alt[:], ALU.add))
            ch.link(V.tensor_copy(step_group[:], grp[:]))

        @block.scalar
        def _(act):
            act.wait_ge(self_shifted, 1)
            nc.scalar.activation(ex_self[:], s_self[:], ACT.Exp).then_inc(self_weight, 1)

        @block.tensor
        def _(pe):
            pe.wait_ge(marks, CHUNKS)
            for c in range(CHUNKS):
                k = CH - (c == CHUNKS - 1)
                nc.tensor.matmul(psG[:, 0:LISTED], ones[0:k, 0:EP], below[0:k, c, :], start=c == 0,
                                 stop=c == CHUNKS - 1)
            nc.tensor.matmul(psF[:, 0:CHUNKS], ones[0:CH, 0:EP], broken[:], start=True, stop=True).then_inc(counted, 1)


def edges(nc, scope, table, ident, zeros, node, ad_m, agg, src_i, dst_f, neg_base, step_group, step_block, sweeps):
    with ExitStack() as ctx:
        sb, ps, sem = scope(ctx)
        idx = sb("idx", [EP, SLOTS, GT], I32)
        rel = sb("rel", [EP, SLOTS, GT])
        msg = sb("msg", [EP, SLOTS, GT, ROW])
        hot = sb("hot", [EP, SLOTS, GT, NB])
        hotT = sb("hotT", [NB, 2, GT, EP])
        lg = sb("lg", [EP, SLOTS, GT, GH])
        psT = ps("psT_e", [NB, 2, 512])
        psD = ps("psD_e", [EP, 2, 512])
        psS = ps("psS_e", [NB, 2, 512])
        staged = sem("staged")
        opened = sem("opened")
        gathered = [[sem(f"gathered{u}_{j}") for j in range(GT)] for u in range(SLOTS)]
        assert BLOCKS * (STEPS // SLOTS) * 16 < 65536
        hot_ready = sem("hot_ready")
        hot_turned = sem("hot_turned")
        hotT_ready = sem("hotT_ready")
        dst_picked = sem("dst_picked")
        logits = sem("logits")
        weights = sem("weights")
        weighed = sem("weighed")
        summed = sem("summed")
        added = sem("added")
        chain = sem("edge_chain")
        moved = sem("moved")
        block = ctx.enter_context(nc.Block())
        TRIPS = STEPS // SLOTS
        assert TRIPS * SLOTS == STEPS

        def count(eng):
            return eng.value_load(sweeps[0:1, 0:1], min_val=1, max_val=BLOCKS)

        @block.gpsimd
        def _(pool):
            n_sweeps = count(pool)
            with pool.Fori(0, n_sweeps) as s:
                with pool.Fori(0, TRIPS) as i:
                    for u in range(SLOTS):
                        pool.wait_ge(staged, s * LISTED + i * SLOTS + (u + 1))
                        pool.sem_inc(opened, 1)
                        for j in range(GT):
                            nc.gpsimd.indirect_dma_start(
                                msg[:, u, j, :], None, table[:, :],
                                bass.IndirectOffsetOnAxis(ap=idx[:, u, j:j + 1], axis=0)).then_inc(gathered[u][j], 16)

        @block.scalar
        def _(act):
            n_sweeps = count(act)

            def stage(at, u, free, done):
                g = act.value_load(step_group[0:1, bass.ds(at, 1)], min_val=0, max_val=GROUPS - 1)
                act.wait_ge(free, done)
                nc.scalar.copy(idx[:, u, :], src_i[:, bass.ds(g, 1), :].rearrange("p a j -> p (a j)"))
                nc.scalar.activation(rel[:, u, :], dst_f[:, bass.ds(g, 1), :].rearrange("p a j -> p (a j)"),
                                     ACT.Identity, bias=neg_base[:, bass.ds(at, 1)]).then_inc(staged, 1)

            def keep_turned(u, done):
                act.wait_ge(hot_turned, done)
                nc.scalar.copy(hotT[:, u % 2, :, :], psT[:, u % 2, 0:GT * EP].rearrange("p (j e) -> p j e", j=GT)) \
                    .then_inc(hotT_ready, 1)

            with act.Fori(0, n_sweeps) as s:
                for a in range(AHEAD):
                    stage(a, a, moved, 2 * s + 1)
                keep_turned(0, s * (STEPS + 2) + 1)
                with act.Fori(0, TRIPS) as i:
                    for u in range(SLOTS):
                        act.wait_ge(logits, s * STEPS + i * SLOTS + (u + 1))
                        nc.scalar.activation(msg[:, u, :, D:ROW], lg[:, u, :, :], ACT.Exp).then_inc(weights, 1)
                        keep_turned(u + 1, s * (STEPS + 2) + i * SLOTS + (u + 2))
                        stage(i * SLOTS + (u + AHEAD), (u + AHEAD) % SLOTS, summed,
                              s * (STEPS + 1) + i * SLOTS + (u + 2))

        @block.vector
        def _(dve):
            dve.sem_inc(moved, 1)
            n_sweeps = count(dve)
            PER = 3

            def one_hot(u, done):
                dve.wait_ge(staged, done)
                nc.vector.tensor_tensor(hot[:, u, :, :], bcast(node[0:EP, :], 1, GT), bcast(rel[:, u, :], 2, NB),
                                        ALU.is_equal).then_inc(hot_ready, 1)

            def add(at, bank, s):
                b = dve.value_load(step_block[0:1, bass.ds(at, 1)], min_val=0, max_val=BLOCKS - 1)
                to = agg[:, bass.ds(b, 1), :]
                dve.wait_ge(summed, s * (STEPS + 1) + at + (1 + AHEAD))
                dve.wait_ge(added, s * (STEPS + 1) + at + 1)
                nc.vector.tensor_tensor(to, to, psS[:, bank, 0:ROW].rearrange("p (a r) -> p a r", a=1),
                                        ALU.add).then_inc(added, 1)

            with dve.Fori(0, n_sweeps) as s:
                one_hot(0, s * LISTED + 1)
                one_hot(1, s * LISTED + 2)
                with dve.Fori(0, TRIPS) as i:
                    for u in range(SLOTS):
                        k = s * STEPS + i * SLOTS + u
                        ch = Chain(dve, chain, PER * k)
                        for j in range(GT):
                            dve.wait_ge(gathered[u][j], (s * TRIPS + i + 1) * 16)
                        dve.wait_ge(dst_picked, s * (STEPS + 1) + i * SLOTS + (u + 1))
                        pick = psD[:, u % 2, 0:GT * 2 * GH].rearrange("p (j f) -> p j f", j=GT)
                        ch.link(nc.vector.tensor_tensor(lg[:, u, :, :], msg[:, u, :, D:ROW], pick[:, :, 0:GH], ALU.add))
                        ch.link(nc.vector.scalar_tensor_tensor(lg[:, u, :, :], lg[:, u, :, :], SLOPE, lg[:, u, :, :],
                                                               ALU.mult, ALU.max))
                        ch.link(nc.vector.tensor_tensor(lg[:, u, :, :], lg[:, u, :, :], pick[:, :, GH:], ALU.subtract))
                        nc.vector.tensor_scalar(lg[:, u, :, :], lg[:, u, :, :], 80.0, None, ALU.min).then_inc(logits, 1)
                        assert ch.n == PER
                        one_hot((u + 2) % SLOTS, s * LISTED + i * SLOTS + (u + 3))
                        add(i * SLOTS + u, (u + 1) % 2, s)
                        dve.wait_ge(weights, k + 1)
                        m = msg[:, u, :, 0:D].rearrange("p j (h c) -> p j h c", h=GH)
                        nc.vector.tensor_tensor(m, m, bcast(msg[:, u, :, D:ROW], 3, GC), ALU.mult).then_inc(weighed, 1)
                add(STEPS, (STEPS + 1) % 2, s)
                dve.wait_ge(staged, (s + 1) * LISTED)
                dve.wait_ge(dst_picked, (s + 1) * (STEPS + 1))
                dve.wait_ge(hot_turned, (s + 1) * (STEPS + 2))
                dve.wait_ge(added, (s + 1) * (STEPS + 1) + 1)
                nc.vector.tensor_scalar(neg_base[:], neg_base[:], float(-NB), None, ALU.add).then_inc(moved, 1)
                nc.vector.tensor_scalar(step_block[:], step_block[:], 1, None, ALU.add).then_inc(moved, 1)
                dve.wait_ge(moved, 2 * s + 3)

        @block.tensor
        def _(pe):
            pe.sem_inc(summed, AHEAD)
            pe.sem_inc(added, 1)
            n_sweeps = count(pe)

            def turn(u, done):
                pe.wait_ge(hot_ready, done)
                for j in range(GT):
                    last = nc.tensor.transpose(psT[:, u % 2, j * EP:(j + 1) * EP], hot[:, u, j, :],
                                               ident[0:EP, 0:EP])
                last.then_inc(hot_turned, 1)

            def pick(at, u, done):
                b = pe.value_load(step_block[0:1, bass.ds(at + 1, 1)], min_val=0, max_val=BLOCKS - 1)
                pe.wait_ge(hotT_ready, done)
                for j in range(GT):
                    last = nc.tensor.matmul(psD[:, u % 2, j * 2 * GH:(j + 1) * 2 * GH], hotT[:, u % 2, j, :],
                                            ad_m[:, bass.ds(b, 1), :].rearrange("p a f -> p (a f)"),
                                            start=True, stop=True)
                last.then_inc(dst_picked, 1)

            with pe.Fori(0, n_sweeps) as s:
                turn(0, s * (STEPS + 2) + 1)
                turn(1, s * (STEPS + 2) + 2)
                pick(0, 0, s * (STEPS + 1) + 1)
                pe.wait_ge(added, s * (STEPS + 1) + 1)
                nc.tensor.matmul(psS[:, 1, 0:ROW], zeros[:, 0:NB], zeros[:, 0:ROW], start=True, stop=True) \
                    .then_inc(summed, 1)
                with pe.Fori(0, TRIPS) as i:
                    for u in range(SLOTS):
                        k = i * SLOTS + u
                        pick(k + 1, u + 1, s * (STEPS + 1) + k + 2)
                        pe.wait_ge(weighed, s * STEPS + k + 1)
                        pe.wait_ge(added, s * (STEPS + 1) + k + 1)
                        for j in range(GT):
                            last = nc.tensor.matmul(psS[:, u % 2, 0:ROW], hot[:, u, j, :], msg[:, u, j, :],
                                                    start=j == 0, stop=j == GT - 1)
                        last.then_inc(summed, 1)
                        turn((u + 2) % SLOTS, s * (STEPS + 2) + k + 3)


def nodes(nc, scope, table, W_gat, xatt_src, xatt_dst, xtable, xtable_dst, x_all, ident, agg, ex_self, xnT_all,
          hg_all, xad_all, row):
    U = 2
    with ExitStack() as ctx:
        sb, ps, sem = scope(ctx)
        wg = sb("wg", [P, KC, XF])
        atS = sb("atS", [NB, XF])
        atD = sb("atD", [NB, XF])
        hs = sb("hs", [NB, U, D])
        den = sb("den", [NB, U, GH])
        num = sb("num", [NB, U, D])
        stats = sb("stats_n", [NB, BLOCKS, 6])
        mean = sb("mean_n", [NB, BLOCKS])
        rstd = sb("rstd_n", [NB, BLOCKS])
        eps = sb("eps_n", [NB, 1])
        xn = sb("xn_n", [NB, U, D])
        xT = sb("xT_n", [P, U, KC, NB])
        prod = sb("prod_n", [NB, BLOCKS, XF])
        top = sb("top_n", [NB, XH])
        topall = sb("topall_n", [NB, XH])
        s_self = sb("s_self_n", [NB, BLOCKS, XH])
        s_top = sb("s_top_n", [NB, BLOCKS, XH])
        psT = ps("psT_n", [P, U, 512])
        psG = ps("psG_n", [NB, U, 512])
        loaded = sem("loaded_n")
        h_back = [sem(f"h_back{u}") for u in range(U)]
        self_message = sem("self_message")
        messages_summed = sem("messages_summed")
        chain = sem("chain_n")
        measured = sem("measured_n")
        var_ready = sem("var_ready_n")
        std_ready = sem("std_ready_n")
        normed = sem("normed_n")
        turned = sem("turned_n")
        kept = sem("kept_n")
        projected = sem("projected_n")
        proj_kept = sem("proj_kept_n")
        top_known = sem("top_known_n")
        top_shared = sem("top_shared_n")
        tables = sem("tables_n")
        stored = sem("stored_n")
        block = ctx.enter_context(nc.Block())

        @block.sync
        def _(sp):
            sp.dma_start(wg[:], W_gat.rearrange("(c p) n -> p c n", p=P)).then_inc(loaded, 16)
            for tile, vec in ((atS, xatt_src), (atD, xatt_dst)):
                sp.dma_start(tile[:], row(vec.rearrange("h c -> (h c)")).to_broadcast([NB, XF])).then_inc(loaded, 16)

            def load_h(n, u, first, last):
                if not first:
                    sp.wait_ge(messages_summed, n - 1)
                sp.dma_start(hs[:, u, :], table[bass.ds(n * NB, NB), 0:D]).then_inc(h_back[u], 16)

            each_block(sp, load_h)
            sp.wait_ge(tables, 1)
            sp.dma_start(xtable.rearrange("(b p) f -> p b f", p=NB), hg_all[:]).then_inc(stored, 16)
            sp.dma_start(xtable_dst.rearrange("(b p) f -> p b f", p=NB), xad_all[:]).then_inc(stored, 16)
            sp.wait_ge(stored, 32)

        @block.vector
        def _(dve):
            V = nc.vector
            PER = 5
            dve.wait_ge(loaded, 48)

            def update(n, u, first, last):
                ch = Chain(dve, chain, PER * n)
                xb = x_all[:, bass.ds(n, 1), :].rearrange("p a d -> p (a d)")
                ex = ex_self[:, bass.ds(n, 1), :].rearrange("p a h -> p (a h)")
                ag = agg[:, bass.ds(n, 1), :].rearrange("p a r -> p (a r)")
                numu = num[:, u, :].rearrange("p (h c) -> p h c", h=GH)
                ch.link(V.tensor_tensor(den[:, u, :], ag[:, D:ROW], ex, ALU.add))
                ch.link(V.scalar_tensor_tensor(den[:, u, :], ex, 1e-16, den[:, u, :], ALU.mult, ALU.add))
                ch.link(V.reciprocal(den[:, u, :], den[:, u, :]))
                dve.wait_ge(messages_summed, n + 1)
                ch.link(V.tensor_tensor(numu, numu, bcast(den[:, u, :], 2, GC), ALU.mult))
                ch.link(V.tensor_tensor(xb, xb, num[:, u, :], ALU.add))
                assert ch.n == PER
                V.bn_stats(stats[:, bass.ds(n, 1), :].rearrange("p a s -> p (a s)"), xb).then_inc(measured, 1)

            each_block(dve, update)
            ch = Chain(dve, chain, PER * BLOCKS)
            dve.wait_ge(measured, BLOCKS)
            mean_and_variance(nc, ch, stats, mean[:], rstd[:])
            ch.link(V.memset(eps[:], EPS))
            V.tensor_copy(stats[:, :, 0], rstd[:]).then_inc(var_ready, 1)
            dve.wait_ge(std_ready, 1)
            ch.link(V.reciprocal(rstd[:], rstd[:]))

            def normalize(n, u, first, last):
                if not first:
                    dve.wait_ge(turned, n - 1)
                V.tensor_scalar(xn[:, u, :], x_all[:, bass.ds(n, 1), :].rearrange("p a d -> p (a d)"),
                                mean[:, bass.ds(n, 1)], rstd[:, bass.ds(n, 1)], ALU.subtract, ALU.mult) \
                    .then_inc(normed, 1)

            each_block(dve, normalize)
            dve.wait_ge(proj_kept, BLOCKS)
            h4 = hg_all[:, :, 0:XF]
            ch.link(V.tensor_tensor(prod[:], h4, bcast(atS[:], 1, BLOCKS), ALU.mult))
            ch.link(V.reduce_sum(hg_all[:, :, XF:], prod[:].rearrange("p b (h e) -> p b h e", h=XH), AX_X))
            ch.link(V.tensor_tensor(prod[:], h4, bcast(atD[:], 1, BLOCKS), ALU.mult))
            ch.link(V.reduce_sum(xad_all[:, :, 0:XH], prod[:].rearrange("p b (h e) -> p b h e", h=XH), AX_X))
            V.tensor_reduce(top[:], hg_all[:, :, XF:].rearrange("p b h -> p h b"), AX_X, ALU.max).then_inc(top_known, 1)
            ch.link(V.tensor_tensor(s_self[:], hg_all[:, :, XF:], xad_all[:, :, 0:XH], ALU.add))
            ch.link(V.scalar_tensor_tensor(s_self[:], s_self[:], SLOPE, s_self[:], ALU.mult, ALU.max))
            dve.wait_ge(top_shared, 1)
            ch.link(V.tensor_tensor(s_top[:], xad_all[:, :, 0:XH], bcast(topall[:], 1, BLOCKS), ALU.add))
            ch.link(V.scalar_tensor_tensor(s_top[:], s_top[:], SLOPE, s_top[:], ALU.mult, ALU.max))
            V.scalar_tensor_tensor(xad_all[:, :, XH:], s_self[:], SPREAD, s_top[:], ALU.add, ALU.min) \
                .then_inc(tables, 1)

        @block.gpsimd
        def _(pool):
            def sum_messages(n, u, first, last):
                ex = ex_self[:, bass.ds(n, 1), :].rearrange("p a h -> p (a h)")
                ag = agg[:, bass.ds(n, 1), 0:D].rearrange("p a r -> p (a r)")
                if not first:
                    pool.wait_ge(measured, n - 1)
                pool.wait_ge(h_back[u], (n - u) * (16 // U) + 16)
                nc.gpsimd.tensor_tensor(hs[:, u, :].rearrange("p (h c) -> p h c", h=GH),
                                        hs[:, u, :].rearrange("p (h c) -> p h c", h=GH), bcast(ex, 2, GC),
                                        ALU.mult).then_inc(self_message, 1)
                pool.wait_ge(self_message, n + 1)
                nc.gpsimd.tensor_tensor(num[:, u, :], hs[:, u, :], ag, ALU.add).then_inc(messages_summed, 1)

            each_block(pool, sum_messages)
            pool.wait_ge(top_known, 1)
            nc.gpsimd.partition_all_reduce(topall[:], top[:], NB, RMAX).then_inc(top_shared, 1)

        @block.scalar
        def _(act):
            act.wait_ge(var_ready, 1)
            nc.scalar.activation(rstd[:], stats[:, :, 0], ACT.Sqrt, bias=eps[:]).then_inc(std_ready, 1)

            def keep_turned(n, u):
                act.wait_ge(turned, n + 1)
                nc.scalar.copy(xnT_all[:, bass.ds(n, 1), :],
                               psT[:, u, 0:KC * NB].rearrange("p (a n) -> p a n", a=1))
                nc.scalar.copy(xT[:, u, :, :], psT[:, u, 0:KC * NB].rearrange("p (c n) -> p c n", c=KC)) \
                    .then_inc(kept, 1)

            def keep_projected(n, u, first, last):
                if not (last and u == U - 1):
                    keep_turned(n + 1, (u + 1) % U)
                act.wait_ge(projected, n + 1)
                nc.scalar.copy(hg_all[:, bass.ds(n, 1), 0:XF],
                               psG[:, u, 0:XF].rearrange("p (a f) -> p a f", a=1)).then_inc(proj_kept, 1)

            keep_turned(0, 0)
            each_block(act, keep_projected)

        @block.tensor
        def _(pe):
            pe.wait_ge(loaded, 48)

            def turn(n, u):
                pe.wait_ge(normed, n + 1)
                for c in range(KC):
                    last = nc.tensor.transpose(psT[:, u, c * NB:(c + 1) * NB], xn[:, u, c * P:(c + 1) * P],
                                               ident[0:NB, 0:NB])
                last.then_inc(turned, 1)

            def project(n, u, first, last):
                if not (last and u == U - 1):
                    turn(n + 1, (u + 1) % U)
                pe.wait_ge(kept, n + 1)
                if not first:
                    pe.wait_ge(proj_kept, n - 1)
                for c in range(KC):
                    mm = nc.tensor.matmul(psG[:, u, 0:XF], xT[:, u, c, :], wg[:, c, :], start=c == 0,
                                          stop=c == KC - 1)
                mm.then_inc(projected, 1)

            turn(0, 0)
            each_block(pe, project)


def gating_sums_and_experts(nc, scope, xedges, xtable, xtable_dst, W1, b1, W2, b2, zeros, node, xnT, acc, y_dram, row):
    HALF = BLOCKS // 2
    PAIR = 2
    PN = PAIR * NB
    SPAN = 10
    TRIPS = BLOCKS // PAIR
    TAIL = range(TRIPS * SPAN, XGROUPS)
    assert SPAN % XSLOTS == 0 and 0 < len(TAIL) <= SPAN
    with ExitStack() as ctx:
        sb, ps, sem = scope(ctx)
        src_i = sb("xsrc_i", [P, XGROUPS, XT], I32)
        dst_i = sb("xdst_i", [P, XGROUPS, XT], I32)
        blk = sb("blk", [P, XGROUPS, XT])
        loc = sb("loc", [P, XGROUPS, XT])
        idx = sb("xidx", [P, XSLOTS, 2, XT], I32)
        pos = sb("pos", [P, XSLOTS, 2, XT])
        msg = sb("xmsg", [P, XSLOTS, XT, XROW])
        adm = sb("xadm", [P, XSLOTS, XT, 2 * XH])
        lg = sb("xlg", [P, XSLOTS, XT, XH])
        lo = sb("lo", [P, 2, XWHOLE, NB])
        lo_r = sb("lo_r", [P, 2, XPARTS, NB], F32R)
        hi = sb("hi", [P, 2, XT, BLOCKS])
        wide = sb("wide", [P, XWHOLE, BLOCKS, XROW])
        part = sb("part", [P, 2, XPARTS, XROW], F32R)
        wide_r = sb("wide_r", [P, XPARTS, 2, BLOCKS, XROW], F32R)
        b2f = wide[0:1].rearrange("p j b r -> p (j b r)")[:, 0:2 * XE * D].rearrange("p (s n) -> p s n", s=2)
        bid = sb("bid", [P, BLOCKS])
        w1 = sb("w1", [P, XE, KC, HID])
        w2 = sb("w2", [P, XE, HC, D])
        b1c = sb("b1c", [P, XE, HC])
        b2k = sb("b2k", [3, XE * D], BF16)
        ones3 = sb("ones3", [3, NB], BF16)
        hid = sb("hid", [P, 2, HC, PN])
        b2p = hid[0:1].rearrange("p s c n -> p (s c n)").bitcast(BF16)[:, 0:3 * XE * D] \
            .rearrange("p (s n) -> p s n", s=3)
        y_room = sb("y_room", [P, 2, PAIR, D])
        y_sb = y_room[0:NB]
        tmp = y_room[:].rearrange("p s h d -> p (s h d)")[:, 0:XGROUPS * XT].rearrange("p (g j) -> p g j", j=XT)
        psA = ps("psA", [P, HC, 256])
        psY = ps("psY", [NB, PAIR, D])
        loaded = sem("loaded_g")
        iotas = sem("iotas_g")
        chain = sem("chain_g")
        prepared = sem("prepared")
        staged = sem("staged_g")
        opened = sem("opened_g")
        gathered = [sem(f"gathered_g{u}") for u in range(XSLOTS)]
        logits = sem("logits_g")
        weights = sem("weights_g")
        widened = sem("widened")
        summed = sem("summed_g")
        weights_loaded = sem("weights_loaded")
        hid_ready = sem("hid_ready")
        act_done = sem("act_done")
        y_ready = sem("y_ready")
        y_kept = sem("y_kept")
        y_stored = sem("y_stored")
        y_free = sem("y_free")
        b2_loaded = sem("b2_loaded")
        b2_split = sem("b2_split")
        b2_spread = sem("b2_spread")
        ones3_set = sem("ones3_set")
        block = ctx.enter_context(nc.Block())
        LOADS = 1 + 2 * XE

        @block.sync
        def _(sp):
            v = xedges.rearrange("s (g p j) -> s p g j", p=P, j=XT)
            sp.dma_start(src_i[:], v[0]).then_inc(loaded, 16)
            sp.dma_start(dst_i[:], v[1]).then_inc(loaded, 16)
            sp.dma_start(b2f[:, 0, :], row(b2.rearrange("e n -> (e n)"))).then_inc(b2_loaded, 16)
            for e in range(XE):
                sp.dma_start(w1[:, e], W1[e].rearrange("(c p) n -> p c n", p=P)).then_inc(weights_loaded, 16)
                sp.dma_start(w2[:, e], W2[e].rearrange("(c p) n -> p c n", p=P)).then_inc(weights_loaded, 16)
            sp.dma_start(b1c[:], b1.rearrange("e (c p) -> p e c", p=P), allow_slow_non_contiguous=True) \
                .then_inc(weights_loaded, 16)
            sp.wait_ge(b2_split, 5)
            for n in range(3):
                sp.dma_start(b2k[n:n + 1, :], b2p[:, n, :]).then_inc(b2_spread, 16)

            def store(q, u):
                sp.wait_ge(y_kept, q + 1)
                sp.dma_start(y_dram[bass.ds(q, 1)].rearrange("a p f -> p (a f)"),
                             y_sb[:, u].rearrange("p h d -> p (h d)")).then_inc(y_stored, 16)
                sp.wait_ge(y_stored, q * 16 + 16)
                sp.sem_inc(y_free, 1)

            with sp.Fori(0, XE * TRIPS // 2) as i:
                for u in range(2):
                    store(2 * i + u, u)
            store(XE * TRIPS, 0)

        @block.gpsimd
        def _(pool):
            nc.gpsimd.iota(bid[:], [[1, BLOCKS]], base=0, channel_multiplier=0,
                           allow_small_or_imprecise_dtypes=True).then_inc(iotas, 1)

            def gather(k, u):
                pool.wait_ge(staged, k + 1)
                pool.sem_inc(opened, 1)
                for j in range(XT):
                    nc.gpsimd.indirect_dma_start(
                        msg[:, u, j, :], None, xtable[:, :],
                        bass.IndirectOffsetOnAxis(ap=idx[:, u, 0, j:j + 1], axis=0)).then_inc(gathered[u], 16)
                    nc.gpsimd.indirect_dma_start(
                        adm[:, u, j, :], None, xtable_dst[:, :],
                        bass.IndirectOffsetOnAxis(ap=idx[:, u, 1, j:j + 1], axis=0)).then_inc(gathered[u], 16)

            with pool.Fori(0, TRIPS) as i:
                for w in range(SPAN):
                    gather(i * SPAN + w, w % XSLOTS)
            for k in TAIL:
                gather(k, k % XSLOTS)

        @block.scalar
        def _(act):
            act.sem_inc(act_done, HC)
            act.sem_inc(y_free, 2)
            act.wait_ge(prepared, 1)
            act.wait_ge(weights_loaded, 16 * LOADS)

            def stage(at, u):
                for s, (ints, where) in enumerate(((src_i, blk), (dst_i, loc))):
                    nc.scalar.copy(idx[:, u, s, :], ints[:, bass.ds(at, 1), :].rearrange("p a j -> p (a j)"))
                    last = nc.scalar.copy(pos[:, u, s, :], where[:, bass.ds(at, 1), :].rearrange("p a j -> p (a j)"))
                last.then_inc(staged, 1)

            def step(k, u, more):
                act.wait_ge(logits, k + 1)
                nc.scalar.activation(msg[:, u, :, XF:], lg[:, u, :, :], ACT.Exp).then_inc(weights, 1)
                if more:
                    stage(k + XAHEAD, (u + XAHEAD) % XSLOTS)

            def gelu(m, e):
                for c in range(HC):
                    act.wait_ge(hid_ready, m * HC + (c // 2 * 2 + 2))
                    nc.scalar.activation(hid[:, e % 2, c, :], psA[:, c, 0:PN], ACT.Gelu, bias=b1c[:, e, c:c + 1]) \
                        .then_inc(act_done, 1)

            def keep_y(q, u):
                act.wait_ge(y_ready, q + 1)
                act.wait_ge(y_free, q + 1)
                nc.scalar.copy(y_sb[:, u], psY[:]).then_inc(y_kept, 1)

            for a in range(XAHEAD):
                stage(a, a)
            with act.Fori(0, TRIPS) as i:
                for w in range(SPAN):
                    step(i * SPAN + w, w % XSLOTS, True)
                    if w % 2 == 1 and w < 2 * XE:
                        gelu(i * XE + w // 2, w // 2)
                    if w == 1:
                        keep_y(i * XE, 0)
                    if w % 2 == 0 and w >= 4:
                        keep_y(i * XE + (w - 2) // 2, (w - 2) // 2 % 2)
            for k in TAIL:
                step(k, k % XSLOTS, k + XAHEAD < XGROUPS)
                if k == TAIL[0]:
                    keep_y(XE * TRIPS, 0)

        @block.vector
        def _(dve):
            V = nc.vector
            V.memset(ones3[:], 1.0).then_inc(ones3_set, 1)
            dve.wait_ge(b2_loaded, 16)
            ch = Chain(dve, b2_split)
            ch.link(V.tensor_copy(b2p[:, 0, :], b2f[:, 0, :]))
            ch.link(V.tensor_tensor(b2f[:, 1, :], b2f[:, 0, :], b2p[:, 0, :], ALU.subtract))
            ch.link(V.tensor_copy(b2p[:, 1, :], b2f[:, 1, :]))
            ch.link(V.tensor_tensor(b2f[:, 0, :], b2f[:, 1, :], b2p[:, 1, :], ALU.subtract))
            ch.link(V.tensor_copy(b2p[:, 2, :], b2f[:, 0, :]))
            ch = Chain(dve, chain)
            dve.wait_ge(loaded, 16 * 2)
            ch.link(V.tensor_copy(loc[:], dst_i[:]))
            floor_div(nc, ch, loc[:], blk[:], dst_i[:], tmp, NB)
            ch.link(V.tensor_scalar(dst_i[:], loc[:], float(N - 1), None, ALU.min))
            ch.link(V.scalar_tensor_tensor(loc[:], blk[:], float(-NB), loc[:], ALU.mult, ALU.add))
            dve.wait_ge(iotas, 1)
            V.tensor_scalar(src_i[:], src_i[:], N - 1, None, ALU.min).then_inc(prepared, 1)
            base = ch.n
            PER = 6

            def step(k, u, half, visit):
                ch = Chain(dve, chain, base + PER * k)
                dve.wait_ge(gathered[u], visit * (16 * 2 * XT))
                l = lg[:, u, :, :]
                ch.link(V.tensor_tensor(l, msg[:, u, :, XF:], adm[:, u, :, 0:XH], ALU.add))
                ch.link(V.scalar_tensor_tensor(l, l, SLOPE, l, ALU.mult, ALU.max))
                V.tensor_tensor(l, l, adm[:, u, :, XH:], ALU.subtract).then_inc(logits, 1)
                V.tensor_tensor(lo[:, half, :, :], bcast(node[:], 1, XWHOLE), bcast(pos[:, u, 1, 0:XWHOLE], 2, NB),
                                ALU.is_equal)
                V.tensor_tensor(lo_r[:, half, :, :], bcast(node[:], 1, XPARTS), bcast(pos[:, u, 1, XWHOLE:], 2, NB),
                                ALU.is_equal)
                ch.link(V.tensor_tensor(hi[:, half, :, :], bcast(bid[:], 1, XT), bcast(pos[:, u, 0, :], 2, BLOCKS),
                                        ALU.is_equal))
                dve.wait_ge(weights, k + 1)
                m = msg[:, u, :, 0:XF].rearrange("p j (h e) -> p j h e", h=XH)
                ch.link(V.tensor_tensor(m, m, bcast(msg[:, u, :, XF:], 3, XE), ALU.mult))
                whole = msg[:, u, XWHOLE:, :]
                ch.link(V.tensor_scalar(part[:, 0], whole, 1.0, None, ALU.mult))
                V.tensor_tensor(part[:, 1], whole, part[:, 0], ALU.subtract).then_inc(chain, 1)
                for j in range(XT):
                    dve.wait_ge(summed, k * XT + (j + 1))
                    if j < XWHOLE:
                        V.tensor_tensor(wide[:, j], bcast(hi[:, half, j, :], 2, XROW),
                                        bcast(msg[:, u, j, :], 1, BLOCKS), ALU.mult).then_inc(widened, 1)
                    else:
                        if j == XWHOLE:
                            dve.wait_ge(chain, base + PER * k + PER)
                        V.tensor_tensor(wide_r[:, j - XWHOLE], bcast(bcast(hi[:, half, j, :], 2, XROW), 1, 2),
                                        bcast(part[:, :, j - XWHOLE, :], 2, BLOCKS), ALU.mult).then_inc(widened, 1)
                assert ch.n == PER - 1

            with dve.Fori(0, TRIPS) as i:
                for w in range(SPAN):
                    step(i * SPAN + w, w % XSLOTS, w % 2, i * (SPAN // XSLOTS) + (w // XSLOTS + 1))
            for k in TAIL:
                step(k, k % XSLOTS, k % 2, k // XSLOTS + 1)

        @block.tensor
        def _(pe):
            pe.sem_inc(summed, XT)
            for half in range(2):
                nc.tensor.matmul(acc[:, half, 0:HALF * XROW], zeros[:, 0:NB], zeros[:, 0:HALF * XROW],
                                 start=True, stop=False, skip_group_check=True)
            nc.tensor.matmul(psY[:].rearrange("p h d -> p (h d)"), zeros[:, 0:NB], zeros[:, 0:PAIR * D],
                             start=True, stop=True).then_inc(y_ready, 1)
            pe.wait_ge(weights_loaded, 16 * LOADS)
            pe.wait_ge(b2_spread, 16 * 3)
            pe.wait_ge(ones3_set, 1)

            def step(k, half):
                for j in range(XT):
                    pe.wait_ge(widened, k * XT + (j + 1))
                    if j < XWHOLE:
                        mine, parts = lo[:, half, j, :], [wide[:, j]]
                    else:
                        mine, parts = lo_r[:, half, j - XWHOLE, :], [wide_r[:, j - XWHOLE, n] for n in range(2)]
                    for w in parts:
                        for h in range(2):
                            last = nc.tensor.matmul(
                                acc[:, h, 0:HALF * XROW], mine,
                                w[:, h * HALF:(h + 1) * HALF, :].rearrange("p b r -> p (b r)"),
                                start=False, stop=False, skip_group_check=True)
                    last.then_inc(summed, 1)

            def first_products(i, e):
                pe.wait_ge(act_done, i * (XE * HC) + (e * HC + HC))
                for c in range(HC):
                    for kc in range(KC):
                        last = nc.tensor.matmul(psA[:, c, 0:PN], w1[:, e, kc, c * P:(c + 1) * P],
                                                xnT[:, bass.ds(i * PAIR, PAIR), kc * NB:(kc + 1) * NB],
                                                start=kc == 0, stop=kc == KC - 1)
                    last.then_inc(hid_ready, 1)

            def second_products(i, e):
                pe.wait_ge(act_done, i * (XE * HC) + (e + 2) * HC)
                pe.wait_ge(y_kept, i * XE + (e + 1))
                for h in range(PAIR):
                    for c in range(HC):
                        nc.tensor.matmul(psY[:, h, :], hid[:, e % 2, c, h * NB:(h + 1) * NB], w2[:, e, c, :],
                                         start=c == 0, stop=False)
                    last = nc.tensor.matmul(psY[:, h, :], ones3[:], b2k[:, e * D:(e + 1) * D], start=False, stop=True)
                last.then_inc(y_ready, 1)

            with pe.Fori(0, TRIPS) as i:
                for w in range(SPAN):
                    step(i * SPAN + w, w % 2)
                    if w % 2 == 0 and w < 2 * XE:
                        first_products(i, w // 2)
                    if w % 2 == 1 and w >= 3:
                        second_products(i, (w - 3) // 2)
            for k in TAIL:
                step(k, k % 2)
            for half in range(2):
                nc.tensor.matmul(acc[:, half, 0:HALF * XROW], zeros[:, 0:NB], zeros[:, 0:HALF * XROW],
                                 start=False, stop=True, skip_group_check=True)


def gates(nc, scope, b_gat, gamma, beta, hg_all, xad_all, acc, gate, row):
    HALF = BLOCKS // 2
    with ExitStack() as ctx:
        sb, _, sem = scope(ctx)
        bg = sb("bg", [NB, 3, XF])
        ext = sb("xext", [NB, BLOCKS, XH])
        num = sb("xnum", [NB, BLOCKS, XROW])
        a1 = sb("a1", [NB, BLOCKS, XF])
        red = sb("red", [NB, BLOCKS, 1])
        red2 = sb("red2", [NB, BLOCKS, 1])
        sc = sb("sc", [NB, BLOCKS, XE])
        rank = sb("rank", [NB, BLOCKS, XE])
        cmp = sb("cmp", [NB, BLOCKS, 1])
        first = sb("first", [NB, BLOCKS, XE])
        second = sb("second", [NB, BLOCKS, XE])
        loaded = sem("loaded_h")
        chain = sem("chain_h")
        to_exp = sem("to_exp")
        exped = sem("exped")
        block = ctx.enter_context(nc.Block())

        @block.sync
        def _(sp):
            for n, vec in enumerate((b_gat, gamma, beta)):
                sp.dma_start(bg[:, n, :], row(vec).to_broadcast([NB, XF])).then_inc(loaded, 16)

        @block.scalar
        def _(act):
            act.wait_ge(to_exp, 1)
            nc.scalar.activation(ext[:], ext[:], ACT.Exp).then_inc(exped, 1)
            act.wait_ge(to_exp, 2)
            nc.scalar.activation(red2[:], red2[:], ACT.Sqrt).then_inc(exped, 1)
            act.wait_ge(to_exp, 3)
            nc.scalar.activation(cmp[:], cmp[:], ACT.Exp).then_inc(exped, 1)

        @block.vector
        def _(dve):
            V = nc.vector
            ch = Chain(dve, chain)
            dve.wait_ge(loaded, 48)
            ch.link(V.tensor_tensor(ext[:], hg_all[:, :, XF:], xad_all[:, :, 0:XH], ALU.add))
            ch.link(V.scalar_tensor_tensor(ext[:], ext[:], SLOPE, ext[:], ALU.mult, ALU.max))
            V.tensor_tensor(ext[:], ext[:], xad_all[:, :, XH:], ALU.subtract).then_inc(to_exp, 1)
            dve.wait_ge(exped, 1)

            def heads(t):
                return t.rearrange("p b (h e) -> p b h e", h=XH)

            ch.link(V.tensor_tensor(heads(num[:, :, 0:XF]), heads(hg_all[:, :, 0:XF]), bcast(ext[:], 3, XE), ALU.mult))
            for half in range(2):
                s = slice(half * HALF, (half + 1) * HALF)
                sums = acc[:, half, 0:HALF * XROW].rearrange("p (b r) -> p b r", r=XROW)
                ch.link(V.tensor_tensor(num[:, s, 0:XF], num[:, s, 0:XF], sums[:, :, 0:XF], ALU.add))
                ch.link(V.tensor_tensor(num[:, s, XF:], ext[:, s, :], sums[:, :, XF:], ALU.add))
            ch.link(V.scalar_tensor_tensor(num[:, :, XF:], ext[:], 1e-16, num[:, :, XF:], ALU.mult, ALU.add))
            ch.link(V.reciprocal(num[:, :, XF:], num[:, :, XF:]))
            ch.link(V.tensor_tensor(heads(a1[:]), heads(num[:, :, 0:XF]), bcast(num[:, :, XF:], 3, XE), ALU.mult))
            ch.link(V.tensor_tensor(a1[:], a1[:], bcast(bg[:, 0, :], 1, BLOCKS), ALU.add))
            r1 = red[:].rearrange("p b a -> p (b a)")
            r2 = red2[:].rearrange("p b a -> p (b a)")
            ch.link(V.reduce_sum(r1, a1[:], AX_X))
            ch.link(V.tensor_scalar(r1, r1, 1.0 / XF, None, ALU.mult))
            ch.link(V.tensor_tensor(a1[:], a1[:], bcast(r1, 2, XF), ALU.subtract))
            ch.link(V.tensor_tensor(num[:, :, 0:XF], a1[:], a1[:], ALU.mult))
            ch.link(V.reduce_sum(r2, num[:, :, 0:XF], AX_X))
            V.tensor_scalar(r2, r2, 1.0 / XF, EPS, ALU.mult, ALU.add).then_inc(to_exp, 1)
            dve.wait_ge(exped, 2)
            ch.link(V.reciprocal(r2, r2))
            ch.link(V.tensor_tensor(a1[:], a1[:], bcast(r2, 2, XF), ALU.mult))
            ch.link(V.tensor_tensor(a1[:], a1[:], bcast(bg[:, 1, :], 1, BLOCKS), ALU.mult))
            ch.link(V.tensor_tensor(a1[:], a1[:], bcast(bg[:, 2, :], 1, BLOCKS), ALU.add))
            ch.link(V.reduce_sum(sc[:], a1[:].rearrange("p b (h e) -> p b e h", h=XH), AX_X))
            ch.link(V.tensor_scalar(sc[:], sc[:], 1.0 / XH, None, ALU.mult))
            ch.link(V.memset(rank[:], 0.0))
            for e in range(XE):
                for o in range(XE):
                    if o != e:
                        op = ALU.is_ge if o < e else ALU.is_gt
                        ch.link(V.tensor_tensor(cmp[:], sc[:, :, o:o + 1], sc[:, :, e:e + 1], op))
                        ch.link(V.tensor_tensor(rank[:, :, e:e + 1], rank[:, :, e:e + 1], cmp[:], ALU.add))
            ch.link(V.tensor_scalar(first[:], rank[:], 0.0, None, ALU.is_equal))
            ch.link(V.tensor_scalar(second[:], rank[:], 1.0, None, ALU.is_equal))
            ch.link(V.tensor_tensor(rank[:], first[:], sc[:], ALU.mult))
            ch.link(V.reduce_sum(r1, rank[:], AX_X))
            ch.link(V.tensor_tensor(rank[:], second[:], sc[:], ALU.mult))
            ch.link(V.reduce_sum(r2, rank[:], AX_X))
            V.tensor_tensor(cmp[:], red2[:], red[:], ALU.subtract).then_inc(to_exp, 1)
            dve.wait_ge(exped, 3)
            ch.link(V.tensor_scalar(red[:], cmp[:], 1.0, None, ALU.add))
            ch.link(V.reciprocal(red[:], red[:]))
            ch.link(V.tensor_tensor(red2[:], red[:], cmp[:], ALU.mult))
            ch.link(V.tensor_tensor(first[:], first[:], bcast(r1, 2, XE), ALU.mult))
            ch.link(V.tensor_tensor(second[:], second[:], bcast(r2, 2, XE), ALU.mult))
            ch.link(V.tensor_tensor(gate[:], first[:], second[:], ALU.add))


def combine(nc, scope, x_all, gate, y_dram, out):
    PAIR = 2
    SLOTS_Y = 5
    TRIPS = BLOCKS // PAIR // SLOTS_Y
    PER = XE * PAIR
    with ExitStack() as ctx:
        sb, _, sem = scope(ctx)
        y_sb = sb("y_back", [NB, SLOTS_Y, XE, PAIR * D])
        back = [sem(f"y_back{u}") for u in range(SLOTS_Y)]
        added = sem("y_added")
        stored = sem("stored_x")
        block = ctx.enter_context(nc.Block())

        def each_pair(eng, step):
            for u in range(SLOTS_Y):
                step(u, u, 0, True)
            with eng.Fori(1, TRIPS) as i:
                for u in range(SLOTS_Y):
                    step(i * SLOTS_Y + u, u, i, False)

        @block.sync
        def _(sp):
            def load(n, u, trip, first):
                if not first:
                    sp.wait_ge(added, (n - (SLOTS_Y - 1)) * PER)
                sp.dma_start(y_sb[:, u], y_dram[bass.ds(n * XE + 1, XE)].rearrange("e p f -> p e f")) \
                    .then_inc(back[u], 16)

            each_pair(sp, load)

        @block.vector
        def _(dve):
            def add(n, u, trip, first):
                dve.wait_ge(back[u], trip * 16 + 16)
                for e in range(XE):
                    for h in range(PAIR):
                        xb = x_all[:, bass.ds(n * PAIR + h, 1), :].rearrange("p a d -> p (a d)")
                        g = gate[:, bass.ds(n * PAIR + h, 1), e:e + 1].rearrange("p a d -> p (a d)")
                        if e > 0:
                            dve.wait_ge(added, n * PER + ((e - 1) * PAIR + h + 1))
                        nc.vector.scalar_tensor_tensor(xb, y_sb[:, u, e, h * D:(h + 1) * D], g, xb, ALU.mult, ALU.add) \
                            .then_inc(added, 1)

            each_pair(dve, add)

        @block.scalar
        def _(act):
            ov = out.rearrange("(b p) d -> p b d", p=NB)
            with act.Fori(0, BLOCKS // PAIR) as i:
                act.wait_ge(added, i * PER + PER)
                act.dma_start(ov[:, bass.ds(i * PAIR, PAIR), :], x_all[:, bass.ds(i * PAIR, PAIR), :]) \
                    .then_inc(stored, 16)
            act.wait_ge(stored, 16 * (BLOCKS // PAIR))


_INS = ['x', 'src', 'dst', 'L0_gnn_W', 'L0_gnn_att_src', 'L0_gnn_att_dst', 'L0_gnn_bias', 'L0_mix_W_qkv',
        'L0_mix_W_out', 'L0_mix_b_out', 'L0_ffn_W_gat', 'L0_ffn_att_src', 'L0_ffn_att_dst', 'L0_ffn_b_gat',
        'L0_ffn_ln_gamma', 'L0_ffn_ln_beta', 'L0_ffn_W1', 'L0_ffn_b1', 'L0_ffn_W2', 'L0_ffn_b2',
        'L0_ffn_edge_index']


def kernel(**inputs):
    import numpy as _np
    import concourse.bacc as _bacc
    from concourse import mybir as _mybir
    from concourse.bass_utils import run_bass_kernel_spmd as _run

    nc = _bacc.Bacc("TRN2", target_bir_lowering=False, num_devices=1)
    arrays, args = {}, []
    for name in _INS:
        a = _np.ascontiguousarray(inputs[name])
        arrays[f"in_{name}"] = a
        args.append(nc.dram_tensor(f"in_{name}", a.shape, _mybir.dt.from_np(a.dtype), kind="ExternalInput").ap())
    o = nc.dram_tensor("out_0", (N, D), F32, kind="ExternalOutput").ap()
    build(nc, *args, o)
    r = _run(nc, [arrays], core_ids=[0])
    return r.results[0]["out_0"]
```

```python
from contextlib import ExitStack

import concourse.bass as bass
from concourse import mybir

ALU = mybir.AluOpType
ACT = mybir.ActivationFunctionType
F32 = mybir.dt.float32
BF16 = mybir.dt.bfloat16
F32R = mybir.dt.float32r
I32 = mybir.dt.int32
AX_X = mybir.AxisListType.X
RMAX = bass.bass_isa.ReduceOp.max

P = 128
N = 6250
D = 256
NB = 125
BLOCKS = N // NB
KC = D // P
EPS = 1e-5
SLOPE = 0.2

GH, GC = 4, 64
EDGES = 200000
EP = 125
GT = 2
GROUPS = EDGES // (EP * GT)
ROW = D + GH
SLOTS = 6
AHEAD = 4
PAIRS = GROUPS + BLOCKS - 1
PG = 2
ST = PG * GT
STEPS = -(-PAIRS // (PG * SLOTS)) * SLOTS
LISTED = (STEPS + AHEAD) * PG
LH = LISTED // 2
CH = 100
CHUNKS = GROUPS // CH
EL = EP * GT
FAR = -1.0e7
SPREAD = 70.0

MH, MD = 4, 32
MW = MH * MD

XH, XE = 4, 4
XF = XH * XE
XROW = XF + XH
XEDGES = 131072
XT = 4
XGROUPS = XEDGES // (P * XT)
XSLOTS = 5
XAHEAD = 2
XWHOLE = (3, 2)
XPARTS = XT - min(XWHOLE)
YSLOTS = 5
HID = 2 * D
HC = HID // P


class Chain:

    def __init__(self, eng, sem, base=0):
        self.eng, self.sem, self.base, self.n = eng, sem, base, 0

    def link(self, ins):
        ins.then_inc(self.sem, 1)
        self.n += 1
        self.eng.wait_ge(self.sem, self.base + self.n)


def each_block(eng, step):
    SOME = 6
    trips = (BLOCKS - 4) // SOME
    for n in range(2):
        step(n, n % 2, True, False)
    with eng.Fori(0, trips) as i:
        for r in range(SOME):
            step(i * SOME + (2 + r), r % 2, False, False)
    for n in range(2 + trips * SOME, BLOCKS):
        step(n, n % 2, False, n >= BLOCKS - 2)


def bcast(ap, axis, n):
    shape = list(ap.shape)
    shape.insert(axis, n)
    return ap.unsqueeze(axis).to_broadcast(shape)


def floor_div(nc, ch, x, q, qi, t, d):
    ch.link(nc.vector.tensor_scalar(qi, x, 1.0 / d, None, ALU.mult))
    ch.link(nc.vector.tensor_copy(q, qi))
    ch.link(nc.vector.scalar_tensor_tensor(t, q, float(-d), x, ALU.mult, ALU.add))
    ch.link(nc.vector.tensor_scalar(t, t, 0.0, None, ALU.is_lt))
    ch.link(nc.vector.tensor_tensor(q, q, t, ALU.subtract))
    ch.link(nc.vector.scalar_tensor_tensor(t, q, float(-d), x, ALU.mult, ALU.add))
    ch.link(nc.vector.tensor_scalar(t, t, float(d), None, ALU.is_ge))
    ch.link(nc.vector.tensor_tensor(q, q, t, ALU.add))


def mean_and_variance(nc, ch, stats, mean, var):
    V = nc.vector
    m0, v0, m1, v1 = stats[:, :, 1], stats[:, :, 2], stats[:, :, 4], stats[:, :, 5]
    ch.link(V.tensor_tensor(var, m0, m1, ALU.subtract))
    ch.link(V.tensor_tensor(var, var, var, ALU.mult))
    ch.link(V.tensor_tensor(mean, v0, v1, ALU.add))
    ch.link(V.tensor_scalar(mean, mean, 1.0 / D, None, ALU.mult))
    ch.link(V.scalar_tensor_tensor(var, var, 0.25, mean, ALU.mult, ALU.add))
    ch.link(V.tensor_tensor(mean, m0, m1, ALU.add))
    ch.link(V.tensor_scalar(mean, mean, 0.5, None, ALU.mult))


def build(nc, x, src, dst, W, att_src, att_dst, gbias, W_qkv, W_out, b_out, W_gat, xatt_src, xatt_dst, b_gat,
          gamma, beta, W1, b1, W2, b2, xedges, out):
    table = nc.dram_tensor("table", [N, ROW], F32).ap()
    xtable = nc.dram_tensor("xtable", [N, XROW], F32).ap()
    xtable_dst = nc.dram_tensor("xtable_dst", [N, 2 * XH], F32).ap()

    def row(v):
        return v.rearrange("(a n) -> a n", a=1)

    with ExitStack() as whole:
        def scope(ctx):
            def sb(name, shape, dt=F32):
                return ctx.enter_context(nc.sbuf_tensor(name, shape, dt))

            def ps(name, shape):
                return ctx.enter_context(nc.psum_tensor(name, shape, F32))

            def sem(name):
                return ctx.enter_context(nc.semaphore(name))
            return sb, ps, sem

        sb, _, sem = scope(whole)
        x_all = sb("x_all", [NB, BLOCKS, D])
        ident = sb("ident", [P, P])
        ones = sb("ones", [P, P])
        zeros = sb("zeros", [P, 512])
        node = sb("node", [P, NB])
        hg_all = sb("hg_all", [NB, BLOCKS, XROW])
        xad_all = sb("xad_all", [NB, BLOCKS, 2 * XH])
        gate = sb("gate", [NB, BLOCKS, XE])
        room = sb("room", [P, BLOCKS, ROW])
        qk = room[:, :, 0:2 * NB]
        agg = room[0:NB, :, :]
        xnT = room[:, :, 0:KC * NB]

        xsrc_i = sb("xsrc_i", [P, XGROUPS, XT], I32)
        xdst_i = sb("xdst_i", [P, XGROUPS, XT], I32)
        xedges_loaded = sem("xedges_loaded")

        with ExitStack() as first:
            fsb, _, _ = scope(first)
            as_all = fsb("as_all", [NB, BLOCKS, GH])
            ad_m = fsb("ad_m", [NB, BLOCKS, 2 * GH])
            ex_self = fsb("ex_self", [NB, BLOCKS, GH])
            with ExitStack() as inner:
                isb, _, _ = scope(inner)
                src_i = isb("src_i", [EP, GROUPS, GT], I32)
                dst_f = isb("dst_f", [EP, GROUPS, GT])
                neg_base = isb("neg_base", [EP, LISTED])
                step_group = isb("step_group", [EP, LISTED], I32)
                step_block = isb("step_block", [EP, LISTED + PG], I32)
                sweeps = isb("sweeps", [EP, 1], I32)
                with ExitStack() as raw:
                    rsb, _, _ = scope(raw)
                    rows = rsb("rows", [CH, 2, CHUNKS, EL], I32)
                    prod = xsrc_i[0:NB].rearrange("p g j -> p (g j)").bitcast(F32) \
                        .rearrange("p (u t d) -> p u t d", u=2, t=2)
                    m_sb = xdst_i[0:MW].rearrange("p g j -> p (g j)").bitcast(F32)[:, 0:D]
                    edges_loaded = sem("edges_loaded")
                    linear_attention_and_projections(nc, scope, x, W, att_src, att_dst, gbias, W_qkv, W_out, b_out,
                                                     table, x_all, ident, ones, zeros, node, as_all, ad_m, qk, row,
                                                     src, dst, rows, prod, m_sb, edges_loaded)
                    schedule(nc, scope, rows, ident, ones, as_all, ad_m, ex_self, agg, src_i, dst_f, neg_base,
                             step_group, step_block, sweeps, edges_loaded)
                edges(nc, scope, xedges, xsrc_i, xdst_i, xedges_loaded, table, ident, zeros, node, ad_m, agg, src_i,
                      dst_f, neg_base, step_group, step_block, sweeps)
            nodes(nc, scope, table, W_gat, xatt_src, xatt_dst, xtable, xtable_dst, x_all, ident, agg, ex_self,
                  xnT, hg_all, xad_all, row)
        y_dram = nc.dram_tensor("experts_out", [XE * (BLOCKS // 2) + 1, NB, 2 * D], F32).ap()
        acc = whole.enter_context(nc.psum_tensor("acc", [NB, 2, 512], F32))
        gating_sums_and_experts(nc, scope, xsrc_i, xdst_i, xedges_loaded, xtable, xtable_dst, W1, b1, W2, b2, zeros,
                                node, xnT, acc, y_dram, row)
        y_sb = sb("y_back", [NB, YSLOTS, XE, 2 * D])
        y_loaded = [sem(f"y_loaded{u}") for u in range(YSLOTS)]
        gates(nc, scope, b_gat, gamma, beta, hg_all, xad_all, acc, gate, row, y_dram, y_sb, y_loaded)
        combine(nc, scope, x_all, gate, y_dram, y_sb, y_loaded, out)


def linear_attention_and_projections(nc, scope, x, W, att_src, att_dst, gbias, W_qkv, W_out, b_out, table,
                                     x_all, ident, ones, zeros, node, as_all, ad_m, qk, row, src, dst,
                                     rows, prod, m_sb, edges_loaded):
    U = 2
    with ExitStack() as ctx:
        sb, ps, sem = scope(ctx)
        w_sb = sb("w_sb", [P, KC, D])
        qkv_sb = sb("qkv_sb", [P, KC, 3 * MW])
        wout_sb = sb("wout_sb", [MW, D])
        att = sb("att", [NB, 2, D])
        bias = sb("bias", [NB, 2, D])
        stats = sb("stats", [NB, BLOCKS, 6])
        mean = sb("mean", [NB, BLOCKS])
        rstd = sb("rstd", [NB, BLOCKS])
        eps = sb("eps", [NB, 1])
        xn = sb("xn", [NB, U, D])
        xnT = sb("xnT_a", [P, U, KC, NB])
        hrow = sb("hrow", [NB, U, ROW])
        v_all = sb("v_all", [NB, BLOCKS, MW + 1])
        nmax = sb("nmax", [MW, 1])
        kx = sb("kx", [MW, U, NB])
        kxT = sb("kxT", [NB, U, MW])
        rk = sb("rk", [MW, 1])
        cbd = sb("cbd", [MW, MW])
        cbdT = sb("cbdT", [MW, MW])
        qs = sb("qs", [MW, U, NB])

        psT = ps("psT", [P, U, 512])
        psH = ps("psH", [NB, U, 512])
        psQ = ps("psQ", [P, U, 512])
        psC = ps("psC", [P, 512])

        loaded = sem("loaded")
        consts = sem("consts")
        consts0 = sem("consts0")
        bias_summed = sem("bias_summed")
        biased = sem("biased")
        var_ready = sem("var_ready")
        std_ready = sem("std_ready")
        normed = sem("normed")
        turned = sem("turned")
        turned_sb = sem("turned_sb")
        projected = sem("projected")
        qk_kept = sem("qk_kept")
        h_kept = sem("h_kept")
        v_kept = sem("v_kept")
        logits_kept = sem("logits_kept")
        row_stored = [sem(f"row_stored{u}") for u in range(U)]
        dve_chain = sem("dve_chain_a")
        max_known = sem("max_known")
        k_exp = sem("k_exp")
        k_turned = sem("k_turned")
        k_kept = sem("k_kept")
        context_part = sem("context_part")
        context_masked = sem("context_masked")
        context_turned = sem("context_turned")
        context_kept = sem("context_kept")
        m_ready = sem("m_ready")
        m_kept = sem("m_kept")
        q_staged = sem("q_staged")
        mixed = sem("mixed")
        mix_added = sem("mix_added")
        LOADS = 7
        XCH = 5
        XB = BLOCKS // XCH
        x_loaded = [sem(f"x_loaded{c}") for c in range(XCH)]
        block = ctx.enter_context(nc.Block())

        @block.sync
        def _(sp):
            xv = x.rearrange("(b p) d -> p b d", p=NB)
            for c in range(XCH):
                sp.dma_start(x_all[:, c * XB:(c + 1) * XB, :], xv[:, c * XB:(c + 1) * XB, :]) \
                    .then_inc(x_loaded[c], 16)
            sp.dma_start(w_sb[:], W.rearrange("(c p) n -> p c n", p=P)).then_inc(loaded, 16)
            sp.dma_start(qkv_sb[:], W_qkv.rearrange("(c p) n -> p c n", p=P)).then_inc(loaded, 16)
            sp.dma_start(wout_sb[:], W_out).then_inc(loaded, 16)
            for n, vec in enumerate((att_src, att_dst)):
                flat = row(vec.rearrange("h c -> (h c)"))
                sp.dma_start(att[:, n, :], flat.to_broadcast([NB, D])).then_inc(loaded, 16)
            for n, vec in enumerate((b_out, gbias)):
                sp.dma_start(bias[:, n, :], row(vec).to_broadcast([NB, D])).then_inc(loaded, 16)
            for a, ends in enumerate((dst, src)):
                sp.dma_start(rows[:, a, :, :], ends.rearrange("(c p e) -> p c e", c=CHUNKS, e=EL)) \
                    .then_inc(edges_loaded, 16)

            def store_row(n, u, first, last):
                sp.wait_ge(h_kept, n + 1)
                sp.wait_ge(logits_kept, n + 1)
                sp.dma_start(table[bass.ds(n * NB, NB), :], hrow[:, u, :]).then_inc(row_stored[u], 16)

            each_block(sp, store_row)
            for u in range(U):
                sp.wait_ge(row_stored[u], 16 * (BLOCKS // U))

        @block.gpsimd
        def _(pool):
            nc.gpsimd.memset(ones[:], 1.0).then_inc(consts0, 1)
            nc.gpsimd.memset(zeros[:], 0.0).then_inc(consts0, 1)
            nc.gpsimd.iota(node[:], [[1, NB]], base=0, channel_multiplier=0,
                           allow_small_or_imprecise_dtypes=True).then_inc(consts, 1)
            pool.wait_ge(consts0, 2)
            nc.gpsimd.affine_select(out=ident[:], in_=ones[:], compare_op=ALU.is_equal, fill=0.0, base=0,
                                    pattern=[[-1, P]], channel_multiplier=1).then_inc(consts, 1)
            nc.gpsimd.memset(v_all[:, :, MW:], 1.0).then_inc(consts, 1)
            nc.gpsimd.memset(cbd[:], 0.0).then_inc(consts, 1)
            pool.wait_ge(loaded, 16 * LOADS)
            nc.gpsimd.tensor_tensor(bias[:, 0, :], bias[:, 0, :], bias[:, 1, :], ALU.add).then_inc(bias_summed, 1)
            pool.wait_ge(bias_summed, 1)
            pool.wait_ge(normed, BLOCKS)
            nc.gpsimd.tensor_tensor(x_all[:], x_all[:], bcast(bias[:, 0, :], 1, BLOCKS), ALU.add).then_inc(biased, 1)

        @block.vector
        def _(dve):
            for c in range(XCH):
                dve.wait_ge(x_loaded[c], 16)
                with dve.Fori(0, XB // 5) as i:
                    for r in range(5):
                        n = i * 5 + (c * XB + r)
                        nc.vector.bn_stats(stats[:, bass.ds(n, 1), :].rearrange("p a s -> p (a s)"),
                                           x_all[:, bass.ds(n, 1), :].rearrange("p a d -> p (a d)")) \
                            .then_inc(dve_chain, 1)
            dve.wait_ge(dve_chain, BLOCKS)
            ch = Chain(dve, dve_chain, BLOCKS)
            mean_and_variance(nc, ch, stats, mean[:], rstd[:])
            ch.link(nc.vector.memset(eps[:], EPS))
            nc.vector.tensor_copy(stats[:, :, 0], rstd[:]).then_inc(var_ready, 1)
            dve.wait_ge(std_ready, 1)
            ch.link(nc.vector.reciprocal(rstd[:], rstd[:]))
            dve.wait_ge(loaded, 16 * LOADS)
            dve.wait_ge(consts, 4)
            base = ch.base + ch.n
            PER = 3

            def normalize(n, u):
                nc.vector.tensor_scalar(xn[:, u, :], x_all[:, bass.ds(n, 1), :].rearrange("p a d -> p (a d)"),
                                        mean[:, bass.ds(n, 1)], rstd[:, bass.ds(n, 1)],
                                        ALU.subtract, ALU.mult).then_inc(normed, 1)

            def logits_of(n, u, first, last):
                ch = Chain(dve, dve_chain, base + PER * n)
                if not last:
                    dve.wait_ge(turned, n + 1)
                    normalize(n + 2, u)
                dve.wait_ge(h_kept, n + 1)
                ch.link(nc.vector.tensor_tensor(prod[:, u, :, :], bcast(hrow[:, u, 0:D], 1, 2), att[:], ALU.mult))
                ch.link(nc.vector.reduce_sum(as_all[:, bass.ds(n, 1), :],
                                             prod[:, u, 0, :].rearrange("p (a h c) -> p a h c", a=1, h=GH), AX_X))
                ch.link(nc.vector.reduce_sum(ad_m[:, bass.ds(n, 1), 0:GH],
                                             prod[:, u, 1, :].rearrange("p (a h c) -> p a h c", a=1, h=GH), AX_X))
                assert ch.n == PER
                nc.vector.tensor_scalar(hrow[:, u, D:ROW].rearrange("p (a h) -> p a h", a=1),
                                        as_all[:, bass.ds(n, 1), :], 1.0, None, ALU.mult).then_inc(logits_kept, 1)

            for u in range(U):
                normalize(u, u)
            each_block(dve, logits_of)
            ch = Chain(dve, dve_chain, base + PER * BLOCKS)
            dve.wait_ge(qk_kept, BLOCKS)
            nc.vector.tensor_reduce(nmax[:], qk[:, :, NB:], mybir.AxisListType.XY, ALU.max, negate=True) \
                .then_inc(max_known, 1)

            def keep_k(n, u, first, last):
                dve.wait_ge(k_turned, n + 1)
                if not first:
                    dve.wait_ge(context_part, n)
                nc.vector.tensor_copy(kxT[:, u, :], psT[0:NB, u, 0:MW]).then_inc(k_kept, 1)

            each_block(dve, keep_k)
            dve.wait_ge(context_part, BLOCKS + 1)
            ch.link(nc.vector.reciprocal(rk[:], psC[:, MW:MW + 1]))
            for h in range(MH):
                s = slice(h * MD, (h + 1) * MD)
                nc.vector.tensor_scalar(cbd[s, s], psC[s, s], rk[s, :], float(MD) ** -0.5, ALU.mult, ALU.mult) \
                    .then_inc(context_masked, 1)
            dve.wait_ge(context_turned, 1)
            nc.vector.tensor_copy(cbdT[:], psT[:, 0, 0:MW]).then_inc(context_kept, 1)
            dve.wait_ge(m_ready, 1)
            nc.vector.tensor_copy(m_sb, psQ[:, 0, 0:D]).then_inc(m_kept, 1)

            dve.wait_ge(biased, 1)

            def add_mix(n, u, first, last):
                dve.wait_ge(mixed, n + 1)
                xb = x_all[:, bass.ds(n, 1), :]
                nc.vector.tensor_tensor(xb, xb, psH[:, u, 0:D].rearrange("p (a d) -> p a d", a=1), ALU.add) \
                    .then_inc(mix_added, 1)

            each_block(dve, add_mix)

        @block.scalar
        def _(act):
            act.wait_ge(var_ready, 1)
            nc.scalar.activation(rstd[:], stats[:, :, 0], ACT.Sqrt, bias=eps[:]).then_inc(std_ready, 1)

            def keep_turned(n, u):
                act.wait_ge(turned, n + 1)
                nc.scalar.copy(xnT[:, u, :, :], psT[:, u, 0:KC * NB].rearrange("p (c n) -> p c n", c=KC)) \
                    .then_inc(turned_sb, 1)

            def keep_projected(n, u, first, last):
                if not (last and u == U - 1):
                    keep_turned(n + 1, (u + 1) % U)
                act.wait_ge(projected, n + 1)
                nc.scalar.copy(qk[:, bass.ds(n, 1), :], psQ[:, u, 0:2 * NB].rearrange("p (a n) -> p a n", a=1)) \
                    .then_inc(qk_kept, 1)
                if not first:
                    act.wait_ge(row_stored[u], (n - u) * (16 // U))
                nc.scalar.copy(hrow[:, u, 0:D], psH[:, u, 0:D]).then_inc(h_kept, 1)
                nc.scalar.copy(v_all[:, bass.ds(n, 1), 0:MW],
                               psH[:, u, D:D + MW].rearrange("p (a h) -> p a h", a=1)).then_inc(v_kept, 1)

            keep_turned(0, 0)
            each_block(act, keep_projected)
            act.wait_ge(max_known, 1)

            def exp_k(n, u, first, last):
                if not first:
                    act.wait_ge(k_turned, n - 1)
                nc.scalar.activation(kx[:, u, :], qk[:, bass.ds(n, 1), NB:].rearrange("p a n -> p (a n)"), ACT.Exp,
                                     bias=nmax[:]).then_inc(k_exp, 1)

            each_block(act, exp_k)

            def stage_q(n, u, first, last):
                if not first:
                    act.wait_ge(mixed, n - 1)
                nc.scalar.copy(qs[:, u, :], qk[:, bass.ds(n, 1), 0:NB].rearrange("p a n -> p (a n)")) \
                    .then_inc(q_staged, 1)

            each_block(act, stage_q)

        @block.tensor
        def _(pe):
            pe.wait_ge(loaded, 16 * LOADS)
            pe.wait_ge(consts, 4)

            def turn(n, u):
                pe.wait_ge(normed, n + 1)
                for c in range(KC):
                    last = nc.tensor.transpose(psT[:, u, c * NB:(c + 1) * NB], xn[:, u, c * P:(c + 1) * P],
                                               ident[0:NB, 0:NB])
                last.then_inc(turned, 1)

            def project(n, u, first, last):
                if not (last and u == U - 1):
                    turn(n + 1, (u + 1) % U)
                pe.wait_ge(turned_sb, n + 1)
                if not first:
                    pe.wait_ge(v_kept, n - 1)
                for w, a, b in ((w_sb[:], 0, D), (qkv_sb[:, :, 2 * MW:], D, D + MW)):
                    for c in range(KC):
                        nc.tensor.matmul(psH[:, u, a:b], xnT[:, u, c, :], w[:, c, :], start=c == 0,
                                         stop=c == KC - 1)
                for t in range(2):
                    for c in range(KC):
                        mm = nc.tensor.matmul(psQ[:, u, t * NB:(t + 1) * NB], qkv_sb[:, c, t * MW:(t + 1) * MW],
                                              xnT[:, u, c, :], start=c == 0, stop=c == KC - 1)
                mm.then_inc(projected, 1)

            turn(0, 0)
            each_block(pe, project)
            nc.tensor.matmul(psC[:, 0:MW + 1], zeros[:, 0:P], zeros[:, 0:MW + 1], start=True, stop=False,
                             skip_group_check=True).then_inc(context_part, 1)

            def turn_k(n, u):
                pe.wait_ge(k_exp, n + 1)
                nc.tensor.transpose(psT[0:NB, u, 0:MW], kx[:, u, :], ident[:]).then_inc(k_turned, 1)

            def context(n, u, first, last):
                if not (last and u == U - 1):
                    turn_k(n + 1, (u + 1) % U)
                pe.wait_ge(k_kept, n + 1)
                nc.tensor.matmul(psC[:, 0:MW + 1], kxT[:, u, :],
                                 v_all[:, bass.ds(n, 1), :].rearrange("p a d -> p (a d)"), start=False,
                                 stop=False, skip_group_check=True).then_inc(context_part, 1)

            turn_k(0, 0)
            each_block(pe, context)
            pe.wait_ge(context_masked, MH)
            nc.tensor.transpose(psT[:, 0, 0:MW], cbd[:], ident[:]).then_inc(context_turned, 1)
            pe.wait_ge(context_kept, 1)
            nc.tensor.matmul(psQ[:, 0, 0:D], cbdT[:], wout_sb[:], start=True, stop=True).then_inc(m_ready, 1)
            pe.wait_ge(m_kept, 1)

            def mix(n, u, first, last):
                pe.wait_ge(q_staged, n + 1)
                if not first:
                    pe.wait_ge(mix_added, n - 1)
                nc.tensor.matmul(psH[:, u, 0:D], qs[:, u, :], m_sb, start=True, stop=True).then_inc(mixed, 1)

            each_block(pe, mix)


def schedule(nc, scope, rows, ident, ones, as_all, ad_m, ex_self, agg, src_i, dst_f, neg_base, step_group,
             step_block, sweeps, edges_loaded):
    with ExitStack() as ctx:
        sb, ps, sem = scope(ctx)
        rowsf = rows[:].bitcast(F32)
        ext = sb("ext", [CH, 3, CHUNKS])
        extb = sb("extb", [CH, 3, CHUNKS])
        exti = sb("exti", [CH, 3, CHUNKS], I32)
        extt = sb("extt", [CH, 3, CHUNKS])
        gid = sb("gid", [CH, CHUNKS])
        stp = sb("stp", [P, LISTED])
        below = sb("below", [CH, CHUNKS, LISTED], BF16)
        ones_h = sb("ones_h", [CH, EP], BF16)
        broken = sb("broken", [CH, CHUNKS])
        flag = sb("flag", [EP, 1])
        keep = sb("keep", [EP, 1])
        grp = sb("grp", [EP, LISTED])
        alt = sb("alt", [EP, LISTED])
        top = sb("top", [NB, GH])
        topall = sb("topall", [NB, GH])
        s_self = sb("s_self", [NB, BLOCKS, GH])
        s_top = sb("s_top", [NB, BLOCKS, GH])
        psG = ps("psG", [EP, 2, 512])
        psF = ps("psF", [EP, 512])
        psX = ps("psX", [EP, 2, 512])
        spread = [sem("dst_spread"), sem("src_spread")]
        edges_turned = sem("edges_turned")
        edges_kept = sem("edges_kept")
        largest = sem("largest")
        shifted = sem("shifted")
        iotas = sem("iotas")
        cleared = sem("cleared")
        chain = sem("sched_chain")
        marks = sem("marks")
        counted = sem("counted")
        top_known = sem("top_known")
        top_shared = sem("top_shared")
        self_shifted = sem("self_shifted")
        self_weight = sem("self_weight")
        block = ctx.enter_context(nc.Block())

        @block.sync
        def _(sp):
            sp.wait_ge(largest, 1)
            sp.dma_start(ext[1:CH, 2, :], ext[0:CH - 1, 0, :]).then_inc(shifted, 16)
            sp.dma_start(ext[0:1, 2, 1:CHUNKS], ext[CH - 1:CH, 0, 0:CHUNKS - 1]).then_inc(shifted, 16)

        @block.gpsimd
        def _(pool):
            nc.gpsimd.iota(gid[:], [[CH, CHUNKS]], base=0, channel_multiplier=1,
                           allow_small_or_imprecise_dtypes=True).then_inc(iotas, 1)
            nc.gpsimd.iota(stp[:], [[1, LISTED]], base=0, channel_multiplier=0,
                           allow_small_or_imprecise_dtypes=True).then_inc(iotas, 1)
            nc.gpsimd.memset(ones_h[:], 1.0).then_inc(iotas, 1)
            pool.wait_ge(top_known, 1)
            nc.gpsimd.partition_all_reduce(topall[:], top[:], NB, RMAX).then_inc(top_shared, 1)
            nc.gpsimd.memset(agg[:], 0.0).then_inc(cleared, 1)

        @block.vector
        def _(dve):
            ch = Chain(dve, chain)
            V = nc.vector
            dve.wait_ge(edges_loaded, 16 * 2)
            V.tensor_scalar(rowsf[:, 0], rows[:, 0], 1.0, None, ALU.mult).then_inc(spread[0], 1)
            V.tensor_scalar(rowsf[:, 1], rows[:, 1], float(N - 1), None, ALU.min).then_inc(spread[1], 1)
            V.tensor_reduce(top[:], as_all[:].rearrange("p b h -> p h b"), AX_X, ALU.max).then_inc(top_known, 1)
            dve.wait_ge(iotas, 3)
            dve.wait_ge(spread[0], 1)
            ch.link(V.memset(ext[:], 0.0))
            V.tensor_reduce(ext[:, 0, :], rowsf[:, 0, :, :], AX_X, ALU.max).then_inc(largest, 1)
            ch.link(V.tensor_reduce(ext[:, 1, :], rowsf[:, 0, :, :], AX_X, ALU.min))
            dve.wait_ge(largest, 1)
            dve.wait_ge(shifted, 32)
            ch.link(V.tensor_scalar(ext[:], ext[:], float(N - 1), None, ALU.min))
            floor_div(nc, ch, ext[:], extb[:], exti[:], extt[:], NB)
            ch.link(V.tensor_tensor(broken[:], extb[:, 2, :], extb[:, 1, :], ALU.is_gt))
            ch.link(V.tensor_tensor(gid[:], gid[:], extb[:, 0, :], ALU.add))
            for c in range(CHUNKS):
                V.tensor_scalar(below[:, c, :], stp[0:CH, :], gid[:, c:c + 1], None, ALU.is_gt).then_inc(marks, 1)
            ch.link(V.tensor_tensor(s_self[:], as_all[:], ad_m[:, :, 0:GH], ALU.add))
            ch.link(V.scalar_tensor_tensor(s_self[:], s_self[:], SLOPE, s_self[:], ALU.mult, ALU.max))
            dve.wait_ge(top_shared, 1)
            ch.link(V.tensor_tensor(s_top[:], ad_m[:, :, 0:GH], bcast(topall[:], 1, BLOCKS), ALU.add))
            ch.link(V.scalar_tensor_tensor(s_top[:], s_top[:], SLOPE, s_top[:], ALU.mult, ALU.max))
            ch.link(V.scalar_tensor_tensor(ad_m[:, :, GH:], s_self[:], SPREAD, s_top[:], ALU.add, ALU.min))
            V.tensor_tensor(s_self[:], s_self[:], ad_m[:, :, GH:], ALU.subtract).then_inc(self_shifted, 1)
            dve.wait_ge(counted, 2)
            ch.link(V.tensor_reduce(flag[:], psF[:, 0:CHUNKS], AX_X, ALU.max))
            ch.link(V.tensor_scalar(flag[:], flag[:], 0.5, None, ALU.is_gt))
            ch.link(V.tensor_scalar(keep[:], flag[:], -1.0, 1.0, ALU.mult, ALU.add))
            ch.link(V.tensor_scalar(sweeps[:], flag[:], float(BLOCKS - 1), 1.0, ALU.mult, ALU.add))
            ch.link(V.tensor_scalar(grp[:].rearrange("p (h l) -> p h l", h=2), psG[:, :, 0:LH], float(GROUPS - 1),
                                    None, ALU.min))
            ch.link(V.tensor_tensor(alt[:], stp[0:EP, :], grp[:], ALU.subtract))
            ch.link(V.tensor_scalar(alt[:], alt[:], float(BLOCKS - 1), keep[:], ALU.min, ALU.mult))
            ch.link(V.tensor_copy(step_block[:, PG:], alt[:]))
            ch.link(V.tensor_copy(step_block[:, 0:PG], alt[:, 0:PG]))
            ch.link(V.tensor_scalar(neg_base[:], alt[:], float(-NB), None, ALU.mult))
            ch.link(V.tensor_scalar(alt[:], stp[0:EP, :], GROUPS - 0.5, flag[:], ALU.is_gt, ALU.mult))
            ch.link(V.scalar_tensor_tensor(neg_base[:], alt[:], FAR, neg_base[:], ALU.mult, ALU.add))
            ch.link(V.memset(neg_base[:, PAIRS:], FAR))
            ch.link(V.tensor_scalar(grp[:], grp[:], keep[:], None, ALU.mult))
            ch.link(V.tensor_scalar(alt[:], stp[0:EP, :], float(GROUPS - 1), flag[:], ALU.min, ALU.mult))
            ch.link(V.tensor_tensor(grp[:], grp[:], alt[:], ALU.add))
            ch.link(V.tensor_copy(step_group[:], grp[:]))

        @block.scalar
        def _(act):
            for a, ends in ((0, dst_f), (1, src_i)):
                for c in range(CHUNKS):
                    n = a * CHUNKS + c
                    act.wait_ge(edges_turned, n + 1)
                    nc.scalar.copy(ends[:, c * CH:(c + 1) * CH, :].rearrange("p g j -> p j g"),
                                   psX[:, n % 2, 0:GT * CH].rearrange("p (j g) -> p j g", j=GT)) \
                        .then_inc(edges_kept, 1)
            act.wait_ge(self_shifted, 1)
            nc.scalar.activation(ex_self[:], s_self[:], ACT.Exp).then_inc(self_weight, 1)

        @block.tensor
        def _(pe):
            tiles = rowsf.rearrange("p a c (e j) -> p a c j e", j=GT)
            for a in range(2):
                pe.wait_ge(spread[a], 1)
                for c in range(CHUNKS):
                    n = a * CHUNKS + c
                    if n >= 2:
                        pe.wait_ge(edges_kept, n - 1)
                    for j in range(GT):
                        last = nc.tensor.transpose(psX[:, n % 2, j * CH:(j + 1) * CH], tiles[:, a, c, j, :],
                                                   ident[0:CH, 0:CH])
                    last.then_inc(edges_turned, 1)
            pe.wait_ge(marks, CHUNKS)
            nc.tensor.matmul(psF[:, 0:CHUNKS], ones[0:CH, 0:EP], broken[:], start=True, stop=True).then_inc(counted, 1)
            for c in range(CHUNKS):
                k = CH - (c == CHUNKS - 1)
                for h in range(2):
                    last = nc.tensor.matmul(psG[:, h, 0:LH], ones_h[0:k, :], below[0:k, c, h * LH:(h + 1) * LH],
                                            start=c == 0, stop=c == CHUNKS - 1)
            last.then_inc(counted, 1)


def edges(nc, scope, xedges, xsrc_i, xdst_i, xedges_loaded, table, ident, zeros, node, ad_m, agg, src_i, dst_f,
          neg_base, step_group, step_block, sweeps):
    with ExitStack() as ctx:
        sb, ps, sem = scope(ctx)
        idx = sb("idx", [EP, SLOTS, ST], I32)
        rel = sb("rel", [EP, SLOTS, ST])
        msg = sb("msg", [EP, SLOTS, ST, ROW])
        hot = sb("hot", [EP, SLOTS, ST, NB])
        hotT = sb("hotT", [NB, 2, ST, EP])
        lg = sb("lg", [EP, SLOTS, ST, GH])
        psT = ps("psT_e", [NB, 2, 512])
        psD = ps("psD_e", [EP, 2, 512])
        psS = ps("psS_e", [NB, 2, PG, 512])
        staged = sem("staged")
        opened = sem("opened")
        gathered = [[sem(f"gathered{u}_{j}") for j in range(ST)] for u in range(SLOTS)]
        assert BLOCKS * (STEPS // SLOTS) * 16 < 65536
        hot_ready = sem("hot_ready")
        hot_turned = sem("hot_turned")
        hotT_ready = sem("hotT_ready")
        dst_picked = sem("dst_picked")
        logits = sem("logits")
        weights = sem("weights")
        weighed = sem("weighed")
        summed = sem("summed")
        added = sem("added")
        chain = sem("edge_chain")
        moved = sem("moved")
        block = ctx.enter_context(nc.Block())
        TRIPS = STEPS // SLOTS
        assert TRIPS * SLOTS == STEPS

        def count(eng):
            return eng.value_load(sweeps[0:1, 0:1], min_val=1, max_val=BLOCKS)

        @block.sync
        def _(sp):
            v = xedges.rearrange("s (p g j) -> s p g j", p=P, j=XT)
            sp.dma_start(xsrc_i[:], v[0]).then_inc(xedges_loaded, 16)
            sp.dma_start(xdst_i[:], v[1]).then_inc(xedges_loaded, 16)

        @block.gpsimd
        def _(pool):
            n_sweeps = count(pool)
            with pool.Fori(0, n_sweeps) as s:
                with pool.Fori(0, TRIPS) as i:
                    for u in range(SLOTS):
                        pool.wait_ge(staged, s * (STEPS + AHEAD) + i * SLOTS + (u + 1))
                        pool.sem_inc(opened, 1)
                        for j in range(ST):
                            nc.gpsimd.indirect_dma_start(
                                msg[:, u, j, :], None, table[:, :],
                                bass.IndirectOffsetOnAxis(ap=idx[:, u, j:j + 1], axis=0)).then_inc(gathered[u][j], 16)

        @block.scalar
        def _(act):
            n_sweeps = count(act)

            def stage(at, u, free, done):
                gs = [act.value_load(step_group[0:1, bass.ds(at * PG + n, 1)], min_val=0, max_val=GROUPS - 1)
                      for n in range(PG)]
                act.wait_ge(free, done)
                for n, g in enumerate(gs):
                    t = slice(n * GT, (n + 1) * GT)
                    nc.scalar.copy(idx[:, u, t], src_i[:, bass.ds(g, 1), :].rearrange("p a j -> p (a j)"))
                    last = nc.scalar.activation(rel[:, u, t], dst_f[:, bass.ds(g, 1), :].rearrange("p a j -> p (a j)"),
                                                ACT.Identity, bias=neg_base[:, bass.ds(at * PG + n, 1)])
                last.then_inc(staged, 1)

            def keep_turned(u, done):
                act.wait_ge(hot_turned, done)
                nc.scalar.copy(hotT[:, u % 2, :, :], psT[:, u % 2, 0:ST * EP].rearrange("p (j e) -> p j e", j=ST)) \
                    .then_inc(hotT_ready, 1)

            with act.Fori(0, n_sweeps) as s:
                for a in range(AHEAD):
                    stage(a, a, moved, 2 * s + 1)
                keep_turned(0, s * (STEPS + 3) + 1)
                keep_turned(1, s * (STEPS + 3) + 2)
                with act.Fori(0, TRIPS) as i:
                    for u in range(SLOTS):
                        act.wait_ge(logits, s * STEPS + i * SLOTS + (u + 1))
                        nc.scalar.activation(msg[:, u, :, D:ROW], lg[:, u, :, :], ACT.Exp).then_inc(weights, 1)
                        keep_turned(u + 2, s * (STEPS + 3) + i * SLOTS + (u + 3))
                        stage(i * SLOTS + (u + AHEAD), (u + AHEAD) % SLOTS, summed,
                              s * (STEPS + 1) + i * SLOTS + (u + 2 * AHEAD - SLOTS + 2))

        @block.vector
        def _(dve):
            dve.sem_inc(moved, 1)
            n_sweeps = count(dve)
            PER = 3

            def one_hot(u, done):
                dve.wait_ge(staged, done)
                nc.vector.tensor_tensor(hot[:, u, :, :], bcast(node[0:EP, :], 1, ST), bcast(rel[:, u, :], 2, NB),
                                        ALU.is_equal).then_inc(hot_ready, 1)

            def add(at, bank, s):
                bs = [dve.value_load(step_block[0:1, bass.ds(at * PG + n, 1)], min_val=0, max_val=BLOCKS - 1)
                      for n in range(PG)]
                dve.wait_ge(summed, s * (STEPS + 1) + at + (1 + AHEAD))
                for n, b in enumerate(bs):
                    to = agg[:, bass.ds(b, 1), :]
                    dve.wait_ge(added, s * ((STEPS + 1) * PG) + at * PG + (n + 1))
                    nc.vector.tensor_tensor(to, to, psS[:, bank, n, 0:ROW].rearrange("p (a r) -> p a r", a=1),
                                            ALU.add).then_inc(added, 1)

            with dve.Fori(0, n_sweeps) as s:
                one_hot(0, s * (STEPS + AHEAD) + 1)
                one_hot(1, s * (STEPS + AHEAD) + 2)
                one_hot(2, s * (STEPS + AHEAD) + 3)
                with dve.Fori(0, TRIPS) as i:
                    for u in range(SLOTS):
                        k = s * STEPS + i * SLOTS + u
                        ch = Chain(dve, chain, PER * k)
                        for j in range(ST):
                            dve.wait_ge(gathered[u][j], (s * TRIPS + i + 1) * 16)
                        dve.wait_ge(dst_picked, s * (STEPS + 1) + i * SLOTS + (u + 1))
                        pick = psD[:, u % 2, 0:ST * 2 * GH].rearrange("p (j f) -> p j f", j=ST)
                        ch.link(nc.vector.tensor_tensor(lg[:, u, :, :], msg[:, u, :, D:ROW], pick[:, :, 0:GH], ALU.add))
                        ch.link(nc.vector.scalar_tensor_tensor(lg[:, u, :, :], lg[:, u, :, :], SLOPE, lg[:, u, :, :],
                                                               ALU.mult, ALU.max))
                        ch.link(nc.vector.tensor_tensor(lg[:, u, :, :], lg[:, u, :, :], pick[:, :, GH:], ALU.subtract))
                        nc.vector.tensor_scalar(lg[:, u, :, :], lg[:, u, :, :], 80.0, None, ALU.min).then_inc(logits, 1)
                        assert ch.n == PER
                        one_hot((u + 3) % SLOTS, s * (STEPS + AHEAD) + i * SLOTS + (u + 4))
                        dve.wait_ge(weights, k + 1)
                        m = msg[:, u, :, 0:D].rearrange("p j (h c) -> p j h c", h=GH)
                        nc.vector.tensor_tensor(m, m, bcast(msg[:, u, :, D:ROW], 3, GC), ALU.mult).then_inc(weighed, 1)
                        add(i * SLOTS + u, (u + 1) % 2, s)
                add(STEPS, (STEPS + 1) % 2, s)
                dve.wait_ge(staged, (s + 1) * (STEPS + AHEAD))
                dve.wait_ge(dst_picked, (s + 1) * (STEPS + 1))
                dve.wait_ge(hot_turned, (s + 1) * (STEPS + 3))
                dve.wait_ge(hotT_ready, (s + 1) * (STEPS + 2))
                dve.wait_ge(added, (s + 1) * ((STEPS + 1) * PG) + 1)
                nc.vector.tensor_scalar(neg_base[:], neg_base[:], float(-NB), None, ALU.add).then_inc(moved, 1)
                nc.vector.tensor_scalar(step_block[:], step_block[:], 1, None, ALU.add).then_inc(moved, 1)
                dve.wait_ge(moved, 2 * s + 3)

        @block.tensor
        def _(pe):
            pe.sem_inc(summed, AHEAD)
            pe.sem_inc(added, 1)
            n_sweeps = count(pe)

            def turn(u, done):
                pe.wait_ge(hot_ready, done)
                for j in range(ST):
                    last = nc.tensor.transpose(psT[:, u % 2, j * EP:(j + 1) * EP], hot[:, u, j, :],
                                               ident[0:EP, 0:EP])
                last.then_inc(hot_turned, 1)

            def pick(at, u, done):
                bs = [pe.value_load(step_block[0:1, bass.ds(at * PG + (PG + n), 1)], min_val=0, max_val=BLOCKS - 1)
                      for n in range(PG)]
                pe.wait_ge(hotT_ready, done)
                for j in range(ST):
                    last = nc.tensor.matmul(psD[:, u % 2, j * 2 * GH:(j + 1) * 2 * GH], hotT[:, u % 2, j, :],
                                            ad_m[:, bass.ds(bs[j // GT], 1), :].rearrange("p a f -> p (a f)"),
                                            start=True, stop=True)
                last.then_inc(dst_picked, 1)

            with pe.Fori(0, n_sweeps) as s:
                turn(0, s * (STEPS + 3) + 1)
                turn(1, s * (STEPS + 3) + 2)
                pick(0, 0, s * (STEPS + 2) + 1)
                turn(2, s * (STEPS + 3) + 3)
                pe.wait_ge(added, s * ((STEPS + 1) * PG) + 1)
                for n in range(PG):
                    last = nc.tensor.matmul(psS[:, 1, n, 0:ROW], zeros[:, 0:NB], zeros[:, 0:ROW], start=True,
                                            stop=True)
                last.then_inc(summed, 1)
                with pe.Fori(0, TRIPS) as i:
                    for u in range(SLOTS):
                        k = i * SLOTS + u
                        pick(k + 1, u + 1, s * (STEPS + 2) + k + 2)
                        pe.wait_ge(weighed, s * STEPS + k + 1)
                        pe.wait_ge(added, s * ((STEPS + 1) * PG) + k * PG + 1)
                        for j in range(ST):
                            last = nc.tensor.matmul(psS[:, u % 2, j // GT, 0:ROW], hot[:, u, j, :], msg[:, u, j, :],
                                                    start=j % GT == 0, stop=j % GT == GT - 1)
                        last.then_inc(summed, 1)
                        turn((u + 3) % SLOTS, s * (STEPS + 3) + k + 4)


def nodes(nc, scope, table, W_gat, xatt_src, xatt_dst, xtable, xtable_dst, x_all, ident, agg, ex_self, xnT_all,
          hg_all, xad_all, row):
    U = 2
    with ExitStack() as ctx:
        sb, ps, sem = scope(ctx)
        wg = sb("wg", [P, KC, XF])
        atS = sb("atS", [NB, XF])
        atD = sb("atD", [NB, XF])
        hs = sb("hs", [NB, BLOCKS, D])
        den = sb("den", [NB, BLOCKS, GH])
        stats = sb("stats_n", [NB, BLOCKS, 6])
        mean = sb("mean_n", [NB, BLOCKS])
        rstd = sb("rstd_n", [NB, BLOCKS])
        eps = sb("eps_n", [NB, 1])
        xn = sb("xn_n", [NB, U, D])
        xT = sb("xT_n", [P, U, KC, NB])
        prod = sb("prod_n", [NB, BLOCKS, XF])
        top = sb("top_n", [NB, XH])
        topall = sb("topall_n", [NB, XH])
        s_self = sb("s_self_n", [NB, BLOCKS, XH])
        s_top = sb("s_top_n", [NB, BLOCKS, XH])
        psT = ps("psT_n", [P, U, 512])
        psG = ps("psG_n", [NB, U, 512])
        loaded = sem("loaded_n")
        SOME = 5
        HCH = 5
        HB = BLOCKS // HCH
        h_back = [sem(f"h_back{c}") for c in range(HCH)]
        self_message = sem("self_message")
        weighed = sem("weighed_n")
        updated = sem("updated")
        messages_summed = sem("messages_summed")
        chain = sem("chain_n")
        measured = sem("measured_n")
        var_ready = sem("var_ready_n")
        std_ready = sem("std_ready_n")
        normed = sem("normed_n")
        turned = sem("turned_n")
        kept = sem("kept_n")
        projected = sem("projected_n")
        proj_kept = sem("proj_kept_n")
        top_known = sem("top_known_n")
        top_shared = sem("top_shared_n")
        tables = sem("tables_n")
        stored = sem("stored_n")
        block = ctx.enter_context(nc.Block())

        def each_few(eng, step):
            with eng.Fori(0, BLOCKS // (2 * SOME)) as i:
                for r in range(2):
                    step(i * (2 * SOME) + r * SOME, i * 2 + r)

        @block.sync
        def _(sp):
            sp.dma_start(wg[:], W_gat.rearrange("(c p) n -> p c n", p=P)).then_inc(loaded, 16)
            for tile, vec in ((atS, xatt_src), (atD, xatt_dst)):
                sp.dma_start(tile[:], row(vec.rearrange("h c -> (h c)")).to_broadcast([NB, XF])).then_inc(loaded, 16)
            hv = table.rearrange("(b p) r -> p b r", p=NB)
            for c in range(HCH):
                b = slice(c * HB, (c + 1) * HB)
                sp.dma_start(hs[:, b, :], hv[:, b, 0:D]).then_inc(h_back[c], 16)
            sp.wait_ge(tables, 1)
            sp.dma_start(xtable.rearrange("(b p) f -> p b f", p=NB), hg_all[:]).then_inc(stored, 16)
            sp.dma_start(xtable_dst.rearrange("(b p) f -> p b f", p=NB), xad_all[:]).then_inc(stored, 16)
            sp.wait_ge(stored, 32)

        @block.vector
        def _(dve):
            V = nc.vector
            dve.wait_ge(loaded, 48)
            ch = Chain(dve, chain)
            ch.link(V.tensor_tensor(den[:], agg[:, :, D:ROW], ex_self[:], ALU.add))
            ch.link(V.scalar_tensor_tensor(den[:], ex_self[:], 1e-16, den[:], ALU.mult, ALU.add))
            ch.link(V.reciprocal(den[:], den[:]))

            def update(n, t):
                dve.wait_ge(messages_summed, n + SOME)
                sums = hs[:, bass.ds(n, SOME), :].rearrange("p b (h c) -> p b h c", h=GH)
                V.tensor_tensor(sums, sums, bcast(den[:, bass.ds(n, SOME), :], 3, GC), ALU.mult).then_inc(weighed, 1)
                dve.wait_ge(weighed, t + 1)
                xb = x_all[:, bass.ds(n, SOME), :]
                V.tensor_tensor(xb, xb, hs[:, bass.ds(n, SOME), :], ALU.add).then_inc(updated, 1)
                dve.wait_ge(updated, t + 1)
                for b in range(SOME):
                    V.bn_stats(stats[:, bass.ds(n + b, 1), :].rearrange("p a s -> p (a s)"),
                               x_all[:, bass.ds(n + b, 1), :].rearrange("p a d -> p (a d)")).then_inc(measured, 1)

            each_few(dve, update)
            dve.wait_ge(measured, BLOCKS)
            mean_and_variance(nc, ch, stats, mean[:], rstd[:])
            ch.link(V.memset(eps[:], EPS))
            V.tensor_copy(stats[:, :, 0], rstd[:]).then_inc(var_ready, 1)
            dve.wait_ge(std_ready, 1)
            ch.link(V.reciprocal(rstd[:], rstd[:]))

            def normalize(n, u, first, last):
                if not first:
                    dve.wait_ge(turned, n - 1)
                V.tensor_scalar(xn[:, u, :], x_all[:, bass.ds(n, 1), :].rearrange("p a d -> p (a d)"),
                                mean[:, bass.ds(n, 1)], rstd[:, bass.ds(n, 1)], ALU.subtract, ALU.mult) \
                    .then_inc(normed, 1)

            each_block(dve, normalize)
            dve.wait_ge(proj_kept, BLOCKS)
            h4 = hg_all[:, :, 0:XF]
            ch.link(V.tensor_tensor(prod[:], h4, bcast(atS[:], 1, BLOCKS), ALU.mult))
            ch.link(V.reduce_sum(hg_all[:, :, XF:], prod[:].rearrange("p b (h e) -> p b h e", h=XH), AX_X))
            ch.link(V.tensor_tensor(prod[:], h4, bcast(atD[:], 1, BLOCKS), ALU.mult))
            ch.link(V.reduce_sum(xad_all[:, :, 0:XH], prod[:].rearrange("p b (h e) -> p b h e", h=XH), AX_X))
            V.tensor_reduce(top[:], hg_all[:, :, XF:].rearrange("p b h -> p h b"), AX_X, ALU.max).then_inc(top_known, 1)
            ch.link(V.tensor_tensor(s_self[:], hg_all[:, :, XF:], xad_all[:, :, 0:XH], ALU.add))
            ch.link(V.scalar_tensor_tensor(s_self[:], s_self[:], SLOPE, s_self[:], ALU.mult, ALU.max))
            dve.wait_ge(top_shared, 1)
            ch.link(V.tensor_tensor(s_top[:], xad_all[:, :, 0:XH], bcast(topall[:], 1, BLOCKS), ALU.add))
            ch.link(V.scalar_tensor_tensor(s_top[:], s_top[:], SLOPE, s_top[:], ALU.mult, ALU.max))
            V.scalar_tensor_tensor(xad_all[:, :, XH:], s_self[:], SPREAD, s_top[:], ALU.add, ALU.min) \
                .then_inc(tables, 1)

        @block.gpsimd
        def _(pool):
            def sum_messages(n, t):
                pool.wait_ge(self_message, n + SOME)
                part = hs[:, bass.ds(n, SOME), :]
                nc.gpsimd.tensor_tensor(part, part, agg[:, bass.ds(n, SOME), 0:D], ALU.add) \
                    .then_inc(messages_summed, SOME)

            each_few(pool, sum_messages)
            pool.wait_ge(top_known, 1)
            nc.gpsimd.partition_all_reduce(topall[:], top[:], NB, RMAX).then_inc(top_shared, 1)

        @block.scalar
        def _(act):
            def weigh_self(n):
                for h in range(GH):
                    part = hs[:, bass.ds(n, 1), h * GC:(h + 1) * GC].rearrange("p a d -> p (a d)")
                    done = nc.scalar.activation(part, part, ACT.Copy,
                                                scale=ex_self[:, bass.ds(n, 1), h:h + 1].rearrange("p a h -> p (a h)"))
                done.then_inc(self_message, 1)

            for c in range(HCH):
                act.wait_ge(h_back[c], 16)
                with act.Fori(0, HB // SOME) as i:
                    for r in range(SOME):
                        weigh_self(i * SOME + (c * HB + r))
            act.wait_ge(var_ready, 1)
            nc.scalar.activation(rstd[:], stats[:, :, 0], ACT.Sqrt, bias=eps[:]).then_inc(std_ready, 1)

            def keep_turned(n, u):
                act.wait_ge(turned, n + 1)
                nc.scalar.copy(xnT_all[:, bass.ds(n, 1), :],
                               psT[:, u, 0:KC * NB].rearrange("p (a n) -> p a n", a=1))
                nc.scalar.copy(xT[:, u, :, :], psT[:, u, 0:KC * NB].rearrange("p (c n) -> p c n", c=KC)) \
                    .then_inc(kept, 1)

            def keep_projected(n, u, first, last):
                if not (last and u == U - 1):
                    keep_turned(n + 1, (u + 1) % U)
                act.wait_ge(projected, n + 1)
                nc.scalar.copy(hg_all[:, bass.ds(n, 1), 0:XF],
                               psG[:, u, 0:XF].rearrange("p (a f) -> p a f", a=1)).then_inc(proj_kept, 1)

            keep_turned(0, 0)
            each_block(act, keep_projected)

        @block.tensor
        def _(pe):
            pe.wait_ge(loaded, 48)

            def turn(n, u):
                pe.wait_ge(normed, n + 1)
                for c in range(KC):
                    last = nc.tensor.transpose(psT[:, u, c * NB:(c + 1) * NB], xn[:, u, c * P:(c + 1) * P],
                                               ident[0:NB, 0:NB])
                last.then_inc(turned, 1)

            def project(n, u, first, last):
                if not (last and u == U - 1):
                    turn(n + 1, (u + 1) % U)
                pe.wait_ge(kept, n + 1)
                if not first:
                    pe.wait_ge(proj_kept, n - 1)
                for c in range(KC):
                    mm = nc.tensor.matmul(psG[:, u, 0:XF], xT[:, u, c, :], wg[:, c, :], start=c == 0,
                                          stop=c == KC - 1)
                mm.then_inc(projected, 1)

            turn(0, 0)
            each_block(pe, project)


def gating_sums_and_experts(nc, scope, src_i, dst_i, edges_loaded, xtable, xtable_dst, W1, b1, W2, b2, zeros, node,
                            xnT, acc, y_dram, row):
    HALF = BLOCKS // 2
    PAIR = 2
    PN = PAIR * NB
    SPAN = 10
    TRIPS = BLOCKS // PAIR
    TAIL = range(TRIPS * SPAN, XGROUPS)
    assert SPAN % XSLOTS == 0 and 0 < len(TAIL) <= SPAN
    with ExitStack() as ctx:
        sb, ps, sem = scope(ctx)
        blk = sb("blk", [P, XGROUPS, XT], BF16)
        loc = sb("loc", [P, XGROUPS, XT])
        idx = sb("xidx", [P, XSLOTS, 2, XT], I32)
        pos = sb("pos", [P, XSLOTS, 2, XT])
        msg = sb("xmsg", [P, XSLOTS, XT, XROW])
        adm = sb("xadm", [P, XSLOTS, XT, 2 * XH])
        lg = sb("xlg", [P, XSLOTS, XT, XH])
        lo = sb("lo", [P, 2, max(XWHOLE), NB])
        lo_r = sb("lo_r", [P, 2, XPARTS, NB], F32R)
        hi = sb("hi", [P, 2, XT, BLOCKS])
        wide = sb("wide", [P, max(XWHOLE), BLOCKS, XROW])
        part = sb("part", [P, 2, XPARTS, XROW], F32R)
        wide_r = sb("wide_r", [P, XPARTS, 2, BLOCKS, XROW], F32R)
        b2f = wide[0:1].rearrange("p j b r -> p (j b r)")[:, 0:XE * D]
        bid = sb("bid", [P, BLOCKS])
        w1 = sb("w1", [P, XE, KC, HID])
        w2 = sb("w2", [P, XE, HC, D])
        b1c = sb("b1c", [P, XE, HC])
        b2k = sb("b2k", [3, XE * D], BF16)
        ones3 = sb("ones3", [3, NB], BF16)
        hid = sb("hid", [P, 2, HC, PN])
        b2p = hid[0:1].rearrange("p s c n -> p (s c n)").bitcast(BF16)[:, 0:3 * XE * D] \
            .rearrange("p (s n) -> p s n", s=3)
        q = wide[:].rearrange("p j b r -> p (j b r)")[:, XE * D:XE * D + XGROUPS * XT] \
            .rearrange("p (g j) -> p g j", j=XT)
        y_room = sb("y_room", [P, 2, PAIR, D])
        y_sb = y_room[0:NB]
        tmp = y_room[:].rearrange("p s h d -> p (s h d)")[:, 0:XGROUPS * XT].rearrange("p (g j) -> p g j", j=XT)
        psA = ps("psA", [P, HC, 256])
        psY = ps("psY", [NB, PAIR, D])
        iotas = sem("iotas_g")
        chain = sem("chain_g")
        prepared = sem("prepared")
        staged = sem("staged_g")
        opened = sem("opened_g")
        gathered = [sem(f"gathered_g{u}") for u in range(XSLOTS)]
        logits = sem("logits_g")
        weights = sem("weights_g")
        widened = sem("widened")
        summed = sem("summed_g")
        weights_loaded = sem("weights_loaded")
        hid_ready = sem("hid_ready")
        act_done = sem("act_done")
        y_ready = sem("y_ready")
        y_kept = sem("y_kept")
        y_stored = sem("y_stored")
        y_free = sem("y_free")
        b2_loaded = sem("b2_loaded")
        b2_split = sem("b2_split")
        b2_spread = sem("b2_spread")
        ones3_set = sem("ones3_set")
        block = ctx.enter_context(nc.Block())
        LOADS = 1 + 2 * XE

        @block.sync
        def _(sp):
            sp.dma_start(b2f, row(b2.rearrange("e n -> (e n)"))).then_inc(b2_loaded, 16)
            for e in range(XE):
                sp.dma_start(w1[:, e], W1[e].rearrange("(c p) n -> p c n", p=P)).then_inc(weights_loaded, 16)
                sp.dma_start(w2[:, e], W2[e].rearrange("(c p) n -> p c n", p=P)).then_inc(weights_loaded, 16)
            sp.dma_start(b1c[:], b1.rearrange("e (c p) -> p e c", p=P), allow_slow_non_contiguous=True) \
                .then_inc(weights_loaded, 16)
            sp.wait_ge(b2_split, 5)
            for n in range(3):
                sp.dma_start(b2k[n:n + 1, :], b2p[:, n, :]).then_inc(b2_spread, 16)

            def store(q, u):
                sp.wait_ge(y_kept, q + 1)
                sp.dma_start(y_dram[bass.ds(q, 1)].rearrange("a p f -> p (a f)"),
                             y_sb[:, u].rearrange("p h d -> p (h d)")).then_inc(y_stored, 16)
                sp.wait_ge(y_stored, q * 16 + 16)
                sp.sem_inc(y_free, 1)

            with sp.Fori(0, XE * TRIPS // 2) as i:
                for u in range(2):
                    store(2 * i + u, u)
            store(XE * TRIPS, 0)

        @block.gpsimd
        def _(pool):
            nc.gpsimd.iota(bid[:], [[1, BLOCKS]], base=0, channel_multiplier=0,
                           allow_small_or_imprecise_dtypes=True).then_inc(iotas, 1)

            def gather(k, u):
                pool.wait_ge(staged, k + 1)
                pool.sem_inc(opened, 1)
                for j in range(XT):
                    nc.gpsimd.indirect_dma_start(
                        msg[:, u, j, :], None, xtable[:, :],
                        bass.IndirectOffsetOnAxis(ap=idx[:, u, 0, j:j + 1], axis=0)).then_inc(gathered[u], 16)
                    nc.gpsimd.indirect_dma_start(
                        adm[:, u, j, :], None, xtable_dst[:, :],
                        bass.IndirectOffsetOnAxis(ap=idx[:, u, 1, j:j + 1], axis=0)).then_inc(gathered[u], 16)

            with pool.Fori(0, TRIPS) as i:
                for w in range(SPAN):
                    gather(i * SPAN + w, w % XSLOTS)
            for k in TAIL:
                gather(k, k % XSLOTS)

        @block.scalar
        def _(act):
            act.sem_inc(act_done, HC)
            act.sem_inc(y_free, 2)
            act.wait_ge(prepared, 1)
            act.wait_ge(weights_loaded, 16 * LOADS)

            def stage(at, u):
                for s, (ints, where) in enumerate(((src_i, blk), (dst_i, loc))):
                    nc.scalar.copy(idx[:, u, s, :], ints[:, bass.ds(at, 1), :].rearrange("p a j -> p (a j)"))
                    last = nc.scalar.copy(pos[:, u, s, :], where[:, bass.ds(at, 1), :].rearrange("p a j -> p (a j)"))
                last.then_inc(staged, 1)

            def step(k, u, more):
                act.wait_ge(logits, k + 1)
                nc.scalar.activation(msg[:, u, :, XF:], lg[:, u, :, :], ACT.Exp).then_inc(weights, 1)
                if more:
                    stage(k + XAHEAD, (u + XAHEAD) % XSLOTS)

            def gelu(m, e):
                for c in range(HC):
                    act.wait_ge(hid_ready, m * HC + (c // 2 * 2 + 2))
                    nc.scalar.activation(hid[:, e % 2, c, :], psA[:, c, 0:PN], ACT.Gelu, bias=b1c[:, e, c:c + 1]) \
                        .then_inc(act_done, 1)

            def keep_y(q, u):
                act.wait_ge(y_ready, q + 1)
                act.wait_ge(y_free, q + 1)
                nc.scalar.copy(y_sb[:, u], psY[:]).then_inc(y_kept, 1)

            for a in range(XAHEAD):
                stage(a, a)
            with act.Fori(0, TRIPS) as i:
                for w in range(SPAN):
                    step(i * SPAN + w, w % XSLOTS, True)
                    if w % 2 == 1 and w < 2 * XE:
                        gelu(i * XE + w // 2, w // 2)
                    if w == 1:
                        keep_y(i * XE, 0)
                    if w % 2 == 0 and w >= 4:
                        keep_y(i * XE + (w - 2) // 2, (w - 2) // 2 % 2)
            for k in TAIL:
                step(k, k % XSLOTS, k + XAHEAD < XGROUPS)
                if k == TAIL[0]:
                    keep_y(XE * TRIPS, 0)

        @block.vector
        def _(dve):
            V = nc.vector
            V.memset(ones3[:], 1.0).then_inc(ones3_set, 1)
            ch = Chain(dve, chain)
            dve.wait_ge(edges_loaded, 16 * 2)
            ch.link(V.tensor_copy(loc[:], dst_i[:]))
            floor_div(nc, ch, loc[:], q, dst_i[:], tmp, NB)
            ch.link(V.tensor_scalar(dst_i[:], loc[:], float(N - 1), None, ALU.min))
            ch.link(V.scalar_tensor_tensor(loc[:], q, float(-NB), loc[:], ALU.mult, ALU.add))
            ch.link(V.tensor_copy(blk[:], q))
            dve.wait_ge(iotas, 1)
            V.tensor_scalar(src_i[:], src_i[:], N - 1, None, ALU.min).then_inc(prepared, 1)
            base = ch.n
            dve.wait_ge(b2_loaded, 16)
            ch = Chain(dve, b2_split)
            ch.link(V.tensor_copy(b2p[:, 0, :], b2f))
            for n in range(1, 3):
                ch.link(V.tensor_tensor(b2f, b2f, b2p[:, n - 1, :], ALU.subtract))
                ch.link(V.tensor_copy(b2p[:, n, :], b2f))
            PER = 6

            def step(k, u, half, visit):
                ch = Chain(dve, chain, base + PER * k)
                dve.wait_ge(gathered[u], visit * (16 * 2 * XT))
                l = lg[:, u, :, :]
                ch.link(V.tensor_tensor(l, msg[:, u, :, XF:], adm[:, u, :, 0:XH], ALU.add))
                ch.link(V.scalar_tensor_tensor(l, l, SLOPE, l, ALU.mult, ALU.max))
                V.tensor_tensor(l, l, adm[:, u, :, XH:], ALU.subtract).then_inc(logits, 1)
                whole = XWHOLE[half]
                split = slice(whole - (XT - XPARTS), XPARTS)
                V.tensor_tensor(lo[:, half, 0:whole], bcast(node[:], 1, whole), bcast(pos[:, u, 1, 0:whole], 2, NB),
                                ALU.is_equal)
                V.tensor_tensor(lo_r[:, half, split], bcast(node[:], 1, XT - whole),
                                bcast(pos[:, u, 1, whole:], 2, NB), ALU.is_equal)
                ch.link(V.tensor_tensor(hi[:, half, :, :], bcast(bid[:], 1, XT), bcast(pos[:, u, 0, :], 2, BLOCKS),
                                        ALU.is_equal))
                dve.wait_ge(weights, k + 1)
                m = msg[:, u, :, 0:XF].rearrange("p j (h e) -> p j h e", h=XH)
                ch.link(V.tensor_tensor(m, m, bcast(msg[:, u, :, XF:], 3, XE), ALU.mult))
                rows = msg[:, u, whole:, :]
                ch.link(V.tensor_scalar(part[:, 0, split], rows, 1.0, None, ALU.mult))
                V.tensor_tensor(part[:, 1, split], rows, part[:, 0, split], ALU.subtract).then_inc(chain, 1)
                for j in range(XT):
                    dve.wait_ge(summed, k * XT + (j + 1))
                    if j < whole:
                        V.tensor_tensor(wide[:, j], bcast(hi[:, half, j, :], 2, XROW),
                                        bcast(msg[:, u, j, :], 1, BLOCKS), ALU.mult).then_inc(widened, 1)
                    else:
                        if j == whole:
                            dve.wait_ge(chain, base + PER * k + PER)
                        r = j - (XT - XPARTS)
                        V.tensor_tensor(wide_r[:, r], bcast(bcast(hi[:, half, j, :], 2, XROW), 1, 2),
                                        bcast(part[:, :, r, :], 2, BLOCKS), ALU.mult).then_inc(widened, 1)
                assert ch.n == PER - 1

            with dve.Fori(0, TRIPS) as i:
                for w in range(SPAN):
                    step(i * SPAN + w, w % XSLOTS, w % 2, i * (SPAN // XSLOTS) + (w // XSLOTS + 1))
            for k in TAIL:
                step(k, k % XSLOTS, k % 2, k // XSLOTS + 1)

        @block.tensor
        def _(pe):
            pe.sem_inc(summed, XT)
            for half in range(2):
                nc.tensor.matmul(acc[:, half, 0:HALF * XROW], zeros[:, 0:NB], zeros[:, 0:HALF * XROW],
                                 start=True, stop=False, skip_group_check=True)
            nc.tensor.matmul(psY[:].rearrange("p h d -> p (h d)"), zeros[:, 0:NB], zeros[:, 0:PAIR * D],
                             start=True, stop=True).then_inc(y_ready, 1)
            pe.wait_ge(weights_loaded, 16 * LOADS)
            pe.wait_ge(b2_spread, 16 * 3)
            pe.wait_ge(ones3_set, 1)

            def step(k, half):
                for j in range(XT):
                    pe.wait_ge(widened, k * XT + (j + 1))
                    if j < XWHOLE[half]:
                        mine, parts = lo[:, half, j, :], [wide[:, j]]
                    else:
                        r = j - (XT - XPARTS)
                        mine, parts = lo_r[:, half, r, :], [wide_r[:, r, n] for n in range(2)]
                    for w in parts:
                        for h in range(2):
                            last = nc.tensor.matmul(
                                acc[:, h, 0:HALF * XROW], mine,
                                w[:, h * HALF:(h + 1) * HALF, :].rearrange("p b r -> p (b r)"),
                                start=False, stop=False, skip_group_check=True)
                    last.then_inc(summed, 1)

            def first_products(i, e):
                pe.wait_ge(act_done, i * (XE * HC) + (e * HC + HC))
                for c in range(HC):
                    for kc in range(KC):
                        last = nc.tensor.matmul(psA[:, c, 0:PN], w1[:, e, kc, c * P:(c + 1) * P],
                                                xnT[:, bass.ds(i * PAIR, PAIR), kc * NB:(kc + 1) * NB],
                                                start=kc == 0, stop=kc == KC - 1)
                    last.then_inc(hid_ready, 1)

            def second_products(i, e):
                pe.wait_ge(act_done, i * (XE * HC) + (e + 2) * HC)
                pe.wait_ge(y_kept, i * XE + (e + 1))
                for h in range(PAIR):
                    for c in range(HC):
                        nc.tensor.matmul(psY[:, h, :], hid[:, e % 2, c, h * NB:(h + 1) * NB], w2[:, e, c, :],
                                         start=c == 0, stop=False)
                    last = nc.tensor.matmul(psY[:, h, :], ones3[:], b2k[:, e * D:(e + 1) * D], start=False, stop=True)
                last.then_inc(y_ready, 1)

            with pe.Fori(0, TRIPS) as i:
                for w in range(SPAN):
                    step(i * SPAN + w, w % 2)
                    if w % 2 == 0 and w < 2 * XE:
                        first_products(i, w // 2)
                    if w % 2 == 1 and w >= 3:
                        second_products(i, (w - 3) // 2)
            for k in TAIL:
                step(k, k % 2)
            for half in range(2):
                nc.tensor.matmul(acc[:, half, 0:HALF * XROW], zeros[:, 0:NB], zeros[:, 0:HALF * XROW],
                                 start=False, stop=True, skip_group_check=True)


def load_experts(sp, y_dram, y_sb, y_loaded, n, u):
    sp.dma_start(y_sb[:, u], y_dram[bass.ds(n * XE + 1, XE)].rearrange("e p f -> p e f")).then_inc(y_loaded[u], 16)


def gates(nc, scope, b_gat, gamma, beta, hg_all, xad_all, acc, gate, row, y_dram, y_sb, y_loaded):
    HALF = BLOCKS // 2
    with ExitStack() as ctx:
        sb, _, sem = scope(ctx)
        bg = sb("bg", [NB, 3, XF])
        ext = sb("xext", [NB, BLOCKS, XH])
        num = sb("xnum", [NB, BLOCKS, XROW])
        a1 = sb("a1", [NB, BLOCKS, XF])
        red = sb("red", [NB, BLOCKS, 1])
        red2 = sb("red2", [NB, BLOCKS, 1])
        sc = sb("sc", [NB, BLOCKS, XE])
        rank = sb("rank", [NB, BLOCKS, XE])
        cmp = sb("cmp", [NB, BLOCKS, 1])
        first = sb("first", [NB, BLOCKS, XE])
        second = sb("second", [NB, BLOCKS, XE])
        loaded = sem("loaded_h")
        chain = sem("chain_h")
        to_exp = sem("to_exp")
        exped = sem("exped")
        block = ctx.enter_context(nc.Block())

        @block.sync
        def _(sp):
            for n, vec in enumerate((b_gat, gamma, beta)):
                sp.dma_start(bg[:, n, :], row(vec).to_broadcast([NB, XF])).then_inc(loaded, 16)
            for u in range(YSLOTS):
                load_experts(sp, y_dram, y_sb, y_loaded, u, u)

        @block.scalar
        def _(act):
            act.wait_ge(to_exp, 1)
            nc.scalar.activation(ext[:], ext[:], ACT.Exp).then_inc(exped, 1)
            act.wait_ge(to_exp, 2)
            nc.scalar.activation(red2[:], red2[:], ACT.Sqrt).then_inc(exped, 1)
            act.wait_ge(to_exp, 3)
            nc.scalar.activation(cmp[:], cmp[:], ACT.Exp).then_inc(exped, 1)

        @block.vector
        def _(dve):
            V = nc.vector
            ch = Chain(dve, chain)
            dve.wait_ge(loaded, 48)
            ch.link(V.tensor_tensor(ext[:], hg_all[:, :, XF:], xad_all[:, :, 0:XH], ALU.add))
            ch.link(V.scalar_tensor_tensor(ext[:], ext[:], SLOPE, ext[:], ALU.mult, ALU.max))
            V.tensor_tensor(ext[:], ext[:], xad_all[:, :, XH:], ALU.subtract).then_inc(to_exp, 1)
            dve.wait_ge(exped, 1)

            def heads(t):
                return t.rearrange("p b (h e) -> p b h e", h=XH)

            ch.link(V.tensor_tensor(heads(num[:, :, 0:XF]), heads(hg_all[:, :, 0:XF]), bcast(ext[:], 3, XE), ALU.mult))
            for half in range(2):
                s = slice(half * HALF, (half + 1) * HALF)
                sums = acc[:, half, 0:HALF * XROW].rearrange("p (b r) -> p b r", r=XROW)
                ch.link(V.tensor_tensor(num[:, s, 0:XF], num[:, s, 0:XF], sums[:, :, 0:XF], ALU.add))
                ch.link(V.tensor_tensor(num[:, s, XF:], ext[:, s, :], sums[:, :, XF:], ALU.add))
            ch.link(V.scalar_tensor_tensor(num[:, :, XF:], ext[:], 1e-16, num[:, :, XF:], ALU.mult, ALU.add))
            ch.link(V.reciprocal(num[:, :, XF:], num[:, :, XF:]))
            ch.link(V.tensor_tensor(heads(a1[:]), heads(num[:, :, 0:XF]), bcast(num[:, :, XF:], 3, XE), ALU.mult))
            ch.link(V.tensor_tensor(a1[:], a1[:], bcast(bg[:, 0, :], 1, BLOCKS), ALU.add))
            r1 = red[:].rearrange("p b a -> p (b a)")
            r2 = red2[:].rearrange("p b a -> p (b a)")
            ch.link(V.reduce_sum(r1, a1[:], AX_X))
            ch.link(V.tensor_scalar(r1, r1, 1.0 / XF, None, ALU.mult))
            ch.link(V.tensor_tensor(a1[:], a1[:], bcast(r1, 2, XF), ALU.subtract))
            ch.link(V.tensor_tensor(num[:, :, 0:XF], a1[:], a1[:], ALU.mult))
            ch.link(V.reduce_sum(r2, num[:, :, 0:XF], AX_X))
            V.tensor_scalar(r2, r2, 1.0 / XF, EPS, ALU.mult, ALU.add).then_inc(to_exp, 1)
            dve.wait_ge(exped, 2)
            ch.link(V.reciprocal(r2, r2))
            ch.link(V.tensor_tensor(a1[:], a1[:], bcast(r2, 2, XF), ALU.mult))
            ch.link(V.tensor_tensor(a1[:], a1[:], bcast(bg[:, 1, :], 1, BLOCKS), ALU.mult))
            ch.link(V.tensor_tensor(a1[:], a1[:], bcast(bg[:, 2, :], 1, BLOCKS), ALU.add))
            ch.link(V.reduce_sum(sc[:], a1[:].rearrange("p b (h e) -> p b e h", h=XH), AX_X))
            ch.link(V.tensor_scalar(sc[:], sc[:], 1.0 / XH, None, ALU.mult))
            ch.link(V.memset(rank[:], 0.0))
            for e in range(XE):
                for o in range(XE):
                    if o != e:
                        op = ALU.is_ge if o < e else ALU.is_gt
                        ch.link(V.tensor_tensor(cmp[:], sc[:, :, o:o + 1], sc[:, :, e:e + 1], op))
                        ch.link(V.tensor_tensor(rank[:, :, e:e + 1], rank[:, :, e:e + 1], cmp[:], ALU.add))
            ch.link(V.tensor_scalar(first[:], rank[:], 0.0, None, ALU.is_equal))
            ch.link(V.tensor_scalar(second[:], rank[:], 1.0, None, ALU.is_equal))
            ch.link(V.tensor_tensor(rank[:], first[:], sc[:], ALU.mult))
            ch.link(V.reduce_sum(r1, rank[:], AX_X))
            ch.link(V.tensor_tensor(rank[:], second[:], sc[:], ALU.mult))
            ch.link(V.reduce_sum(r2, rank[:], AX_X))
            V.tensor_tensor(cmp[:], red2[:], red[:], ALU.subtract).then_inc(to_exp, 1)
            dve.wait_ge(exped, 3)
            ch.link(V.tensor_scalar(red[:], cmp[:], 1.0, None, ALU.add))
            ch.link(V.reciprocal(red[:], red[:]))
            ch.link(V.tensor_tensor(red2[:], red[:], cmp[:], ALU.mult))
            ch.link(V.tensor_tensor(first[:], first[:], bcast(r1, 2, XE), ALU.mult))
            ch.link(V.tensor_tensor(second[:], second[:], bcast(r2, 2, XE), ALU.mult))
            ch.link(V.tensor_tensor(gate[:], first[:], second[:], ALU.add))


def combine(nc, scope, x_all, gate, y_dram, y_sb, y_loaded, out):
    PAIR = 2
    TRIPS = BLOCKS // PAIR // YSLOTS
    PER = XE * PAIR
    with ExitStack() as ctx:
        _, _, sem = scope(ctx)
        added = sem("y_added")
        stored = sem("stored_x")
        block = ctx.enter_context(nc.Block())

        @block.sync
        def _(sp):
            with sp.Fori(1, TRIPS) as i:
                for u in range(YSLOTS):
                    n = i * YSLOTS + u
                    sp.wait_ge(added, (n - (YSLOTS - 1)) * PER)
                    load_experts(sp, y_dram, y_sb, y_loaded, n, u)

        @block.vector
        def _(dve):
            def add(n, u, trip):
                dve.wait_ge(y_loaded[u], trip * 16 + 16)
                for e in range(XE):
                    for h in range(PAIR):
                        xb = x_all[:, bass.ds(n * PAIR + h, 1), :].rearrange("p a d -> p (a d)")
                        g = gate[:, bass.ds(n * PAIR + h, 1), e:e + 1].rearrange("p a d -> p (a d)")
                        if e > 0:
                            dve.wait_ge(added, n * PER + ((e - 1) * PAIR + h + 1))
                        nc.vector.scalar_tensor_tensor(xb, y_sb[:, u, e, h * D:(h + 1) * D], g, xb, ALU.mult, ALU.add) \
                            .then_inc(added, 1)

            for u in range(YSLOTS):
                add(u, u, 0)
            with dve.Fori(1, TRIPS) as i:
                for u in range(YSLOTS):
                    add(i * YSLOTS + u, u, i)

        @block.scalar
        def _(act):
            ov = out.rearrange("(b p) d -> p b d", p=NB)
            with act.Fori(0, BLOCKS // PAIR) as i:
                act.wait_ge(added, i * PER + PER)
                act.dma_start(ov[:, bass.ds(i * PAIR, PAIR), :], x_all[:, bass.ds(i * PAIR, PAIR), :]) \
                    .then_inc(stored, 16)
            act.wait_ge(stored, 16 * (BLOCKS // PAIR))


_INS = ['x', 'src', 'dst', 'L0_gnn_W', 'L0_gnn_att_src', 'L0_gnn_att_dst', 'L0_gnn_bias', 'L0_mix_W_qkv',
        'L0_mix_W_out', 'L0_mix_b_out', 'L0_ffn_W_gat', 'L0_ffn_att_src', 'L0_ffn_att_dst', 'L0_ffn_b_gat',
        'L0_ffn_ln_gamma', 'L0_ffn_ln_beta', 'L0_ffn_W1', 'L0_ffn_b1', 'L0_ffn_W2', 'L0_ffn_b2',
        'L0_ffn_edge_index']


def kernel(**inputs):
    import numpy as _np
    import concourse.bacc as _bacc
    from concourse import mybir as _mybir
    from concourse.bass_utils import run_bass_kernel_spmd as _run

    nc = _bacc.Bacc("TRN2", target_bir_lowering=False, num_devices=1)
    arrays, args = {}, []
    for name in _INS:
        a = _np.ascontiguousarray(inputs[name])
        arrays[f"in_{name}"] = a
        args.append(nc.dram_tensor(f"in_{name}", a.shape, _mybir.dt.from_np(a.dtype), kind="ExternalInput").ap())
    o = nc.dram_tensor("out_0", (N, D), F32, kind="ExternalOutput").ap()
    build(nc, *args, o)
    r = _run(nc, [arrays], core_ids=[0])
    return r.results[0]["out_0"]
```
